# Optimizing a Trainium2 kernel written in Bass

```python
import numpy as np
import jax
import jax.numpy as jnp

def _softmax(x, axis=-1):
    return jax.nn.softmax(x, axis=axis)

def _gelu(x):
    return jax.nn.gelu(x, approximate=True)

def _silu(x):
    return jax.nn.silu(x)

def _sigmoid(x):
    return jax.nn.sigmoid(x)

def _layernorm(x, axis=-1, eps=1e-05):
    m = jnp.mean(x, axis=axis, keepdims=True)
    v = jnp.var(x, axis=axis, keepdims=True)
    return (x - m) / jnp.sqrt(v + eps)

def _scatter_add(tgt, idx, src, axis=0):
    return tgt.at[idx].add(src)

def _segment_sum(src, seg, n):
    return jax.ops.segment_sum(src, seg, n)
kernel_name = 'mk_cond_seq_d4_seqx_r2_ca15e9'

def setup_inputs(seed: int=0):
    np.random.seed(seed)
    _w = jnp.asarray

    def _rec_inputs():
        import jax
        import jax.numpy as jnp
        _rk = jax.random.key(seed)
        x = -0.0005207 + 1.001 * jax.random.normal(jax.random.fold_in(_rk, 1), (2, 2048, 512), jnp.float32)
        _lenS = 2048 - jax.random.randint(jax.random.fold_in(_rk, 7), (2,), 0, max(1, 2048 // 4) + 1, jnp.int32)
        _lenS2 = 2048 - jax.random.randint(jax.random.fold_in(_rk, 8), (2,), 0, max(1, 2048 // 4) + 1, jnp.int32)
        itok_B_34_63 = jax.random.randint(jax.random.fold_in(_rk, 12), (2,), 34, 64, jnp.int32)
        fside_Bx16xSxS_0 = -1.47943e-05 + 1.00017 * jax.random.normal(jax.random.fold_in(_rk, 13), (2, 16, 2048, 2048), jnp.float32)
        itok_B_0_7 = jax.random.randint(jax.random.fold_in(_rk, 14), (2,), 0, 8, jnp.int32)
        condB_safetyscore = -0.927215 + 0.920279 * jax.random.normal(jax.random.fold_in(_rk, 15), (2,), jnp.float32)
        itok_B_0_15 = jax.random.randint(jax.random.fold_in(_rk, 16), (2,), 0, 16, jnp.int32)
        _validS = jnp.arange(2048)[None, :] < _lenS[:, None]
        _validS2 = jnp.arange(2048)[None, :] < _lenS2[:, None]
        _causal = jnp.tril(jnp.ones((2048, 2048), dtype=bool))
        mask_Bx1xSxS_bk0 = jnp.logical_not(jnp.broadcast_to(_validS[:, None, None, :], (2, 1, 2048, 2048)))
        return (x, itok_B_34_63, fside_Bx16xSxS_0, itok_B_0_7, condB_safetyscore, itok_B_0_15, mask_Bx1xSxS_bk0)
    x, itok_B_34_63, fside_Bx16xSxS_0, itok_B_0_7, condB_safetyscore, itok_B_0_15, mask_Bx1xSxS_bk0 = _rec_inputs()

    def _L0_cond_setup():
        import jax, jax.numpy as jnp
        import numpy as np
        import math
        D_MODEL = 512
        N_HEAD = 16
        HEAD_DIM = D_MODEL // N_HEAD
        D_FF = 2048
        NUM_STEPS = 100.0
        RESCALE = 4000.0
        EPS = 1e-05

        def _sin_emb(t):
            half = D_MODEL // 2
            x = t.astype(jnp.float32) / NUM_STEPS * RESCALE
            freqs = jnp.exp(jnp.arange(half, dtype=jnp.float32) * (-math.log(10000.0) / (half - 1)))
            e = x[:, None] * freqs[None, :]
            return jnp.concatenate([jnp.sin(e), jnp.cos(e)], axis=-1)

        def _ln(x):
            m = jnp.mean(x, axis=-1, keepdims=True)
            v = jnp.var(x, axis=-1, keepdims=True)
            return (x - m) / jnp.sqrt(v + EPS)

        def _gelu2(x):
            return x * jax.nn.sigmoid(1.702 * x)
        key = jax.random.key(seed)
        ks = jax.random.split(key, 24)
        B, S, D, F = (4, 256, D_MODEL, D_FF)
        std = 0.02
        inp = {'src': jax.random.normal(ks[0], (B, S, D), dtype=jnp.float32), 'src_mask': jax.random.randint(ks[1], (B, 1, S, S), 0, 2).astype(bool), 'timestep': jax.random.randint(ks[2], (B,), 0, 100, dtype=jnp.int32), 'attention_bias': jax.random.normal(ks[3], (B, N_HEAD, S, S), dtype=jnp.float32), 'W_ada': jax.random.normal(ks[4], (D, 2 * D), dtype=jnp.float32) * std, 'b_ada': jnp.zeros((2 * D,), dtype=jnp.float32), 'Wq': jax.random.normal(ks[5], (D, D), dtype=jnp.float32) * std, 'bq': jnp.zeros((D,), dtype=jnp.float32), 'Wk': jax.random.normal(ks[6], (D, D), dtype=jnp.float32) * std, 'bk': jnp.zeros((D,), dtype=jnp.float32), 'Wv': jax.random.normal(ks[7], (D, D), dtype=jnp.float32) * std, 'bv': jnp.zeros((D,), dtype=jnp.float32), 'Wo': jax.random.normal(ks[8], (D, D), dtype=jnp.float32) * std, 'bo': jnp.zeros((D,), dtype=jnp.float32), 'W1': jax.random.normal(ks[9], (D, F), dtype=jnp.float32) * std, 'b1': jnp.zeros((F,), dtype=jnp.float32), 'W2': jax.random.normal(ks[10], (F, D), dtype=jnp.float32) * std, 'b2': jnp.zeros((D,), dtype=jnp.float32), 'g2': jnp.ones((D,), dtype=jnp.float32), 'beta2': jnp.zeros((D,), dtype=jnp.float32)}
        return inp
    _L0_cond_all = _L0_cond_setup()
    _L0_cond_in = {k: v for k, v in _L0_cond_all.items() if k in ('W_ada', 'b_ada', 'Wq', 'bq', 'Wk', 'bk', 'Wv', 'bv', 'Wo', 'bo', 'W1', 'b1', 'W2', 'b2', 'g2', 'beta2')}
    del _L0_cond_all

    def _L1_cond_setup():
        import jax, jax.numpy as jnp
        import numpy as np
        E, H, I = (8, 512, 2048)
        B, S = (4, 512)
        LN_EPS = 1e-12
        key = jax.random.key(seed)
        ks = jax.random.split(key, 8)
        x = jax.random.normal(ks[0], (B, S, H), dtype=jnp.float32)
        expert_idx = jax.random.randint(ks[1], (B,), 0, E, dtype=jnp.int64)
        Wi = jax.random.normal(ks[2], (E, H, I), dtype=jnp.float32) * 0.02
        bi = jnp.zeros((E, I), dtype=jnp.float32)
        Wo = jax.random.normal(ks[3], (E, I, H), dtype=jnp.float32) * 0.02
        bo = jnp.zeros((E, H), dtype=jnp.float32)
        gamma = jnp.ones((E, H), dtype=jnp.float32)
        beta = jnp.zeros((E, H), dtype=jnp.float32)
        return {'input_tensor': x, 'expert_idx': expert_idx, 'Wi': Wi, 'bi': bi, 'Wo': Wo, 'bo': bo, 'gamma': gamma, 'beta': beta}
    _L1_cond_all = _L1_cond_setup()
    _L1_cond_in = {k: v for k, v in _L1_cond_all.items() if k in ('Wi', 'bi', 'Wo', 'bo', 'gamma', 'beta')}
    del _L1_cond_all

    def _L2_cond_setup():
        import jax, jax.numpy as jnp
        import numpy as np
        TEMPERATURE = 1.0
        ACT_THRESHOLD = 0.1
        MAX_ACT = 1.0
        SAFETY_KNOB = 1.0
        EPS = 1e-08

        def gram_schmidt(X):
            r = X.shape[1]
            Q = X
            for i in range(r):
                q = Q[:, i]
                q = q / (jnp.linalg.norm(q) + EPS)
                Q = Q.at[:, i].set(q)
                coeffs = q @ Q[:, i + 1:]
                Q = Q.at[:, i + 1:].add(-jnp.outer(q, coeffs))
            return Q
        key = jax.random.key(seed)
        ks = jax.random.split(key, 8)
        B, S, D, R = (8, 2048, 512, 32)
        init_std = 0.02
        return {'hidden_states': jax.random.normal(ks[0], (B, S, D), jnp.float32), 'safety_score': jax.random.normal(ks[1], (B,), jnp.float32), 'U': jax.random.normal(ks[2], (D, R), jnp.float32) * init_std, 'V': jax.random.normal(ks[3], (D, R), jnp.float32) * init_std, 'safety_bias': jnp.zeros((D,), jnp.float32), 'gate_w1': jax.random.normal(ks[4], (D // 4, D), jnp.float32) * (1.0 / np.sqrt(D)), 'gate_b1': jnp.zeros((D // 4,), jnp.float32), 'gate_w2': jax.random.normal(ks[5], (1, D // 4), jnp.float32) * (1.0 / np.sqrt(D // 4)), 'gate_b2': jnp.zeros((1,), jnp.float32), 'resp_w': jax.random.normal(ks[6], (D, R), jnp.float32) * (1.0 / np.sqrt(R)), 'resp_b': jnp.zeros((D,), jnp.float32)}
    _L2_cond_all = _L2_cond_setup()
    _L2_cond_in = {k: v for k, v in _L2_cond_all.items() if k in ('U', 'V', 'safety_bias', 'gate_w1', 'gate_b1', 'gate_w2', 'gate_b2', 'resp_w', 'resp_b')}
    del _L2_cond_all

    def _L3_cond_setup():
        import jax, jax.numpy as jnp
        import numpy as np
        B, S, D = (32, 512, 512)
        A = 128
        E = 16
        LN_EPS = 1e-05
        key = jax.random.key(seed)
        ks = jax.random.split(key, 10)
        s = lambda fan_in: 1.0 / np.sqrt(fan_in)
        return {'hidden_states': jax.random.normal(ks[0], (B, S, D), dtype=jnp.float32), 'domain_id': jax.random.randint(ks[1], (B,), 0, E, dtype=jnp.int64), 'down_W': jax.random.uniform(ks[2], (A, D), jnp.float32, -s(D), s(D)), 'down_b': jax.random.uniform(ks[3], (A,), jnp.float32, -s(D), s(D)), 'up_W': jax.random.uniform(ks[4], (D, A), jnp.float32, -s(A), s(A)), 'up_b': jax.random.uniform(ks[5], (D,), jnp.float32, -s(A), s(A)), 'expert_W': jax.random.uniform(ks[6], (E, A, A), jnp.float32, -s(A), s(A)), 'expert_b': jax.random.uniform(ks[7], (E, A), jnp.float32, -s(A), s(A)), 'domain_emb': jax.random.normal(ks[8], (E, A), dtype=jnp.float32), 'ln_gamma': jnp.ones((D,), jnp.float32), 'ln_beta': jnp.zeros((D,), jnp.float32)}
    _L3_cond_all = _L3_cond_setup()
    _L3_cond_in = {k: v for k, v in _L3_cond_all.items() if k in ('down_W', 'down_b', 'up_W', 'up_b', 'expert_W', 'expert_b', 'domain_emb', 'ln_gamma', 'ln_beta')}
    del _L3_cond_all
    return {'x': x, 'itok_B_34_63': itok_B_34_63, 'fside_Bx16xSxS_0': fside_Bx16xSxS_0, 'itok_B_0_7': itok_B_0_7, 'condB_safetyscore': condB_safetyscore, 'itok_B_0_15': itok_B_0_15, 'mask_Bx1xSxS_bk0': mask_Bx1xSxS_bk0, 'L0_cond_W_ada': _L0_cond_in['W_ada'], 'L0_cond_b_ada': _L0_cond_in['b_ada'], 'L0_cond_Wq': _L0_cond_in['Wq'], 'L0_cond_bq': _L0_cond_in['bq'], 'L0_cond_Wk': _L0_cond_in['Wk'], 'L0_cond_bk': _L0_cond_in['bk'], 'L0_cond_Wv': _L0_cond_in['Wv'], 'L0_cond_bv': _L0_cond_in['bv'], 'L0_cond_Wo': _L0_cond_in['Wo'], 'L0_cond_bo': _L0_cond_in['bo'], 'L0_cond_W1': _L0_cond_in['W1'], 'L0_cond_b1': _L0_cond_in['b1'], 'L0_cond_W2': _L0_cond_in['W2'], 'L0_cond_b2': _L0_cond_in['b2'], 'L0_cond_g2': _L0_cond_in['g2'], 'L0_cond_beta2': _L0_cond_in['beta2'], 'L1_cond_Wi': _L1_cond_in['Wi'], 'L1_cond_bi': _L1_cond_in['bi'], 'L1_cond_Wo': _L1_cond_in['Wo'], 'L1_cond_bo': _L1_cond_in['bo'], 'L1_cond_gamma': _L1_cond_in['gamma'], 'L1_cond_beta': _L1_cond_in['beta'], 'L2_cond_U': _L2_cond_in['U'], 'L2_cond_V': _L2_cond_in['V'], 'L2_cond_safety_bias': _L2_cond_in['safety_bias'], 'L2_cond_gate_w1': _L2_cond_in['gate_w1'], 'L2_cond_gate_b1': _L2_cond_in['gate_b1'], 'L2_cond_gate_w2': _L2_cond_in['gate_w2'], 'L2_cond_gate_b2': _L2_cond_in['gate_b2'], 'L2_cond_resp_w': _L2_cond_in['resp_w'], 'L2_cond_resp_b': _L2_cond_in['resp_b'], 'L3_cond_down_W': _L3_cond_in['down_W'], 'L3_cond_down_b': _L3_cond_in['down_b'], 'L3_cond_up_W': _L3_cond_in['up_W'], 'L3_cond_up_b': _L3_cond_in['up_b'], 'L3_cond_expert_W': _L3_cond_in['expert_W'], 'L3_cond_expert_b': _L3_cond_in['expert_b'], 'L3_cond_domain_emb': _L3_cond_in['domain_emb'], 'L3_cond_ln_gamma': _L3_cond_in['ln_gamma'], 'L3_cond_ln_beta': _L3_cond_in['ln_beta']}

def reference(x, itok_B_34_63, fside_Bx16xSxS_0, itok_B_0_7, condB_safetyscore, itok_B_0_15, mask_Bx1xSxS_bk0, L0_cond_W_ada, L0_cond_b_ada, L0_cond_Wq, L0_cond_bq, L0_cond_Wk, L0_cond_bk, L0_cond_Wv, L0_cond_bv, L0_cond_Wo, L0_cond_bo, L0_cond_W1, L0_cond_b1, L0_cond_W2, L0_cond_b2, L0_cond_g2, L0_cond_beta2, L1_cond_Wi, L1_cond_bi, L1_cond_Wo, L1_cond_bo, L1_cond_gamma, L1_cond_beta, L2_cond_U, L2_cond_V, L2_cond_safety_bias, L2_cond_gate_w1, L2_cond_gate_b1, L2_cond_gate_w2, L2_cond_gate_b2, L2_cond_resp_w, L2_cond_resp_b, L3_cond_down_W, L3_cond_down_b, L3_cond_up_W, L3_cond_up_b, L3_cond_expert_W, L3_cond_expert_b, L3_cond_domain_emb, L3_cond_ln_gamma, L3_cond_ln_beta):
    import jax
    import jax.numpy as jnp

    def _L0_cond_ref(src, src_mask, timestep, attention_bias, W_ada, b_ada, Wq, bq, Wk, bk, Wv, bv, Wo, bo, W1, b1, W2, b2, g2, beta2):
        import jax, jax.numpy as jnp
        import numpy as np
        import math
        D_MODEL = 512
        N_HEAD = 16
        HEAD_DIM = D_MODEL // N_HEAD
        D_FF = 2048
        NUM_STEPS = 100.0
        RESCALE = 4000.0
        EPS = 1e-05

        def _sin_emb(t):
            half = D_MODEL // 2
            x = t.astype(jnp.float32) / NUM_STEPS * RESCALE
            freqs = jnp.exp(jnp.arange(half, dtype=jnp.float32) * (-math.log(10000.0) / (half - 1)))
            e = x[:, None] * freqs[None, :]
            return jnp.concatenate([jnp.sin(e), jnp.cos(e)], axis=-1)

        def _ln(x):
            m = jnp.mean(x, axis=-1, keepdims=True)
            v = jnp.var(x, axis=-1, keepdims=True)
            return (x - m) / jnp.sqrt(v + EPS)

        def _gelu2(x):
            return x * jax.nn.sigmoid(1.702 * x)
        B, S, D = src.shape
        emb = jax.nn.silu(_sin_emb(timestep)) @ W_ada + b_ada
        scale, shift = jnp.split(emb[:, None, :], 2, axis=-1)
        x = _ln(src) * (1.0 + scale) + shift
        q = (x @ Wq + bq).reshape(B, S, N_HEAD, HEAD_DIM).transpose(0, 2, 1, 3)
        k = (x @ Wk + bk).reshape(B, S, N_HEAD, HEAD_DIM).transpose(0, 2, 1, 3)
        v = (x @ Wv + bv).reshape(B, S, N_HEAD, HEAD_DIM).transpose(0, 2, 1, 3)
        scores = jnp.einsum('bhqd,bhkd->bhqk', q / math.sqrt(HEAD_DIM), k)
        scores = scores + attention_bias
        scores = jnp.where(src_mask, -jnp.inf, scores.astype(jnp.float32))
        probs = jax.nn.softmax(scores, axis=-1).astype(v.dtype)
        ctx = jnp.einsum('bhqk,bhkd->bhqd', probs, v)
        ctx = ctx.transpose(0, 2, 1, 3).reshape(B, S, D)
        x = x + (ctx @ Wo + bo)
        h = _ln(x) * g2 + beta2
        ff = _gelu2(h @ W1 + b1) @ W2 + b2
        return x + ff

    def _L1_cond_ref(input_tensor, expert_idx, Wi, bi, Wo, bo, gamma, beta):
        import jax, jax.numpy as jnp
        import numpy as np
        E, H, I = (8, 512, 2048)
        B, S = (4, 512)
        LN_EPS = 1e-12
        Wi_b = Wi[expert_idx]
        bi_b = bi[expert_idx]
        Wo_b = Wo[expert_idx]
        bo_b = bo[expert_idx]
        g_b = gamma[expert_idx]
        be_b = beta[expert_idx]
        h = jax.nn.gelu(jnp.einsum('bsh,bhi->bsi', input_tensor, Wi_b) + bi_b[:, None, :], approximate=False)
        o = jnp.einsum('bsi,bih->bsh', h, Wo_b) + bo_b[:, None, :]
        r = o + input_tensor
        mu = jnp.mean(r, axis=-1, keepdims=True)
        var = jnp.mean(jnp.square(r - mu), axis=-1, keepdims=True)
        y = (r - mu) * jax.lax.rsqrt(var + LN_EPS)
        return y * g_b[:, None, :] + be_b[:, None, :]

    def _L2_cond_ref(hidden_states, safety_score, U, V, safety_bias, gate_w1, gate_b1, gate_w2, gate_b2, resp_w, resp_b):
        import jax, jax.numpy as jnp
        import numpy as np
        TEMPERATURE = 1.0
        ACT_THRESHOLD = 0.1
        MAX_ACT = 1.0
        SAFETY_KNOB = 1.0
        EPS = 1e-08

        def gram_schmidt(X):
            r = X.shape[1]
            Q = X
            for i in range(r):
                q = Q[:, i]
                q = q / (jnp.linalg.norm(q) + EPS)
                Q = Q.at[:, i].set(q)
                coeffs = q @ Q[:, i + 1:]
                Q = Q.at[:, i + 1:].add(-jnp.outer(q, coeffs))
            return Q
        R = resp_w.shape[1]
        U_o = gram_schmidt(U)
        V_o = gram_schmidt(V)
        basis = U_o @ V_o.T
        pooled = hidden_states.mean(axis=1)
        h1 = jax.nn.relu(pooled @ gate_w1.T + gate_b1)
        base_act = jax.nn.sigmoid(h1 @ gate_w2.T + gate_b2)
        mod = jax.nn.sigmoid(safety_score[:, None] / TEMPERATURE)
        knob = jnp.clip(jnp.asarray(SAFETY_KNOB, hidden_states.dtype), ACT_THRESHOLD, MAX_ACT)
        strength = (base_act * mod * knob)[:, None, :]
        proj = hidden_states @ basis
        feats = proj @ basis.T[:, :R]
        response = feats @ resp_w.T + resp_b + safety_bias
        return hidden_states + strength * response

    def _L3_cond_ref(hidden_states, domain_id, down_W, down_b, up_W, up_b, expert_W, expert_b, domain_emb, ln_gamma, ln_beta):
        import jax, jax.numpy as jnp
        import numpy as np
        B, S, D = (32, 512, 512)
        A = 128
        E = 16
        LN_EPS = 1e-05
        residual = hidden_states
        hidden = jnp.einsum('bsd,ad->bsa', hidden_states, down_W) + down_b
        hidden = jax.nn.gelu(hidden, approximate=False)
        valid = (domain_id >= 0) & (domain_id < E)
        idx = jnp.clip(domain_id, 0, E - 1)
        Wsel = expert_W[idx]
        bsel = expert_b[idx]
        expert_out = jnp.einsum('bsa,boa->bso', hidden, Wsel) + bsel[:, None, :]
        domain_output = jnp.where(valid[:, None, None], expert_out, hidden)
        hidden = domain_output + domain_emb[idx][:, None, :]
        hidden = jnp.einsum('bsa,da->bsd', hidden, up_W) + up_b
        x = hidden + residual
        mu = jnp.mean(x, axis=-1, keepdims=True)
        var = jnp.mean(jnp.square(x - mu), axis=-1, keepdims=True)
        return (x - mu) * jax.lax.rsqrt(var + LN_EPS) * ln_gamma + ln_beta
    x = _L0_cond_ref(x, mask_Bx1xSxS_bk0, itok_B_34_63, fside_Bx16xSxS_0, L0_cond_W_ada, L0_cond_b_ada, L0_cond_Wq, L0_cond_bq, L0_cond_Wk, L0_cond_bk, L0_cond_Wv, L0_cond_bv, L0_cond_Wo, L0_cond_bo, L0_cond_W1, L0_cond_b1, L0_cond_W2, L0_cond_b2, L0_cond_g2, L0_cond_beta2)
    x = _L1_cond_ref(x, itok_B_0_7, L1_cond_Wi, L1_cond_bi, L1_cond_Wo, L1_cond_bo, L1_cond_gamma, L1_cond_beta)
    x = _L2_cond_ref(x, condB_safetyscore, L2_cond_U, L2_cond_V, L2_cond_safety_bias, L2_cond_gate_w1, L2_cond_gate_b1, L2_cond_gate_w2, L2_cond_gate_b2, L2_cond_resp_w, L2_cond_resp_b)
    x = _L3_cond_ref(x, itok_B_0_15, L3_cond_down_W, L3_cond_down_b, L3_cond_up_W, L3_cond_up_b, L3_cond_expert_W, L3_cond_expert_b, L3_cond_domain_emb, L3_cond_ln_gamma, L3_cond_ln_beta)
    return x

_drawn_inputs = setup_inputs


def setup_inputs(seed=0):
    import zlib

    import numpy as np

    out = dict(_drawn_inputs(seed))
    spreads = {'L0_cond_b_ada': (0.0, 0.1),
     'L0_cond_bq': (0.0, 0.8),
     'L0_cond_bk': (0.0, 2.0),
     'L0_cond_bv': (0.0, 0.1),
     'L0_cond_bo': (0.0, 0.1),
     'L0_cond_b1': (0.0, 0.1),
     'L0_cond_b2': (0.0, 0.1),
     'L0_cond_g2': (1.0, 0.2),
     'L0_cond_beta2': (0.0, 0.406),
     'L1_cond_bi': (0.0, 0.1),
     'L1_cond_bo': (0.0, 0.1),
     'L1_cond_gamma': (1.0, 0.2),
     'L1_cond_beta': (0.0, 0.1),
     'L2_cond_safety_bias': (0.0, 2.0),
     'L2_cond_gate_b1': (0.0, 0.8),
     'L2_cond_resp_b': (0.0, 2.0),
     'L3_cond_ln_gamma': (1.0, 0.2),
     'L3_cond_ln_beta': (0.0, 0.1)}
    factors = {'fside_Bx16xSxS_0': 8.0,
     'condB_safetyscore': 200.0,
     'L0_cond_Wq': 8.0,
     'L0_cond_Wk': 8.0,
     'L2_cond_V': 64.0,
     'L2_cond_gate_w1': 64.0,
     'L2_cond_gate_w2': 200.0,
     'L3_cond_down_b': 8.0,
     'L2_cond_U': 64.0,
     'L2_cond_resp_w': 64.0}
    for name, (base, spread) in spreads.items():
        noise = np.random.default_rng([zlib.crc32(name.encode()), seed]).standard_normal(out[name].shape)
        drawn = base * np.exp(spread * noise) if base else spread * noise
        out[name] = jnp.asarray(drawn.astype(out[name].dtype))
    for name, factor in factors.items():
        out[name] = (out[name] * factor).astype(out[name].dtype)
    return out
```

```python
from contextlib import ExitStack

import numpy as np
import concourse.bass as bass
from concourse import mybir

ALU = mybir.AluOpType
ACT = mybir.ActivationFunctionType
F32 = mybir.dt.float32
F32R = mybir.dt.float32r
BF16 = mybir.dt.bfloat16
U8 = mybir.dt.uint8
I32 = mybir.dt.int32
RADD = bass.bass_isa.ReduceOp.add

P = 128
CH = 512
TPC = CH // P
NEG = -1.0e30
LOW = -3.0e38
TWO_PI = (6.28125, 1.9350051879882812e-3, 3.0197990e-7)
MAGIC = 12582912.0


class Count:

    def __init__(self, sem, early=0, unit=1):
        self.sem, self.early, self.unit = sem, early, unit
        self.head_start = early * unit

    def at(self, k):
        return (k + 1 + self.early) * self.unit


def sweep(eng, count, emit, head=0, tail=0, extra=0):
    for n in range(min(head, count)):
        emit(n, n % 2, n // 2)
    if count - tail > head:
        with eng.Fori(head // 2, (count - tail) // 2) as half:
            for j in range(2):
                emit(half * 2 + j, j, half)
    for n in range(max(head, count - tail), count + extra):
        emit(n, n % 2, n // 2)


def exists(n, count):
    return not isinstance(n, int) or 0 <= n < count


class Kit:

    def __init__(self, nc):
        self.nc, self.ctx, self.sems = nc, ExitStack(), []

    def sb(self, name, shape, dtype=F32):
        return self.ctx.enter_context(self.nc.sbuf_tensor(name, shape, dtype))

    def ps(self, name, shape, dtype=F32):
        return self.ctx.enter_context(self.nc.psum_tensor(name, shape, dtype))

    def sem(self, name):
        self.sems.append(self.nc.alloc_semaphore(name=name))
        return self.sems[-1]

    def count(self, name, early=0, unit=1):
        return Count(self.sem(name), early, unit)

    def __enter__(self):
        self.ctx.__enter__()
        return self

    def __exit__(self, *e):
        if e[0] is None and self.sems:
            self.nc.clear_and_free_semaphores(self.sems)
            self.nc.all_engine_barrier()
        return self.ctx.__exit__(*e)


def mm3(pe, out, a, b, start, stop):
    pe.matmul(out, a[0], b[0], start=start, stop=False)
    pe.matmul(out, a[0], b[1], start=False, stop=False)
    return pe.matmul(out, a[1], b[0], start=False, stop=stop)


def read_index(eng, index):
    return None if index is None else eng.value_load(index[0], min_val=0, max_val=index[1] - 1)


def split_weights(nc, tag, parts, index=None):
    with Kit(nc) as k:
        raw = k.sb(f"{tag}_raw", [P, 2, 2048])
        loaded = [k.count(f"{tag}_loaded{j}", unit=16) for j in range(2)]
        hi_done = k.count(f"{tag}_hi")
        lo_done = k.count(f"{tag}_lo")
        with nc.Block() as block:
            @block.sync
            def _(sp):
                e = read_index(sp, index)
                for n, (src, hi, lo, cols) in enumerate(parts):
                    if n >= 2:
                        sp.wait_ge(lo_done.sem, lo_done.at(n - 2))
                    view = src(e)
                    dst = raw[:, n % 2, 0:cols]
                    if len(view.shape) == 3:
                        dst = dst.rearrange("p (c n) -> p c n", n=view.shape[2])
                    sp.dma_start(dst, view).then_inc(loaded[n % 2].sem, 16)

            @block.scalar
            def _(act):
                for n, (src, hi, lo, cols) in enumerate(parts):
                    act.wait_ge(loaded[n % 2].sem, loaded[n % 2].at(n // 2))
                    act.activation(hi, raw[:, n % 2, 0:cols], ACT.Copy).then_inc(hi_done.sem, 1)

            @block.vector
            def _(dve):
                for n, (src, hi, lo, cols) in enumerate(parts):
                    dve.wait_ge(hi_done.sem, hi_done.at(n))
                    dve.tensor_tensor(lo, raw[:, n % 2, 0:cols], hi.bitcast(F32), ALU.subtract)\
                       .then_inc(lo_done.sem, 1)


def layer_stats(dve, st, mv, x):
    for t in range(TPC):
        dve.bn_stats(st[:, t, :], x[:, t, :])
    dve.drain()
    for t in range(TPC):
        dve.bn_aggr(mv[:, t, :], st[:, t, :])
    dve.drain()


def prepare(nc, d, scale1, shift, batches, dim):
    KT = dim // P
    with Kit(nc) as k:
        t_raw = k.sb("t_raw", [P, batches], I32)
        freqs = k.sb("freqs", [P, 2])
        w_ada = k.sb("w_ada", [P, KT, 2 * dim])
        b_ada = k.sb("b_ada", [P, 2 * dim])
        t = k.sb("t_f", [P, batches])
        q = k.sb("q", [P, batches])
        qh = k.sb("qh", [P, batches], F32R)
        ql = k.sb("ql", [P, batches])
        r = k.sb("r", [P, batches])
        x = k.sb("x_ang", [P, batches])
        e = k.sb("e", [P, batches, 2])
        turns = k.sb("turns", [P, batches, 2])
        ang = k.sb("ang", [P, batches, KT])
        sc = k.sb("sc_tab", [P, batches, KT])
        sg = k.sb("sg", [P, batches, KT])
        feat = k.sb("feat", [P, batches, KT])
        ones = k.sb("ones_p", [P, P])
        spread = k.sb("spread", [P, batches, KT, P])
        rows = k.ps("rows", [P, batches, 2, dim])
        loaded = k.sem("p_loaded")
        ang_ready, sin_ready, sig_ready = k.sem("ang_ready"), k.sem("sin_ready"), k.sem("sig_ready")
        spread_ready, rows_ready = k.sem("spread_ready"), k.sem("rows_ready")
        with nc.Block() as block:
            @block.sync
            def _(sp):
                sp.dma_start(t_raw[:], d["itok_B_34_63"].partition_broadcast(P)).then_inc(loaded, 16)
                sp.dma_start(freqs[:], d["freqs"]).then_inc(loaded, 16)
                sp.dma_start(w_ada[:], d["L0_cond_W_ada"].rearrange("(c p) n -> p c n", p=P)).then_inc(loaded, 16)
                sp.dma_start(b_ada[:], d["L0_cond_b_ada"].partition_broadcast(P)).then_inc(loaded, 16)

            @block.vector
            def _(dve):
                dve.wait_ge(loaded, 64)
                dve.memset(ones[:], 1.0)
                dve.tensor_copy(t[:], t_raw[:])
                dve.drain()
                dve.tensor_scalar(q[:], t[:], 0.01, None, ALU.mult)
                dve.drain()
                dve.tensor_copy(qh[:], q[:])
                dve.drain()
                dve.tensor_tensor(ql[:], q[:], qh[:].bitcast(F32), ALU.subtract)
                dve.drain()
                dve.scalar_tensor_tensor(out=r[:], in0=qh[:].bitcast(F32), scalar=-100.0, in1=t[:], op0=ALU.mult, op1=ALU.add)
                dve.drain()
                dve.scalar_tensor_tensor(out=x[:], in0=ql[:], scalar=-100.0, in1=r[:], op0=ALU.mult, op1=ALU.add)
                dve.drain()
                dve.scalar_tensor_tensor(out=r[:], in0=x[:], scalar=0.01, in1=q[:], op0=ALU.mult, op1=ALU.add)
                dve.drain()
                dve.tensor_scalar(x[:], r[:], 4000.0, None, ALU.mult)
                dve.drain()
                for b in range(batches):
                    dve.tensor_scalar(e[:, b, :], freqs[:], x[:, b:b + 1], None, ALU.mult)
                dve.drain()
                dve.tensor_scalar(turns[:], e[:], 1.0 / (2.0 * np.pi), MAGIC, ALU.mult, ALU.add)
                dve.drain()
                dve.tensor_scalar(turns[:], turns[:], MAGIC, None, ALU.subtract)
                for c in TWO_PI:
                    dve.drain()
                    dve.scalar_tensor_tensor(out=e[:], in0=turns[:], scalar=-c, in1=e[:], op0=ALU.mult, op1=ALU.add)
                dve.drain()
                dve.tensor_scalar(ang[:, :, 0:2], e[:], 3.1415925, -3.1415925, ALU.min, ALU.max)
                dve.tensor_scalar(turns[:], e[:], -1.0, None, ALU.mult)
                dve.drain()
                dve.tensor_tensor(turns[:], turns[:], e[:], ALU.max)
                dve.drain()
                dve.tensor_scalar(ang[:, :, 2:4], turns[:], -1.0, float(np.pi / 2), ALU.mult, ALU.add)
                dve.drain()
                dve.tensor_scalar(turns[:], turns[:], -1.0, None, ALU.mult).then_inc(ang_ready, 1)
                dve.wait_ge(sig_ready, 1)
                dve.tensor_tensor(feat[:], sc[:], sg[:], ALU.mult)
                dve.drain()
                for b in range(batches):
                    for c in range(KT):
                        last = dve.tensor_scalar(spread[:, b, c, :], ones[:], feat[:, b, c:c + 1], None, ALU.mult)
                last.then_inc(spread_ready, 1)
                dve.wait_ge(rows_ready, 1)
                for b in range(batches):
                    dve.tensor_tensor(scale1[:, b, :], rows[:, b, 0, :], b_ada[:, 0:dim], ALU.add)
                    dve.tensor_tensor(shift[:, b, :], rows[:, b, 1, :], b_ada[:, dim:], ALU.add)
                dve.drain()
                dve.tensor_scalar(scale1[:], scale1[:], 1.0, None, ALU.add)

            @block.scalar
            def _(act):
                act.wait_ge(ang_ready, 1)
                act.activation(sc[:], ang[:], ACT.Sin).then_inc(sin_ready, 1)
                act.wait_ge(sin_ready, 1)
                act.activation(sg[:], sc[:], ACT.Sigmoid).then_inc(sig_ready, 1)

            @block.tensor
            def _(pe):
                pe.wait_ge(spread_ready, 1)
                for b in range(batches):
                    for part in range(2):
                        for c in range(KT):
                            last = pe.matmul(rows[:, b, part, :], spread[:, b, c, :],
                                             w_ada[:, c, part * dim:(part + 1) * dim],
                                             start=(c == 0), stop=(c == KT - 1))
                last.then_inc(rows_ready, 1)


def project(nc, d, s, ident, scale1, shift, batches, seq, dim, heads):
    KT = dim // P
    HD = dim // heads
    NCB = seq // CH
    n_chunks = batches * NCB
    q_scale = float(HD) ** -0.5
    src_v = d["x"].rearrange("b (n t p) c -> (b n) p t c", p=P, t=TPC)
    x0_v = s["x0"].rearrange("(n t p) c -> n p t c", p=P, t=TPC)
    v_v = s["v"].rearrange("(n t p) c -> n t p c", p=P, t=TPC)
    with Kit(nc) as k:
        w = {n: (k.sb(f"{n}_hi", [P, KT, dim], F32R), k.sb(f"{n}_lo", [P, KT, dim], F32R)) for n in ("wq", "wk", "wv")}
        split_weights(nc, "pw", [
            (lambda e, n=n: d["L0_cond_W" + n[1]].rearrange("(c p) n -> p c n", p=P), w[n][0][:].rearrange("p c n -> p (c n)"),
             w[n][1][:].rearrange("p c n -> p (c n)"), KT * dim) for n in ("wq", "wk", "wv")])
        b_qk = k.sb("b_qk", [P, 2, KT])
        b_v = k.sb("b_v", [P, dim])
        xin = k.sb("xin", [P, 2, TPC, dim])
        xm = k.sb("xm", [P, 2, TPC, dim])
        st = k.sb("st", [P, TPC, 6])
        mv = k.sb("mv", [P, TPC, 2])
        sd = k.sb("sd", [P, TPC])
        rstd = k.sb("rstd", [P, TPC])
        xT = [[k.sb(f"xT{j}{h}", [P, KT, CH], F32R) for h in ("hi", "lo")] for j in range(2)]
        full = k.sb("full", [P, 2, CH])
        parts = [[k.sb(f"part{j}{h}", [P, CH], F32R) for h in ("hi", "lo")] for j in range(2)]
        vt = k.sb("vt", [P, 2, dim])
        turned = k.ps("turned", [P, 2, KT, P])
        pqk = k.ps("pqk", [P, 4, CH])
        pv = k.ps("pv", [P, 2, dim])
        consts = k.sem("consts")
        src_in = [k.count(f"src_in{j}", unit=16) for j in range(2)]
        var_ready, sd_ready = k.count("var_ready"), k.count("sd_ready")
        xm_ready = k.count("xm_ready", early=2)
        x0_out = [k.count(f"x0_out{j}", early=1, unit=16) for j in range(2)]
        tiles_turned = k.count("tiles_turned")
        hi_ready = k.count("hi_ready")
        lo_ready = k.count("lo_ready", early=2)
        qk_ready, v_ready = k.count("qk_ready"), k.count("v_ready", early=2 * TPC)
        full_ready = k.count("full_ready", early=4)
        parts_ready = k.count("parts_ready", early=2)
        parts_out = [k.count(f"parts_out{j}", early=1, unit=32) for j in range(2)]
        vt_ready = k.count("vt_ready", early=2)
        v_out = [k.count(f"v_out{j}", early=1, unit=16) for j in range(2)]
        passed = k.sem("passed_p")
        bias_ready = k.sem("bias_ready")
        NQK = 2 * KT

        with nc.Block() as block:
            @block.gpsimd
            def _(pool):
                pool.dma_start(b_qk[:, 0, :], d["L0_cond_bq"].rearrange("(c p) -> p c", p=P)).then_inc(consts, 16)
                pool.dma_start(b_qk[:, 1, :], d["L0_cond_bk"].rearrange("(c p) -> p c", p=P)).then_inc(consts, 16)
                pool.dma_start(b_v[:], d["L0_cond_bv"].partition_broadcast(P)).then_inc(consts, 16)

                def load(n, j, half):
                    pool.wait_ge(xm_ready.sem, xm_ready.at(n - 2))
                    pool.sem_inc(passed, 1)
                    pool.dma_start(xin[:, j], src_v[n]).then_inc(src_in[j].sem, 16)
                sweep(pool, n_chunks, load)

            @block.sync
            def _(sp):
                for c in x0_out + parts_out + v_out:
                    sp.sem_inc(c.sem, c.head_start)
                with sp.Fori(0, batches) as b:
                    with sp.Fori(0, NCB // 2) as half:
                        for j in range(2):
                            nb = half * 2 + j
                            n = b * NCB + nb
                            sp.wait_ge(xm_ready.sem, xm_ready.at(n))
                            sp.dma_start(x0_v[n], xm[:, j]).then_inc(x0_out[j].sem, 16)
                            for p in range(NQK):
                                sp.wait_ge(parts_ready.sem, parts_ready.at(n * NQK + p))
                                dst = s["q"] if p < KT else s["k"]
                                for part in range(2):
                                    sp.dma_start(dst[b, p % KT, part, :, bass.ds(nb * CH, CH)], parts[p % 2][part][:].bitcast(F32))\
                                      .then_inc(parts_out[p % 2].sem, 16)
                            for t in range(TPC):
                                sp.wait_ge(vt_ready.sem, vt_ready.at(n * TPC + t))
                                sp.dma_start(v_v[n, t], vt[:, t % 2]).then_inc(v_out[t % 2].sem, 16)
                for j in range(2):
                    sp.wait_ge(x0_out[j].sem, x0_out[j].at(n_chunks // 2 - 1))
                    sp.wait_ge(parts_out[j].sem, parts_out[j].at(n_chunks * NQK // 2 - 1))
                    sp.wait_ge(v_out[j].sem, v_out[j].at(n_chunks * TPC // 2 - 1))

            @block.vector
            def _(dve):
                for c in (xm_ready, lo_ready, parts_ready, vt_ready):
                    dve.sem_inc(c.sem, c.head_start)
                dve.wait_ge(consts, 48)
                dve.tensor_scalar(b_qk[:, 0, :], b_qk[:, 0, :], q_scale, None, ALU.mult).then_inc(bias_ready, 1)
                with dve.Fori(0, batches) as b:
                    with dve.Fori(0, NCB // 2) as half:
                        for j in range(2):
                            n = b * NCB + half * 2 + j
                            use = b * (NCB // 2) + half
                            dve.wait_ge(src_in[j].sem, src_in[j].at(use))
                            dve.wait_ge(x0_out[j].sem, x0_out[j].at(use - 1))
                            layer_stats(dve, st, mv, xin[:, j])
                            dve.tensor_scalar(rstd[:], mv[:, :, 1], 1e-5, None, ALU.add).then_inc(var_ready.sem, 1)
                            dve.wait_ge(sd_ready.sem, sd_ready.at(n))
                            dve.reciprocal(rstd[:], sd[:])
                            dve.drain()
                            for t in range(TPC):
                                dve.tensor_scalar(xm[:, j, t, :], xin[:, j, t, :], mv[:, t, 0:1], rstd[:, t:t + 1],
                                                  ALU.subtract, ALU.mult)
                            dve.drain()
                            for t in range(TPC):
                                dve.tensor_tensor(xm[:, j, t, :], xm[:, j, t, :], scale1[:, b, :], ALU.mult)
                            dve.drain()
                            for t in range(TPC):
                                last = dve.tensor_tensor(xm[:, j, t, :], xm[:, j, t, :], shift[:, b, :], ALU.add)
                            last.then_inc(xm_ready.sem, 1)
                            for t in range(TPC):
                                dve.wait_ge(hi_ready.sem, hi_ready.at(n * TPC + t))
                                dve.tensor_tensor(xT[j][1][:, :, t * P:(t + 1) * P], turned[:, t % 2],
                                                  xT[j][0][:, :, t * P:(t + 1) * P].bitcast(F32), ALU.subtract)\
                                   .then_inc(lo_ready.sem, 1)
                            for p in range(NQK):
                                dve.wait_ge(full_ready.sem, full_ready.at(n * NQK + p))
                                dve.wait_ge(parts_out[p % 2].sem, parts_out[p % 2].at(n * (NQK // 2) + p // 2 - 1))
                                hi, lo = parts[p % 2]
                                dve.tensor_copy(hi[:], full[:, p % 2])
                                dve.drain()
                                dve.tensor_tensor(lo[:], full[:, p % 2], hi[:].bitcast(F32), ALU.subtract)\
                                   .then_inc(parts_ready.sem, 1)
                            for t in range(TPC):
                                dve.wait_ge(v_ready.sem, v_ready.at(n * TPC + t))
                                dve.wait_ge(v_out[t % 2].sem, v_out[t % 2].at(n * (TPC // 2) + t // 2 - 1))
                                dve.tensor_tensor(vt[:, t % 2], pv[:, t % 2], b_v[:], ALU.add).then_inc(vt_ready.sem, 1)

            @block.scalar
            def _(act):
                act.sem_inc(full_ready.sem, full_ready.head_start)
                act.wait_ge(bias_ready, 1)

                def chunk(n, j, half):
                    act.wait_ge(var_ready.sem, var_ready.at(n))
                    act.activation(sd[:], rstd[:], ACT.Sqrt).then_inc(sd_ready.sem, 1)
                    act.wait_ge(v_ready.sem, v_ready.at((n - 1) * TPC - 1))
                    for t in range(TPC):
                        act.wait_ge(tiles_turned.sem, tiles_turned.at(n * TPC + t))
                        act.activation(xT[j][0][:, :, t * P:(t + 1) * P], turned[:, t % 2], ACT.Copy).then_inc(hi_ready.sem, 1)
                    for p in range(NQK):
                        act.wait_ge(qk_ready.sem, qk_ready.at(n * NQK + p))
                        act.wait_ge(parts_ready.sem, parts_ready.at(n * NQK + p - 2))
                        act.activation(full[:, p % 2], pqk[:, p % 4], ACT.Identity,
                                       bias=b_qk[:, p // KT, p % KT:p % KT + 1],
                                       scale=q_scale if p < KT else 1.0).then_inc(full_ready.sem, 1)
                sweep(act, n_chunks, chunk)

            @block.tensor
            def _(pe):
                pe.sem_inc(v_ready.sem, v_ready.head_start)

                def chunk(n, j, half):
                    pe.wait_ge(xm_ready.sem, xm_ready.at(n))
                    for t in range(TPC):
                        pe.wait_ge(lo_ready.sem, lo_ready.at(n * TPC + t - 2))
                        for c in range(KT):
                            last = pe.transpose(turned[:, t % 2, c, :], xm[:, j, t, c * P:(c + 1) * P], ident[:])
                        last.then_inc(tiles_turned.sem, 1)
                    pe.wait_ge(lo_ready.sem, lo_ready.at(n * TPC + TPC - 1))
                    for p in range(NQK):
                        pe.wait_ge(full_ready.sem, full_ready.at(n * NQK + p - 4))
                        wh, wl = w["wq" if p < KT else "wk"]
                        o = (p % KT) * P
                        for c in range(KT):
                            last = mm3(pe, pqk[:, p % 4], (wh[:, c, o:o + P], wl[:, c, o:o + P]),
                                       (xT[j][0][:, c, :], xT[j][1][:, c, :]), c == 0, c == KT - 1)
                        last.then_inc(qk_ready.sem, 1)
                    for t in range(TPC):
                        pe.wait_ge(vt_ready.sem, vt_ready.at(n * TPC + t - 2))
                        for c in range(KT):
                            last = mm3(pe, pv[:, t % 2], (xT[j][0][:, c, t * P:(t + 1) * P], xT[j][1][:, c, t * P:(t + 1) * P]),
                                       (w["wv"][0][:, c, :], w["wv"][1][:, c, :]), c == 0, c == KT - 1)
                        last.then_inc(v_ready.sem, 1)
                sweep(pe, n_chunks, chunk)


def attend(nc, d, s, ident, batches, seq, dim, heads):
    NT = seq // P
    HD = dim // heads
    HG = P // HD
    groups = batches * heads // HG
    NG = heads // HG
    n_it = groups * NT
    n_heads = n_it * HG
    HALF = seq // 2
    MM = min(HALF, 512)
    CT = 4
    TURNS = NT // CT
    bias_v = d["fside_Bx16xSxS_0"].rearrange("b (g i) (t p) m -> (b g) i t p m", i=HG, p=P)
    mask_v = d["mask_Bx1xSxS_bk0"].rearrange("b o (t p) m -> (b o) t p m", p=P)
    q_v = s["q"].rearrange("b g a (i r) (t m) -> (b g) t a r i m", i=HG, m=P)
    k_v = s["k"].rearrange("b g a (i r) m -> (b g) a i r m", i=HG)
    v_v = s["v"].rearrange("(b t p) (g m) -> b g p t m", p=P, b=batches, m=P)
    with Kit(nc) as k:
        scores = k.sb("scores", [P, 2, HG, seq])
        keys = [k.sb(f"keys{h}", [P, seq], F32R) for h in range(HG)]
        queries = [k.sb(f"queries{j}", [P, HG, P], F32R) for j in range(2)]
        values = k.sb("values", [P, NT, P])
        mask = k.sb("mask", [P, 2, seq], BF16)
        neg_ident = k.sb("neg_ident", [P, P], BF16)
        probsT = k.sb("probsT", [P, 2, HG, NT, P])
        top = k.sb("top", [P, HG, 2])
        neg_top = k.sb("neg_top", [P, HG])
        sums = k.sb("sums", [P, 2, HG])
        inv = k.sb("inv", [P, 2, HG])
        ctxT = k.sb("ctxT", [P, P])
        ctx_rows = k.sb("ctx_rows", [P, 2, P])
        ps_s = k.ps("ps_s", [P, 2, 1024])
        ps_t = k.ps("ps_t", [P, 2, 512])
        ps_pv = k.ps("ps_pv", [P, 512])
        ps_c = k.ps("ps_c", [P, 512])

        bias_in = [[k.count(f"bias_in{j}{h}", unit=16) for h in range(HG)] for j in range(2)]
        k_in = [k.count(f"k_in{h}", unit=64) for h in range(HG)]
        q_in = [k.count(f"q_in{j}", unit=64) for j in range(2)]
        v_in = k.count("v_in", unit=16)
        mask_in = [k.count(f"mask_in{j}", unit=16) for j in range(2)]
        neg_ready = k.sem("neg_ready")
        kq_ready = k.count("kq_ready")
        v_ready = k.count("v_ready_b", early=1)
        qk_done = k.count("qk_done")
        scored = k.count("scored", early=2)
        top_ready = k.count("top_ready", early=8)
        exp_done = k.count("exp_done")
        TB = TURNS // 2
        turned = [k.count(f"turned{x}", early=2 * HG * TB) for x in range(2)]
        moved = [k.count(f"moved{x}", early=1) for x in range(2)]
        pv_done = k.count("pv_done", early=2)
        ctxT_ready = k.count("ctxT_ready", early=1)
        ctx_turned = k.count("ctx_turned", early=1)
        inv_ready = k.count("inv_ready", early=2)
        ctx_ready = k.count("ctx_ready", early=1)
        ctx_out = [k.count(f"ctx_out{j}", early=1, unit=16) for j in range(2)]
        passed = k.sem("passed")

        def after_exists(it):
            return not isinstance(it, int) or 0 <= it + 1 < n_it

        def before_exists(it, back):
            return not isinstance(it, int) or 0 <= it - back < n_it

        with nc.Block() as block:
            @block.sync
            def _(sp):
                with sp.Fori(0, groups) as g:
                    with sp.Fori(0, NT // 2) as half:
                        for j in range(2):
                            t = half * 2 + j
                            it = g * NT + t
                            for h in range(HG):
                                if h == 2:
                                    sp.wait_ge(top_ready.sem, top_ready.at(it * HG - HG - 1))
                                    for u in range(4):
                                        sp.dma_start(queries[j][u * HD:(u + 1) * HD].bitcast(F32), q_v[g, t, u // 2])\
                                          .then_inc(q_in[j].sem, 16)
                                sp.wait_ge(turned[1].sem, turned[1].at((it * HG + h - 2 * HG) * TB + TB - 1))
                                sp.dma_start(scores[:, j, h, :], bias_v[g, h, t]).then_inc(bias_in[j][h].sem, 16)

            @block.gpsimd
            def _(pool):
                pool.wait_ge(neg_ready, 1)
                with pool.Fori(0, batches) as b:
                  with pool.Fori(0, NG) as gg:
                    g = b * NG + gg

                    def load_keys(h):
                        pool.wait_ge(top_ready.sem, top_ready.at(g * NT * HG - HG + h))
                        pool.sem_inc(passed, 1)
                        for u in range(4):
                            pool.dma_start(keys[h][u * HD:(u + 1) * HD].bitcast(F32), k_v[g, u % 2, h]).then_inc(k_in[h].sem, 16)

                    def tile(half, j, first):
                        t = half * 2 + j
                        it = g * NT + t
                        use = g * (NT // 2) + half
                        pool.wait_ge(top_ready.sem, top_ready.at(it * HG - HG - 1))
                        pool.sem_inc(passed, 1)
                        pool.dma_start(mask[:, j], mask_v[b, t]).then_inc(mask_in[j].sem, 16)
                        if first and j == 0:
                            load_keys(0)
                        pool.wait_ge(mask_in[j].sem, mask_in[j].at(use))
                        pool.sem_inc(passed, 1)
                        pool.wait_ge(q_in[j].sem, q_in[j].at(use))
                        pool.sem_inc(passed, 1)
                        for h in range(HG):
                            if first and j == 0:
                                if h < HG - 1:
                                    load_keys(h + 1)
                                pool.wait_ge(k_in[h].sem, k_in[h].at(g))
                                pool.sem_inc(passed, 1)
                            pool.sem_inc(kq_ready.sem, 1)
                        if first and j == 1:
                            pool.wait_ge(pv_done.sem, pv_done.at(it - 2))
                            pool.sem_inc(passed, 1)
                            pool.dma_start(values[:], v_v[b, gg]).then_inc(v_in.sem, 16)
                            pool.wait_ge(v_in.sem, v_in.at(g))
                            pool.sem_inc(passed, 1)
                        pool.sem_inc(v_ready.sem, 1)

                    for j in range(2):
                        tile(0, j, True)
                    with pool.Fori(1, NT // 2) as half:
                        for j in range(2):
                            tile(half, j, False)
                pool.sem_inc(v_ready.sem, 1)

            @block.tensor
            def _(pe):
                for c in turned + [pv_done, ctx_turned]:
                    pe.sem_inc(c.sem, c.head_start)

                def qk(n, j, h, half):
                    if half == 0:
                        pe.wait_ge(kq_ready.sem, kq_ready.at(n))
                    pe.wait_ge(scored.sem, scored.at(2 * n + half - 2))
                    for c in range(HALF // MM):
                        a = half * HALF + c * MM
                        out = ps_s[:, half, c * MM:(c + 1) * MM]
                        pe.matmul(out, queries[j][:, h, :], keys[h][:, a:a + MM], start=True, stop=False)
                        last = pe.matmul(out, neg_ident[:], mask[:, j, a:a + MM], start=False, stop=True)
                    last.then_inc(qk_done.sem, 1)

                def turn(n, j, h, half):
                    if half == 0:
                        pe.wait_ge(exp_done.sem, exp_done.at(n))
                    for c in range(half * TURNS // 2, (half + 1) * TURNS // 2):
                        pe.wait_ge(moved[c % 2].sem, moved[c % 2].at(n * TB + c // 2 - 1))
                        for i in range(CT):
                            kt = c * CT + i
                            last = pe.transpose(ps_t[:, c % 2, i * P:(i + 1) * P], scores[:, j, h, kt * P:(kt + 1) * P], ident[:])
                        last.then_inc(turned[c % 2].sem, 1)

                def pv(it, j, quarter):
                    if quarter == 0:
                        pe.wait_ge(v_ready.sem, v_ready.at(it))
                        for x in range(2):
                            pe.wait_ge(moved[x].sem, moved[x].at((it * HG + HG) * TB - 1))
                        pe.wait_ge(ctxT_ready.sem, ctxT_ready.at(it - 1))
                    for kt in range(quarter * NT // HG, (quarter + 1) * NT // HG):
                        for h in range(HG):
                            last = pe.matmul(ps_pv[h * HD:(h + 1) * HD, 0:P], values[:, kt, h * HD:(h + 1) * HD],
                                             probsT[:, j, h, kt, :], start=(kt == 0), stop=(kt == NT - 1), skip_group_check=True)
                    if quarter == HG - 1:
                        last.then_inc(pv_done.sem, 1)

                def turn_ctx(it):
                    pe.wait_ge(ctxT_ready.sem, ctxT_ready.at(it))
                    pe.wait_ge(ctx_ready.sem, ctx_ready.at(it - 1))
                    pe.transpose(ps_c[:, 0:P], ctxT[:], ident[:]).then_inc(ctx_turned.sem, 1)

                def step(it, j, half):
                    for h in range(HG):
                        for x in range(2):
                            if h < 2 and exists(it, n_it):
                                qk(it * HG + h + 2, j, h + 2, x)
                            if h >= 2 and after_exists(it):
                                qk(it * HG + h + 2, 1 - j, h - 2, x)
                            if exists(it, n_it):
                                turn(it * HG + h, j, h, x)
                        if before_exists(it, 1):
                            pv(it - 1, 1 - j, h)
                        if h == 1 and before_exists(it, 2):
                            turn_ctx(it - 2)

                pe.wait_ge(neg_ready, 1)
                for h in range(2):
                    for x in range(2):
                        qk(h, 0, h, x)
                sweep(pe, n_it, step, head=2, tail=2, extra=2)

            @block.vector
            def _(dve):
                for c in (scored, top_ready, moved[0], ctxT_ready, ctx_ready, inv_ready):
                    dve.sem_inc(c.sem, c.head_start)
                dve.tensor_scalar(neg_ident[:], ident[:], NEG, None, ALU.mult).then_inc(neg_ready, 1)

                def score(n, j, h, it, half, x):
                    if x == 0:
                        dve.wait_ge(bias_in[j][h].sem, bias_in[j][h].at(half))
                    else:
                        dve.wait_ge(scored.sem, scored.at(2 * n))
                    dve.wait_ge(qk_done.sem, qk_done.at(2 * n + x))
                    dve.sem_inc(passed, 1)
                    part = scores[:, j, h, x * HALF:(x + 1) * HALF]
                    dve.tensor_tensor_reduce(out=part, in0=ps_s[:, x, 0:HALF], in1=part, scale=1.0,
                                             scalar=LOW if x == 0 else top[:, h, 0:1], op0=ALU.add, op1=ALU.max,
                                             accum_out=top[:, h, x:x + 1]).then_inc(scored.sem, 1)

                def negate(n, h):
                    dve.wait_ge(scored.sem, scored.at(2 * n + 1))
                    dve.tensor_scalar(neg_top[:, h:h + 1], top[:, h, 1:2], -1.0, None, ALU.mult).then_inc(top_ready.sem, 1)

                def move(n, j, h, x):
                    for c in range(x * TURNS // 2, (x + 1) * TURNS // 2):
                        if c % 2 == 0:
                            dve.wait_ge(turned[0].sem, turned[0].at(n * TB + c // 2))
                            dve.tensor_copy(probsT[:, j, h, c * CT:(c + 1) * CT, :],
                                            ps_t[:, 0].rearrange("p (i m) -> p i m", m=P)).then_inc(moved[0].sem, 1)

                def step(it, j, half):
                    here = exists(it, n_it)
                    for h in range(HG):
                        ahead = here if h < 2 else after_exists(it)
                        for x in range(2):
                            if ahead and h < 2:
                                score(it * HG + h + 2, j, h + 2, it, half, x)
                            if ahead and h >= 2:
                                score(it * HG + h + 2, 1 - j, h - 2, it + 1, half + j, x)
                            if here:
                                if h == 0 and x == 0:
                                    dve.wait_ge(pv_done.sem, pv_done.at(it - 2))
                                move(it * HG + h, j, h, x)
                        if ahead:
                            negate(it * HG + h + 2, (h + 2) % HG)
                        if h == 0 and before_exists(it, 2):
                            dve.wait_ge(pv_done.sem, pv_done.at(it - 2))
                            dve.wait_ge(ctx_turned.sem, ctx_turned.at(it - 3))
                            dve.tensor_copy(ctxT[:], ps_pv[:, 0:P]).then_inc(ctxT_ready.sem, 1)
                        if h == 2 and before_exists(it, 2):
                            dve.wait_ge(ctx_turned.sem, ctx_turned.at(it - 2))
                            dve.wait_ge(ctx_out[j].sem, ctx_out[j].at(half - 2))
                            dve.tensor_tensor(ctx_rows[:, j].rearrange("p (h m) -> p h m", m=HD),
                                              ps_c[:, 0:P].rearrange("p (h m) -> p h m", m=HD),
                                              inv[:, j, :].unsqueeze(2).broadcast_to([P, HG, HD]), ALU.mult).then_inc(ctx_ready.sem, 1)
                    if here:
                        dve.drain()
                        dve.wait_ge(exp_done.sem, exp_done.at(it * HG + HG - 1))
                        dve.reciprocal(inv[:, j, :], sums[:, j, :]).then_inc(inv_ready.sem, 1)

                for h in range(2):
                    for x in range(2):
                        score(h, 0, h, 0, 0, x)
                    negate(h, h)
                sweep(dve, n_it, step, head=2, tail=2, extra=2)

            @block.scalar
            def _(act):
                act.sem_inc(moved[1].sem, moved[1].head_start)
                for c in ctx_out:
                    act.sem_inc(c.sem, c.head_start)

                def exp(n, j, h):
                    act.wait_ge(top_ready.sem, top_ready.at(n))
                    act.activation(scores[:, j, h, :], scores[:, j, h, :], ACT.Exp, bias=neg_top[:, h:h + 1],
                                   accum_out=sums[:, j, h:h + 1]).then_inc(exp_done.sem, 1)

                def step(it, j, half):
                    here = exists(it, n_it)
                    for h in range(HG):
                        if h < HG - 1 and here:
                            exp(it * HG + h + 1, j, h + 1)
                        if h == HG - 1 and after_exists(it):
                            act.wait_ge(inv_ready.sem, inv_ready.at(it - 1))
                            exp(it * HG + HG, 1 - j, 0)
                        if here:
                            if h == 0:
                                act.wait_ge(pv_done.sem, pv_done.at(it - 2))
                            for c in range(1, TURNS, 2):
                                act.wait_ge(turned[1].sem, turned[1].at((it * HG + h) * TB + c // 2))
                                act.activation(probsT[:, j, h, c * CT:(c + 1) * CT, :],
                                               ps_t[:, 1].rearrange("p (i m) -> p i m", m=P), ACT.Copy).then_inc(moved[1].sem, 1)

                    if before_exists(it, 2):
                        act.wait_ge(ctx_ready.sem, ctx_ready.at(it - 2))
                        act.dma_start(s["ctx"][it - 2], ctx_rows[:, j]).then_inc(ctx_out[j].sem, 16)

                exp(0, 0, 0)
                sweep(act, n_it, step, head=2, tail=2, extra=2)
                for j in range(2):
                    act.wait_ge(ctx_out[j].sem, ctx_out[j].at(n_it // 2 - 1))


def out_proj(nc, d, s, ident, batches, seq, dim, heads):
    KT = dim // P
    NT = seq // P
    NCB = seq // CH
    n_chunks = batches * NCB
    ctx_v = s["ctx"].rearrange("(b g t) p m -> b t p g m", b=batches, t=NT)
    x0_v = s["x0"].rearrange("(n t p) c -> n p t c", p=P, t=TPC)
    x1_v = s["x1"].rearrange("(n t p) c -> n p t c", p=P, t=TPC)
    with Kit(nc) as k:
        wo = (k.sb("wo_hi", [P, KT, dim], F32R), k.sb("wo_lo", [P, KT, dim], F32R))
        split_weights(nc, "ow", [(lambda e: d["L0_cond_Wo"].rearrange("(c p) n -> p c n", p=P),
                                  wo[0][:].rearrange("p c n -> p (c n)"), wo[1][:].rearrange("p c n -> p (c n)"), KT * dim)])
        bo = k.sb("bo", [P, dim])
        ctx = k.sb("ctx_in", [P, 2, TPC, dim])
        x0 = k.sb("x0_in", [P, 2, TPC, dim])
        x1 = k.sb("x1_sb", [P, 2, TPC, dim])
        cT = [[k.sb(f"cT{j}{h}", [P, KT, P], F32R) for h in ("hi", "lo")] for j in range(2)]
        turned = k.ps("turned_o", [P, 2, KT, P])
        out = k.ps("out_o", [P, 4, dim])
        consts = k.sem("consts_o")
        ctx_in = [k.count(f"ctx_in{j}", unit=16 * TPC) for j in range(2)]
        x0_in = [k.count(f"x0_in{j}", unit=16) for j in range(2)]
        tile_turned, hi_ready = k.count("tile_turned"), k.count("hi_ready_o", early=2)
        lo_ready = k.count("lo_ready_o", early=2)
        out_done = k.count("out_done", early=2)
        passed = k.sem("passed_o")
        x1_ready = k.count("x1_ready", early=2 * TPC)
        x1_out = [k.count(f"x1_out{j}", early=1, unit=16) for j in range(2)]
        with nc.Block() as block:
            @block.gpsimd
            def _(pool):
                pool.dma_start(bo[:], d["L0_cond_bo"].partition_broadcast(P)).then_inc(consts, 16)
                with pool.Fori(0, batches) as b:
                    with pool.Fori(0, NCB // 2) as half:
                        for j in range(2):
                            nb = half * 2 + j
                            n = b * NCB + nb
                            pool.wait_ge(x1_ready.sem, x1_ready.at((n - 1) * TPC - 1))
                            pool.sem_inc(passed, 1)
                            for t in range(TPC):
                                pool.dma_start(ctx[:, j, t].rearrange("p (g m) -> p g m", m=P), ctx_v[b, nb * TPC + t])\
                                    .then_inc(ctx_in[j].sem, 16)
                            pool.dma_start(x0[:, j], x0_v[n]).then_inc(x0_in[j].sem, 16)

            @block.sync
            def _(sp):
                for c in x1_out:
                    sp.sem_inc(c.sem, c.head_start)

                def store(n, j, half):
                    sp.wait_ge(x1_ready.sem, x1_ready.at((n + 1) * TPC - 1))
                    sp.dma_start(x1_v[n], x1[:, j]).then_inc(x1_out[j].sem, 16)
                sweep(sp, n_chunks, store)
                for j in range(2):
                    sp.wait_ge(x1_out[j].sem, x1_out[j].at(n_chunks // 2 - 1))

            @block.tensor
            def _(pe):
                pe.sem_inc(out_done.sem, out_done.head_start)

                def chunk(n, j, half):
                    pe.wait_ge(ctx_in[j].sem, ctx_in[j].at(half))
                    for t in range(TPC + 1):
                        if t < TPC:
                            pe.wait_ge(lo_ready.sem, lo_ready.at(n * TPC + t - 2))
                            for c in range(KT):
                                last = pe.transpose(turned[:, t % 2, c, :], ctx[:, j, t, c * P:(c + 1) * P], ident[:])
                            last.then_inc(tile_turned.sem, 1)
                        if t >= 1:
                            u = t - 1
                            pe.wait_ge(lo_ready.sem, lo_ready.at(n * TPC + u))
                            pe.wait_ge(x1_ready.sem, x1_ready.at(n * TPC + u - 4))
                            for c in range(KT):
                                last = mm3(pe, out[:, u, :], (cT[u % 2][0][:, c, :], cT[u % 2][1][:, c, :]),
                                           (wo[0][:, c, :], wo[1][:, c, :]), c == 0, c == KT - 1)
                            last.then_inc(out_done.sem, 1)
                sweep(pe, n_chunks, chunk)

            @block.scalar
            def _(act):
                act.sem_inc(hi_ready.sem, hi_ready.head_start)

                def chunk(n, j, half):
                    for t in range(TPC):
                        act.wait_ge(out_done.sem, out_done.at(n * TPC + t - 2))
                        act.wait_ge(tile_turned.sem, tile_turned.at(n * TPC + t))
                        act.activation(cT[t % 2][0][:], turned[:, t % 2], ACT.Copy).then_inc(hi_ready.sem, 1)
                sweep(act, n_chunks, chunk)

            @block.vector
            def _(dve):
                dve.sem_inc(lo_ready.sem, lo_ready.head_start)
                dve.sem_inc(x1_ready.sem, x1_ready.head_start)
                dve.wait_ge(consts, 16)

                def chunk(n, j, half):
                    dve.wait_ge(x0_in[j].sem, x0_in[j].at(half))
                    dve.wait_ge(x1_out[j].sem, x1_out[j].at(half - 1))
                    for t in range(TPC + 1):
                        if t < TPC:
                            dve.wait_ge(hi_ready.sem, hi_ready.at(n * TPC + t))
                            dve.tensor_tensor(cT[t % 2][1][:], turned[:, t % 2], cT[t % 2][0][:].bitcast(F32), ALU.subtract)\
                               .then_inc(lo_ready.sem, 1)
                            dve.tensor_tensor(x0[:, j, t, :], x0[:, j, t, :], bo[:], ALU.add)
                        if t >= 1:
                            u = t - 1
                            dve.drain()
                            dve.wait_ge(out_done.sem, out_done.at(n * TPC + u))
                            dve.tensor_tensor(x1[:, j, u, :], out[:, u, :], x0[:, j, u, :], ALU.add).then_inc(x1_ready.sem, 1)
                sweep(dve, n_chunks, chunk)


def ffn(nc, ident, tag, w, index, x_src, x_dst, first, n_chunks, dim, dff, total=None, ortho=None):
    KT = dim // P
    FT = dff // P
    x_v = x_src.rearrange("(n t p) c -> n p t c", p=P, t=TPC)
    y_v = x_dst.rearrange("(n t p) c -> n p t c", p=P, t=TPC)
    eps = 1e-5 if first else 1e-12
    with Kit(nc) as k:
        w1 = [k.sb(f"{tag}_w1{h}", [P, KT, dff], F32R) for h in ("hi", "lo")]
        w2 = [k.sb(f"{tag}_w2{h}", [P, FT, dim], F32R) for h in ("hi", "lo")]
        fp = 2048 // dim
        split_weights(nc, tag, [(lambda e, c=c: w["w1"](e)[c * P:(c + 1) * P, :], w1[0][:, c, :], w1[1][:, c, :], dff) for c in range(KT)]
                      + [(lambda e, c=c: w["w2"](e)[c * fp * P:(c + 1) * fp * P, :].rearrange("(i p) n -> p i n", p=P), w2[0][:, c * fp:(c + 1) * fp, :].rearrange("p c n -> p (c n)"),
                          w2[1][:, c * fp:(c + 1) * fp, :].rearrange("p c n -> p (c n)"), fp * dim) for c in range(FT // fp)], index)
        b1 = k.sb(f"{tag}_b1", [P, FT])
        b2 = k.sb(f"{tag}_b2", [P, dim])
        gain = k.sb(f"{tag}_gain", [P, dim])
        beta = k.sb(f"{tag}_beta", [P, dim])
        x = k.sb(f"{tag}_x", [P, 2, TPC, dim])
        y = k.sb(f"{tag}_y", [P, TPC, dim])
        hn = k.sb(f"{tag}_hn", [P, TPC, dim]) if first else None
        st = k.sb(f"{tag}_st", [P, TPC, 6])
        mv = k.sb(f"{tag}_mv", [P, TPC, 2])
        var = k.sb(f"{tag}_var", [P, TPC])
        sd = k.sb(f"{tag}_sd", [P, TPC])
        xT = [k.sb(f"{tag}_xT{h}", [P, KT, CH], F32R) for h in ("hi", "lo")]
        act_out = k.sb(f"{tag}_act", [P, 2, CH])
        a = [[k.sb(f"{tag}_a{j}{h}", [P, CH], F32R) for h in ("hi", "lo")] for j in range(2)]
        turned = k.ps(f"{tag}_turned", [P, 2, KT, P])
        up = k.ps(f"{tag}_up", [P, 2, CH])
        out = k.ps(f"{tag}_out", [P, TPC, dim])
        consts = k.sem(f"{tag}_consts")
        x_in = [k.count(f"{tag}_x_in{j}", unit=16) for j in range(2)]
        h_ready = k.count(f"{tag}_h_ready")
        var_ready, sd_ready = k.count(f"{tag}_var_ready"), k.count(f"{tag}_sd_ready")
        tile_turned, hi_ready = k.count(f"{tag}_tile_turned"), k.count(f"{tag}_hi_ready")
        lo_ready = k.count(f"{tag}_lo_ready", early=2)
        up_done = k.count(f"{tag}_up_done", early=2)
        act_ready = k.count(f"{tag}_act_ready", early=2)
        split = k.count(f"{tag}_split", early=2)
        down_done = k.count(f"{tag}_down_done", early=2)
        taken = k.count(f"{tag}_taken", early=1)
        y_ready = k.count(f"{tag}_y_ready", early=1)
        y_out = k.count(f"{tag}_y_out", early=1, unit=16)
        y_added = k.count(f"{tag}_y_added", early=1)
        wide = k.sb(f"{tag}_wide", [P, TPC, dim]) if total is not None else None
        wide_set = k.sem(f"{tag}_wide_set")
        gs_sq, gs_root, gs_inv = k.count(f"{tag}_gs_sq"), k.count(f"{tag}_gs_root"), k.count(f"{tag}_gs_inv")
        steps = ortho["R"] // n_chunks if ortho else 1
        spacing = FT // steps
        if ortho:
            assert steps * n_chunks == ortho["R"] and spacing >= 2

        with nc.Block() as block:
            @block.sync
            def _(sp):
                sp.sem_inc(y_out.sem, y_out.head_start)
                e = read_index(sp, index)
                sp.dma_start(b1[:], w["b1"](e).rearrange("(c p) -> p c", p=P)).then_inc(consts, 16)
                for row, name in ((b2, "b2"), (gain, "gain"), (beta, "beta")):
                    sp.dma_start(row[:], w[name](e).partition_broadcast(P)).then_inc(consts, 16)
                sp.dma_start(x[:, 0], x_v[0]).then_inc(x_in[0].sem, 16)

                def chunk(n, j, half):
                    if exists(n + 1 if isinstance(n, int) else n, n_chunks):
                        sp.wait_ge(taken.sem, taken.at(n - 1))
                        sp.dma_start(x[:, 1 - j], x_v[n + 1]).then_inc(x_in[1 - j].sem, 16)
                    sp.wait_ge(y_ready.sem, y_ready.at(n))
                    sp.dma_start(y_v[n], y[:]).then_inc(y_out.sem, 16)
                sweep(sp, n_chunks, chunk, tail=2)
                sp.wait_ge(y_out.sem, y_out.at(n_chunks - 1))

            @block.gpsimd
            def _(pool):
                pool.sem_inc(y_added.sem, y_added.head_start)
                if ortho:
                    gram_schmidt(nc, pool, k, ortho, gs_sq, gs_inv)
                if total is not None:
                    pool.memset(wide[:], 0.0).then_inc(wide_set, 1)
                    pool.wait_ge(wide_set, 1)

                    def chunk(n, j, half):
                        pool.wait_ge(y_ready.sem, y_ready.at(n))
                        pool.wait_ge(y_added.sem, y_added.at(n - 1))
                        pool.tensor_tensor(wide[:], wide[:], y[:], ALU.add).then_inc(y_added.sem, 1)
                    sweep(pool, n_chunks, chunk)
                    pool.wait_ge(y_added.sem, y_added.at(n_chunks - 1))
                    pool.tensor_tensor(wide[:, 0:2], wide[:, 0:2], wide[:, 2:4], ALU.add).then_inc(wide_set, 1)
                    pool.wait_ge(wide_set, 2)
                    pool.tensor_tensor(total, wide[:, 0], wide[:, 1], ALU.add)

            @block.tensor
            def _(pe):
                pe.sem_inc(up_done.sem, up_done.head_start)
                pe.sem_inc(down_done.sem, down_done.head_start)

                def down(n, f):
                    pe.wait_ge(split.sem, split.at(n * FT + f))
                    if f == 0:
                        pe.wait_ge(taken.sem, taken.at(n - 1))
                    for t in range(TPC):
                        last = mm3(pe, out[:, t, :], (a[f % 2][0][:, t * P:(t + 1) * P], a[f % 2][1][:, t * P:(t + 1) * P]),
                                   (w2[0][:, f, :], w2[1][:, f, :]), f == 0, f == FT - 1)
                    last.then_inc(down_done.sem, 1)

                def chunk(n, j, half):
                    if first:
                        pe.wait_ge(h_ready.sem, h_ready.at(n))
                    else:
                        pe.wait_ge(x_in[j].sem, x_in[j].at(half))
                    src = hn[:] if first else x[:, j]
                    for t in range(TPC):
                        pe.wait_ge(lo_ready.sem, lo_ready.at(n * TPC + t - 2))
                        for c in range(KT):
                            last = pe.transpose(turned[:, t % 2, c, :], src[:, t, c * P:(c + 1) * P], ident[:])
                        last.then_inc(tile_turned.sem, 1)
                    pe.wait_ge(lo_ready.sem, lo_ready.at(n * TPC + TPC - 1))
                    for f in range(FT):
                        pe.wait_ge(act_ready.sem, act_ready.at(n * FT + f - 2))
                        for c in range(KT):
                            last = mm3(pe, up[:, f % 2, :], (w1[0][:, c, f * P:(f + 1) * P], w1[1][:, c, f * P:(f + 1) * P]),
                                       (xT[0][:, c, :], xT[1][:, c, :]), c == 0, c == KT - 1)
                        last.then_inc(up_done.sem, 1)
                        if f >= 1:
                            down(n, f - 1)
                    down(n, FT - 1)
                sweep(pe, n_chunks, chunk)

            def ln_at(n):
                return first and exists(n + 1 if isinstance(n, int) else n, n_chunks)

            @block.scalar
            def _(act):
                act.sem_inc(act_ready.sem, act_ready.head_start)
                act.wait_ge(consts, 64)

                def root(i):
                    act.wait_ge(var_ready.sem, var_ready.at(i))
                    act.activation(sd[:], var[:], ACT.Sqrt).then_inc(sd_ready.sem, 1)

                def chunk(n, j, half):
                    for t in range(TPC):
                        act.wait_ge(tile_turned.sem, tile_turned.at(n * TPC + t))
                        act.activation(xT[0][:, :, t * P:(t + 1) * P], turned[:, t % 2], ACT.Copy).then_inc(hi_ready.sem, 1)
                    for f in range(FT):
                        act.wait_ge(up_done.sem, up_done.at(n * FT + f))
                        act.wait_ge(split.sem, split.at(n * FT + f - 2))
                        act.activation(act_out[:, f % 2], up[:, f % 2], ACT.Gelu_apprx_sigmoid if first else ACT.Gelu,
                                       bias=b1[:, f:f + 1]).then_inc(act_ready.sem, 1)
                        if ortho and f % spacing == 0:
                            act.wait_ge(gs_sq.sem, gs_sq.at(n * steps + f // spacing))
                            act.activation(ortho["root"][:], ortho["sq"][:], ACT.Sqrt).then_inc(gs_root.sem, 1)
                        if f == FT // 2 and ln_at(n):
                            root(n + 1)
                    if not first:
                        root(n)
                if first:
                    root(0)
                sweep(act, n_chunks, chunk, tail=2)

            @block.vector
            def _(dve):
                for c in (lo_ready, split, taken, y_ready):
                    dve.sem_inc(c.sem, c.head_start)
                dve.wait_ge(consts, 64)

                def stats(v):
                    layer_stats(dve, st, mv, v)
                    dve.tensor_scalar(var[:], mv[:, :, 1], eps, None, ALU.add).then_inc(var_ready.sem, 1)

                def normalise(i, v, dst, ready):
                    dve.wait_ge(sd_ready.sem, sd_ready.at(i))
                    dve.reciprocal(var[:], sd[:])
                    dve.drain()
                    for t in range(TPC):
                        dve.tensor_scalar(dst[:, t, :], v[:, t, :], mv[:, t, 0:1], var[:, t:t + 1], ALU.subtract, ALU.mult)
                    dve.drain()
                    dve.tensor_tensor(dst[:], dst[:], gain[:].unsqueeze(1).broadcast_to([P, TPC, dim]), ALU.mult)
                    dve.drain()
                    dve.tensor_tensor(dst[:], dst[:], beta[:].unsqueeze(1).broadcast_to([P, TPC, dim]), ALU.add)\
                       .then_inc(ready.sem, 1)

                def chunk(n, j, half):
                    for t in range(TPC):
                        dve.wait_ge(hi_ready.sem, hi_ready.at(n * TPC + t))
                        dve.tensor_tensor(xT[1][:, :, t * P:(t + 1) * P], turned[:, t % 2],
                                          xT[0][:, :, t * P:(t + 1) * P].bitcast(F32), ALU.subtract).then_inc(lo_ready.sem, 1)
                    for f in range(FT):
                        dve.wait_ge(act_ready.sem, act_ready.at(n * FT + f))
                        dve.wait_ge(down_done.sem, down_done.at(n * FT + f - 2))
                        hi, lo = a[f % 2]
                        dve.tensor_copy(hi[:], act_out[:, f % 2])
                        dve.drain()
                        dve.tensor_tensor(lo[:], act_out[:, f % 2], hi[:].bitcast(F32), ALU.subtract).then_inc(split.sem, 1)
                        if ortho and f % spacing == 1:
                            dve.wait_ge(gs_root.sem, gs_root.at(n * steps + f // spacing))
                            dve.tensor_scalar(ortho["inv"][:], ortho["root"][:], 1e-8, None, ALU.add)
                            dve.drain()
                            dve.reciprocal(ortho["inv"][:], ortho["inv"][:]).then_inc(gs_inv.sem, 1)
                        if f == FT // 2 and ln_at(n):
                            dve.wait_ge(x_in[1 - j].sem, x_in[1 - j].at(half + j))
                            stats(x[:, 1 - j])
                        if f == FT // 2 + 1 and ln_at(n):
                            normalise(n + 1, x[:, 1 - j], hn, h_ready)
                    dve.wait_ge(down_done.sem, down_done.at((n + 1) * FT - 1))
                    dve.wait_ge(y_out.sem, y_out.at(n - 1))
                    if total is not None:
                        dve.wait_ge(y_added.sem, y_added.at(n - 1))
                    dve.tensor_tensor(y[:], out[:], b2[:].unsqueeze(1).broadcast_to([P, TPC, dim]), ALU.add)
                    dve.drain()
                    if first:
                        dve.tensor_tensor(y[:], y[:], x[:, j], ALU.add).then_inc(taken.sem, 1)
                        dve.drain().then_inc(y_ready.sem, 1)
                    else:
                        dve.tensor_tensor(y[:], y[:], x[:, j], ALU.add).then_inc(taken.sem, 1)
                        dve.drain()
                        stats(y)
                        normalise(n, y, y, y_ready)
                if first:
                    dve.wait_ge(x_in[0].sem, x_in[0].at(0))
                    stats(x[:, 0])
                    normalise(0, x[:, 0], hn, h_ready)
                else:
                    dve.wait_ge(x_in[0].sem, x_in[0].at(0))
                sweep(dve, n_chunks, chunk, tail=2)


def gram_schmidt(nc, pool, k, o, sq_ready, inv_ready):
    X, R, KT = o["X"], o["R"], o["KT"]
    later = k.sb("gs_later", [P, R, R])
    col = k.sb("gs_col", [P, 2, KT])
    prod = k.sb("gs_prod", [P, 2, R, KT])
    sums = k.sb("gs_sums", [P, 2, R])
    dots = k.sb("gs_dots", [P, 2, R])
    coef = k.sb("gs_coef", [P, 2, R])
    scale = k.sb("gs_scale", [P, 2, R])
    loaded = k.sem("gs_loaded")
    done = k.sem("gs_done")
    for m in range(2):
        for c in range(KT):
            pool.dma_start(o["raw"][:, m, c, :], o["src"][m][c * P:(c + 1) * P, :]).then_inc(loaded, 16)
    pool.dma_start(later[:], o["later_src"].rearrange("i j -> (i j)").partition_broadcast(P)).then_inc(loaded, 16)
    pool.wait_ge(loaded, 16 * (2 * KT + 1))
    pool.tensor_copy(X[:], o["raw"][:].rearrange("p m c j -> p m j c")).then_inc(done, 1)
    ops = 9

    def along(v):
        return v.unsqueeze(3).broadcast_to([P, 2, R, KT])

    with pool.Fori(0, R) as i:
        def after(c):
            pool.wait_ge(done, i * ops + c + 1)
            pool.sem_inc(o["passed"], 1)
        after(0)
        pool.tensor_copy(col[:], X[:, :, i, :]).then_inc(done, 1)
        after(1)
        pool.tensor_tensor(prod[:], X[:], col[:].unsqueeze(2).broadcast_to([P, 2, R, KT]), ALU.mult).then_inc(done, 1)
        after(2)
        pool.tensor_tensor(prod[:, :, :, 0:2], prod[:, :, :, 0:2], prod[:, :, :, 2:4], ALU.add).then_inc(done, 1)
        after(3)
        pool.tensor_tensor(sums[:], prod[:, :, :, 0], prod[:, :, :, 1], ALU.add).then_inc(done, 1)
        after(4)
        pool.partition_all_reduce(dots[:].rearrange("p m j -> p (m j)"), sums[:].rearrange("p m j -> p (m j)"), P, RADD).then_inc(done, 1)
        after(5)
        pool.tensor_copy(o["sq"][:], dots[:, :, i]).then_inc(sq_ready.sem, 1)
        pool.tensor_tensor(coef[:], dots[:], later[:, i, :].unsqueeze(1).broadcast_to([P, 2, R]), ALU.mult).then_inc(done, 1)
        pool.wait_ge(inv_ready.sem, inv_ready.at(i))
        pool.sem_inc(o["passed"], 1)
        after(6)
        pool.tensor_copy(scale[:, :, i], o["inv"][:])
        pool.tensor_tensor(coef[:], coef[:], o["inv"][:].unsqueeze(2).broadcast_to([P, 2, R]), ALU.mult).then_inc(done, 1)
        after(7)
        pool.tensor_tensor(coef[:], coef[:], o["inv"][:].unsqueeze(2).broadcast_to([P, 2, R]), ALU.mult).then_inc(done, 1)
        after(8)
        pool.tensor_tensor(prod[:], along(coef[:]), col[:].unsqueeze(2).broadcast_to([P, 2, R, KT]), ALU.mult)
        pool.drain()
        pool.tensor_tensor(X[:], X[:], prod[:], ALU.subtract).then_inc(done, 1)
    pool.wait_ge(done, R * ops + 1)
    pool.tensor_tensor(X[:], X[:], along(scale[:]), ALU.mult)


def finish(nc, d, s, ident, totals, ortho, experts, out, batches, seq, dim):
    KT = dim // P
    R = ortho["R"]
    X = ortho["X"]
    NCB = seq // CH
    x_v = s["x3"].rearrange("(n t p) c -> n p t c", p=P, t=TPC)
    y_v = out.rearrange("b (n t p) c -> (b n) p t c", p=P, t=TPC)
    NDOM = d["L3_cond_expert_W"].shape[0]
    with Kit(nc) as k:
        maps = k.sb("maps", [P, KT, R])
        resp_wT = k.sb("resp_wT", [R, dim])
        resp_row = k.sb("resp_row", [P, dim])
        strength = k.sb("strength", [P, batches])
        downT = k.sb("downT", [P, KT, P])
        upT = k.sb("upT", [P, dim])
        expertT = k.sb("expertT", [P, batches, P])
        down_b = k.sb("down_b", [P, 1])
        expert_b = k.sb("expert_b", [P, batches])
        up_b = k.sb("up_b", [P, dim])
        gain = k.sb("gain3", [P, dim])
        beta = k.sb("beta3", [P, dim])
        with Kit(nc) as q:
            ones = q.sb("ones_f", [P, P])
            bias2 = q.sb("bias2", [P, dim])
            gw1 = q.sb("gw1", [P, dim])
            gw1T = q.sb("gw1T", [P, KT, P])
            gb1 = q.sb("gb1", [P, 1])
            gw2 = q.sb("gw2", [P, 1])
            gw2_wide = q.sb("gw2_wide", [P, P])
            gb2 = q.sb("gb2", [P, 1])
            safety = q.sb("safety", [P, batches])
            domain = q.sb("domain", [P, batches], I32)
            dom = q.sb("dom", [P, batches])
            valid = q.sb("valid", [P, 2, batches])
            resp_w = q.sb("resp_w_in", [P, KT, R])
            down_w = q.sb("down_w", [P, dim])
            up_w = q.sb("up_w", [P, KT, P])
            exp_w = q.sb("exp_w", [P, batches, P])
            exp_b = q.sb("exp_b", [P, batches, 2])
            pooled = q.sb("pooled", [P, KT, batches])
            h1 = q.sb("h1", [P, batches])
            gate = q.sb("gate", [P, 2, batches])
            uT = q.sb("uT", [R, 2, dim])
            b32T = q.sb("b32T", [P, KT, R])
            mid = q.sb("mid", [R, R])
            ps = q.ps("ps_setup", [P, 8, 512])
            loaded = q.sem("f_loaded")
            pe_done, dve_done, act_done = q.sem("f_pe"), q.sem("f_dve"), q.sem("f_act")
            plain = [
                (bias2[:], d["L2_cond_safety_bias"].partition_broadcast(P)),
                (resp_row[:], d["L2_cond_resp_b"].partition_broadcast(P)),
                (gw1[:], d["L2_cond_gate_w1"]),
                (gb1[:], d["L2_cond_gate_b1"].rearrange("(p o) -> p o", o=1)),
                (gw2[:], d["L2_cond_gate_w2"].rearrange("o p -> p o")),
                (gb2[:], d["L2_cond_gate_b2"].partition_broadcast(P)),
                (safety[:], d["condB_safetyscore"].partition_broadcast(P)),
                (domain[:], d["itok_B_0_15"].partition_broadcast(P)),
                (resp_w[:], d["L2_cond_resp_w"].rearrange("(c p) r -> p c r", p=P)),
                (down_w[:], d["L3_cond_down_W"]),
                (up_w[:], d["L3_cond_up_W"].rearrange("(c p) a -> p c a", p=P)),
                (down_b[:], d["L3_cond_down_b"].rearrange("(p o) -> p o", o=1)),
                (up_b[:], d["L3_cond_up_b"].partition_broadcast(P)),
                (gain[:], d["L3_cond_ln_gamma"].partition_broadcast(P)),
                (beta[:], d["L3_cond_ln_beta"].partition_broadcast(P)),
            ]
            n_loads = len(plain) + 3 * batches
            with nc.Block() as block:
                @block.sync
                def _(sp):
                    for dst, src in plain:
                        sp.dma_start(dst, src).then_inc(loaded, 16)
                    for b in range(batches):
                        e = read_index(sp, (experts[b], NDOM))
                        sp.dma_start(exp_w[:, b, :], d["L3_cond_expert_W"][e]).then_inc(loaded, 16)
                        sp.dma_start(exp_b[:, b, 0:1], d["L3_cond_expert_b"][e].rearrange("(p o) -> p o", o=1)).then_inc(loaded, 16)
                        sp.dma_start(exp_b[:, b, 1:2], d["L3_cond_domain_emb"][e].rearrange("(p o) -> p o", o=1)).then_inc(loaded, 16)

                @block.tensor
                def _(pe):
                    pe.wait_ge(loaded, 16 * n_loads)
                    for c in range(KT):
                        pe.transpose(ps[:, 0, c * P:(c + 1) * P], gw1[:, c * P:(c + 1) * P], ident[:])
                        pe.transpose(ps[:, 1, c * P:(c + 1) * P], down_w[:, c * P:(c + 1) * P], ident[:])
                        pe.transpose(ps[:, 2, c * P:(c + 1) * P], up_w[:, c, :], ident[:])
                        pe.transpose(ps[0:R, 3, c * P:(c + 1) * P], resp_w[:, c, :], ident[:])
                        for m in range(2):
                            pe.transpose(ps[0:R, 4 + m, c * P:(c + 1) * P], X[:, m, :, c], ident[:])
                    for b in range(batches):
                        pe.transpose(ps[:, 6, b * P:(b + 1) * P], exp_w[:, b, :], ident[:])
                    pe.wait_ge(dve_done, 1)
                    for b in range(batches):
                        for c in range(KT):
                            last = pe.matmul(ps[:, 7, c * batches + b:c * batches + b + 1], totals[b][:, c * P:(c + 1) * P],
                                             ones[:, 0:1], start=True, stop=True)
                    last.then_inc(pe_done, 1)
                    pe.wait_ge(dve_done, 2)
                    for c in range(KT):
                        pe.matmul(ps[:, 0, c * R:(c + 1) * R], uT[:, 1, c * P:(c + 1) * P], uT[:, 0, 0:R], start=True, stop=True)
                    for c in range(KT):
                        last = pe.matmul(ps[:, 1, 0:batches], gw1T[:, c, :], pooled[:, c, :], start=(c == 0), stop=(c == KT - 1))
                    last.then_inc(pe_done, 1)
                    pe.wait_ge(dve_done, 3)
                    for c in range(KT):
                        pe.matmul(ps[0:R, 2, 0:R], X[:, 1, :, c], b32T[:, c, :], start=(c == 0), stop=(c == KT - 1))
                    pe.matmul(ps[:, 3, 0:batches], gw2_wide[:], h1[:], start=True, stop=True).then_inc(pe_done, 1)
                    pe.wait_ge(dve_done, 4)
                    for c in range(KT):
                        last = pe.matmul(ps[:, 4, c * R:(c + 1) * R], uT[:, 0, c * P:(c + 1) * P], mid[:], start=True, stop=True)
                    last.then_inc(pe_done, 1)

                @block.scalar
                def _(act):
                    act.wait_ge(pe_done, 3)
                    act.activation(gate[:, 0, :], ps[:, 3, 0:batches], ACT.Sigmoid, bias=gb2[:])
                    act.activation(gate[:, 1, :], safety[:], ACT.Sigmoid).then_inc(act_done, 1)

                @block.vector
                def _(dve):
                    dve.memset(ones[:], 1.0).then_inc(dve_done, 1)
                    dve.wait_ge(loaded, 16 * n_loads)
                    dve.tensor_tensor(resp_row[:], resp_row[:], bias2[:], ALU.add)
                    dve.tensor_copy(dom[:], domain[:])
                    dve.drain()
                    dve.tensor_scalar(valid[:, 0], dom[:], 0.0, None, ALU.is_ge)
                    dve.tensor_scalar(valid[:, 1], dom[:], float(NDOM), None, ALU.is_lt)
                    dve.tensor_scalar(gw2_wide[:], ones[:], gw2[:], None, ALU.mult)
                    dve.drain()
                    dve.tensor_tensor(valid[:, 0], valid[:, 0], valid[:, 1], ALU.mult)
                    dve.drain()
                    dve.tensor_scalar(valid[:, 1], valid[:, 0], -1.0, 1.0, ALU.mult, ALU.add)
                    dve.drain()
                    for b in range(batches):
                        dve.scalar_tensor_tensor(out=expert_b[:, b:b + 1], in0=exp_b[:, b, 0:1], scalar=valid[:, 0, b:b + 1],
                                                 in1=exp_b[:, b, 1:2], op0=ALU.mult, op1=ALU.add)
                        dve.tensor_scalar(expertT[:, b, :], ident[:], valid[:, 1, b:b + 1], None, ALU.mult)
                    dve.wait_ge(pe_done, 1)
                    dve.drain()
                    for b in range(batches):
                        dve.scalar_tensor_tensor(out=expertT[:, b, :], in0=ps[:, 6, b * P:(b + 1) * P], scalar=valid[:, 0, b:b + 1],
                                                 in1=expertT[:, b, :], op0=ALU.mult, op1=ALU.add)
                    dve.tensor_copy(gw1T[:].rearrange("p c a -> p (c a)"), ps[:, 0, :])
                    dve.tensor_copy(downT[:].rearrange("p c a -> p (c a)"), ps[:, 1, :])
                    dve.tensor_copy(upT[:], ps[:, 2, :])
                    dve.tensor_copy(resp_wT[:], ps[0:R, 3, :])
                    for m in range(2):
                        dve.tensor_copy(uT[:, m, :], ps[0:R, 4 + m, :])
                    dve.tensor_scalar(pooled[:].rearrange("p c b -> p (c b)"), ps[:, 7, 0:KT * batches], 1.0 / seq, None, ALU.mult)
                    dve.drain().then_inc(dve_done, 1)
                    dve.wait_ge(pe_done, 2)
                    dve.tensor_copy(b32T[:].rearrange("p c r -> p (c r)"), ps[:, 0, 0:KT * R])
                    dve.tensor_scalar(h1[:], ps[:, 1, 0:batches], gb1[:], 0.0, ALU.add, ALU.max)
                    dve.drain().then_inc(dve_done, 1)
                    dve.wait_ge(pe_done, 3)
                    dve.tensor_copy(mid[:], ps[0:R, 2, 0:R]).then_inc(dve_done, 1)
                    dve.wait_ge(pe_done, 4)
                    dve.tensor_copy(maps[:].rearrange("p c r -> p (c r)"), ps[:, 4, 0:KT * R])
                    dve.wait_ge(act_done, 1)
                    dve.tensor_tensor(strength[:], gate[:, 0, :], gate[:, 1, :], ALU.mult)

        x = k.sb("x_f", [P, 2, TPC, dim])
        x4 = k.sb("x4", [P, TPC, dim])
        resp = k.sb("resp", [P, 2, dim])
        y = k.sb("y_f", [P, 2, TPC, dim])
        xT = k.sb("xT_f", [P, KT, CH])
        x4T = k.sb("x4T", [P, KT, CH])
        feats = k.sb("feats", [R, CH])
        hid = k.sb("hid", [P, CH])
        exo = k.sb("exo", [P, CH])
        st = k.sb("st_f", [P, TPC, 6])
        mv = k.sb("mv_f", [P, TPC, 2])
        var = k.sb("var_f", [P, TPC])
        sd = k.sb("sd_f", [P, TPC])
        turned = k.ps("turned_f", [P, 2, KT, P])
        ps_feat = k.ps("ps_feat", [P, CH])
        ps_hid = k.ps("ps_hid", [P, CH])
        ps_exp = k.ps("ps_exp", [P, CH])
        wide = k.ps("wide_f", [P, 2, dim])
        x_in = [k.count(f"f_x_in{j}", unit=16) for j in range(2)]
        tile_turned = k.count("f_tile_turned")
        turned_out = k.count("f_turned_out", early=2)
        feat_done, feat_ready = k.count("f_feat_done"), k.count("f_feat_ready")
        wide_done = k.count("f_wide_done")
        wide_out = k.count("f_wide_out", early=2)
        x4_ready = k.count("f_x4_ready")
        hid_done, hid_ready = k.count("f_hid_done"), k.count("f_hid_ready")
        exp_done, exp_ready = k.count("f_exp_done"), k.count("f_exp_ready")
        var_ready, sd_ready = k.count("f_var_ready"), k.count("f_sd_ready")
        scaled = k.count("f_scaled", early=2)
        y_ready = k.count("f_y_ready")
        y_out = [k.count(f"f_y_out{j}", early=1, unit=16) for j in range(2)]
        half_done = k.count("f_half_done")
        passed = k.sem("passed_f")
        n_chunks = batches * NCB

        with nc.Block() as block:
            @block.sync
            def _(sp):
                for c in y_out:
                    sp.sem_inc(c.sem, c.head_start)
                sp.dma_start(x[:, 0], x_v[0]).then_inc(x_in[0].sem, 16)

                def chunk(n, j, half):
                    if exists(n + 1 if isinstance(n, int) else n, n_chunks):
                        sp.wait_ge(scaled.sem, scaled.at(n - 1))
                        sp.dma_start(x[:, 1 - j], x_v[n + 1]).then_inc(x_in[1 - j].sem, 16)
                    sp.wait_ge(y_ready.sem, y_ready.at(n))
                    sp.dma_start(y_v[n], y[:, j]).then_inc(y_out[j].sem, 16)
                sweep(sp, n_chunks, chunk, tail=2)
                for j in range(2):
                    sp.wait_ge(y_out[j].sem, y_out[j].at(n_chunks // 2 - 1))

            @block.gpsimd
            def _(pool):
                def chunk(n, j, half):
                    pool.wait_ge(scaled.sem, scaled.at(n))
                    pool.sem_inc(passed, 1)
                    pool.tensor_tensor(y[:, j], y[:, j], gain[:].unsqueeze(1).broadcast_to([P, TPC, dim]), ALU.mult)\
                        .then_inc(half_done.sem, 1)
                    pool.wait_ge(half_done.sem, half_done.at(n))
                    pool.sem_inc(passed, 1)
                    pool.tensor_tensor(y[:, j], y[:, j], beta[:].unsqueeze(1).broadcast_to([P, TPC, dim]), ALU.add)\
                        .then_inc(y_ready.sem, 1)
                sweep(pool, n_chunks, chunk)

            @block.tensor
            def _(pe):
                def turn(src, first_event, t):
                    pe.wait_ge(turned_out.sem, turned_out.at(first_event + t - 2))
                    for c in range(KT):
                        last = pe.transpose(turned[:, t % 2, c, :], src[:, t, c * P:(c + 1) * P], ident[:])
                    last.then_inc(tile_turned.sem, 1)

                for b in range(batches):
                    with pe.Fori(0, NCB // 2) as i:
                        for j in range(2):
                            n = i * 2 + j + b * NCB
                            pe.wait_ge(x_in[j].sem, x_in[j].at(i + b * NCB // 2))
                            for t in range(TPC):
                                turn(x[:, j], n * 8, t)
                            pe.wait_ge(turned_out.sem, turned_out.at(n * 8 + 3))
                            for c in range(KT):
                                last = pe.matmul(ps_feat[0:R, :], maps[:, c, :], xT[:, c, :], start=(c == 0), stop=(c == KT - 1))
                            last.then_inc(feat_done.sem, 1)
                            pe.wait_ge(feat_ready.sem, feat_ready.at(n))
                            for t in range(TPC):
                                pe.wait_ge(wide_out.sem, wide_out.at(n * 8 + t - 2))
                                pe.matmul(wide[:, t % 2, :], feats[:, t * P:(t + 1) * P], resp_wT[:], start=True, stop=True)\
                                  .then_inc(wide_done.sem, 1)
                            for t in range(TPC):
                                pe.wait_ge(x4_ready.sem, x4_ready.at(n * TPC + t))
                                turn(x4, n * 8 + 4, t)
                            pe.wait_ge(turned_out.sem, turned_out.at(n * 8 + 7))
                            for c in range(KT):
                                last = pe.matmul(ps_hid[:], downT[:, c, :], x4T[:, c, :], start=(c == 0), stop=(c == KT - 1))
                            last.then_inc(hid_done.sem, 1)
                            pe.wait_ge(hid_ready.sem, hid_ready.at(n))
                            pe.matmul(ps_exp[:], expertT[:, b, :], hid[:], start=True, stop=True).then_inc(exp_done.sem, 1)
                            pe.wait_ge(exp_ready.sem, exp_ready.at(n))
                            for t in range(TPC):
                                pe.wait_ge(wide_out.sem, wide_out.at(n * 8 + 4 + t - 2))
                                pe.matmul(wide[:, t % 2, :], exo[:, t * P:(t + 1) * P], upT[:], start=True, stop=True)\
                                  .then_inc(wide_done.sem, 1)

            @block.scalar
            def _(act):
                act.sem_inc(turned_out.sem, turned_out.head_start)
                for b in range(batches):
                    with act.Fori(0, NCB // 2) as i:
                        for j in range(2):
                            n = i * 2 + j + b * NCB
                            for dst, e in ((xT, 0), (x4T, 4)):
                                for t in range(TPC):
                                    act.wait_ge(tile_turned.sem, tile_turned.at(n * 8 + e + t))
                                    act.activation(dst[:, :, t * P:(t + 1) * P], turned[:, t % 2], ACT.Copy).then_inc(turned_out.sem, 1)
                            act.wait_ge(hid_done.sem, hid_done.at(n))
                            act.activation(hid[:], ps_hid[:], ACT.Gelu, bias=down_b[:]).then_inc(hid_ready.sem, 1)
                            act.wait_ge(exp_done.sem, exp_done.at(n))
                            act.activation(exo[:], ps_exp[:], ACT.Identity, bias=expert_b[:, b:b + 1]).then_inc(exp_ready.sem, 1)
                            act.wait_ge(var_ready.sem, var_ready.at(n))
                            act.activation(sd[:], var[:], ACT.Sqrt).then_inc(sd_ready.sem, 1)

            @block.vector
            def _(dve):
                dve.sem_inc(wide_out.sem, wide_out.head_start)
                dve.sem_inc(scaled.sem, scaled.head_start)
                for b in range(batches):
                    with dve.Fori(0, NCB // 2) as i:
                        for j in range(2):
                            n = i * 2 + j + b * NCB
                            half = i + b * NCB // 2
                            dve.wait_ge(x_in[j].sem, x_in[j].at(half))
                            dve.wait_ge(feat_done.sem, feat_done.at(n))
                            dve.tensor_copy(feats[:], ps_feat[0:R, :]).then_inc(feat_ready.sem, 1)
                            for t in range(TPC):
                                dve.wait_ge(wide_done.sem, wide_done.at(n * 8 + t))
                                dve.tensor_tensor(resp[:, t % 2], wide[:, t % 2], resp_row[:], ALU.add).then_inc(wide_out.sem, 1)
                                dve.drain()
                                dve.scalar_tensor_tensor(out=x4[:, t, :], in0=resp[:, t % 2], scalar=strength[:, b:b + 1],
                                                         in1=x[:, j, t, :], op0=ALU.mult, op1=ALU.add).then_inc(x4_ready.sem, 1)
                            dve.wait_ge(y_out[j].sem, y_out[j].at(half - 1))
                            for t in range(TPC):
                                if t >= 2:
                                    dve.drain()
                                dve.wait_ge(wide_done.sem, wide_done.at(n * 8 + 4 + t))
                                dve.tensor_tensor(resp[:, t % 2], wide[:, t % 2], up_b[:], ALU.add).then_inc(wide_out.sem, 1)
                                dve.drain()
                                dve.tensor_tensor(y[:, j, t, :], resp[:, t % 2], x4[:, t, :], ALU.add)
                            dve.drain()
                            layer_stats(dve, st, mv, y[:, j])
                            dve.tensor_scalar(var[:], mv[:, :, 1], 1e-5, None, ALU.add).then_inc(var_ready.sem, 1)
                            dve.wait_ge(sd_ready.sem, sd_ready.at(n))
                            dve.reciprocal(var[:], sd[:])
                            dve.drain()
                            for t in range(TPC):
                                last = dve.tensor_scalar(y[:, j, t, :], y[:, j, t, :], mv[:, t, 0:1], var[:, t:t + 1],
                                                         ALU.subtract, ALU.mult)
                            last.then_inc(scaled.sem, 1)


def program(nc, d, out):
    batches, seq, dim = d["x"].shape
    heads = d["fside_Bx16xSxS_0"].shape[1]
    dff = d["L0_cond_W1"].shape[1]
    R = d["L2_cond_U"].shape[1]
    rows = batches * seq
    n_chunks = rows // CH
    E = d["L1_cond_Wi"].shape[0]

    def scratch(name, shape, dtype=F32):
        return nc.dram_tensor(f"scratch_{name}", shape, dtype, kind="Internal").ap()

    s = {
        "x0": scratch("x0", (rows, dim)),
        "q": scratch("q", (batches, dim // P, 2, P, seq)),
        "k": scratch("k", (batches, dim // P, 2, P, seq)),
        "v": scratch("v", (rows, dim)),
        "ctx": scratch("ctx", (rows // P * (dim // P), P, P)),
        "x1": scratch("x1", (rows, dim)),
        "x2": scratch("x2", (rows, dim)),
        "x3": scratch("x3", (rows, dim)),
    }
    with Kit(nc) as k:
        ident = k.sb("ident", [P, P])
        index = k.sb("index", [1, 2, batches], I32)
        start = k.sem("start")
        with nc.Block() as block:
            @block.sync
            def _(sp):
                sp.dma_start(ident[:], d["ident"]).then_inc(start, 16)
                sp.dma_start(index[:, 0, :], d["itok_B_0_7"].rearrange("(o b) -> o b", o=1)).then_inc(start, 16)
                sp.dma_start(index[:, 1, :], d["itok_B_0_15"].rearrange("(o b) -> o b", o=1)).then_inc(start, 16)
                sp.wait_ge(start, 48)
        with Kit(nc) as m:
            scale1 = m.sb("scale1", [P, batches, dim])
            shift = m.sb("shift", [P, batches, dim])
            prepare(nc, d, scale1, shift, batches, dim)
            project(nc, d, s, ident, scale1, shift, batches, seq, dim, heads)
        attend(nc, d, s, ident, batches, seq, dim, heads)
        out_proj(nc, d, s, ident, batches, seq, dim, heads)
        KT = dim // P
        ortho = {"X": k.sb("gs_X", [P, 2, R, KT]), "raw": k.sb("gs_raw", [P, 2, KT, R]), "R": R, "KT": KT,
                 "src": (d["L2_cond_U"], d["L2_cond_V"]), "later_src": d["later"], "root": k.sb("gs_root_t", [P, 2]),
                 "sq": k.sb("gs_sq_t", [P, 2]), "inv": k.sb("gs_inv_t", [P, 2]), "passed": k.sem("gs_passed")}
        totals = [k.sb(f"total{b}", [P, dim]) for b in range(batches)]
        w = {"w1": lambda e: d["L0_cond_W1"], "w2": lambda e: d["L0_cond_W2"], "b1": lambda e: d["L0_cond_b1"],
             "b2": lambda e: d["L0_cond_b2"], "gain": lambda e: d["L0_cond_g2"], "beta": lambda e: d["L0_cond_beta2"]}
        ffn(nc, ident, "fa", w, None, s["x1"], s["x2"], True, n_chunks, dim, dff, ortho=ortho)
        w = {"w1": lambda e: d["L1_cond_Wi"][e], "w2": lambda e: d["L1_cond_Wo"][e], "b1": lambda e: d["L1_cond_bi"][e],
             "b2": lambda e: d["L1_cond_bo"][e], "gain": lambda e: d["L1_cond_gamma"][e], "beta": lambda e: d["L1_cond_beta"][e]}
        for b in range(batches):
            part = slice(b * seq, (b + 1) * seq)
            ffn(nc, ident, f"fb{b}", w, (index[0:1, 0, b:b + 1], E), s["x2"][part], s["x3"][part], False, seq // CH, dim, dff,
                total=totals[b][:])
        finish(nc, d, s, ident, totals, ortho, [index[0:1, 1, b:b + 1] for b in range(batches)], out, batches, seq, dim)


def kernel(**inputs):
    import concourse.bacc as _bacc
    from concourse.bass_utils import run_bass_kernel_spmd as _run

    nc = _bacc.Bacc("TRN2", target_bir_lowering=False, num_devices=1)
    arrays = {name: np.ascontiguousarray(a) for name, a in inputs.items()}
    dim = arrays["x"].shape[-1]
    R = arrays["L2_cond_U"].shape[1]
    half = dim // 2
    freqs = np.exp(np.arange(half, dtype=np.float32) * np.float32(-np.log(10000.0) / (half - 1))).astype(np.float32)
    arrays["freqs"] = np.ascontiguousarray(freqs.reshape(half // P, P).T)
    arrays["ident"] = np.eye(P, dtype=np.float32)
    arrays["later"] = np.triu(np.ones((R, R), np.float32), 1)
    d = {name: nc.dram_tensor(f"in_{name}", a.shape, mybir.dt.from_np(a.dtype), kind="ExternalInput").ap()
         for name, a in arrays.items()}
    shape = arrays["x"].shape
    out = nc.dram_tensor("out_0", shape, F32, kind="ExternalOutput").ap()
    with nc.allow_non_contiguous_dma(reason="bias columns of a few KB"):
        program(nc, d, out)
    r = _run(nc, [{f"in_{name}": a for name, a in arrays.items()}], core_ids=[0])
    return r.results[0]["out_0"]
```

```python
from contextlib import ExitStack

import numpy as np
import concourse.bass as bass
from concourse import mybir

ALU = mybir.AluOpType
ACT = mybir.ActivationFunctionType
F32 = mybir.dt.float32
F32R = mybir.dt.float32r
BF16 = mybir.dt.bfloat16
U8 = mybir.dt.uint8
I32 = mybir.dt.int32
RADD = bass.bass_isa.ReduceOp.add

P = 128
CH = 512
TPC = CH // P
NEG = -1.0e30
LOW = -3.0e38
TWO_PI = (6.28125, 1.9350051879882812e-3, 3.0197990e-7)
MAGIC = 12582912.0


class Count:

    def __init__(self, sem, early=0, unit=1):
        self.sem, self.early, self.unit = sem, early, unit
        self.head_start = early * unit

    def at(self, k):
        return (k + 1 + self.early) * self.unit


def sweep(eng, count, emit, head=0, tail=0, extra=0):
    for n in range(min(head, count)):
        emit(n, n % 2, n // 2)
    if count - tail > head:
        with eng.Fori(head // 2, (count - tail) // 2) as half:
            for j in range(2):
                emit(half * 2 + j, j, half)
    for n in range(max(head, count - tail), count + extra):
        emit(n, n % 2, n // 2)


def sweep_batches(eng, batches, pairs, emit):
    assert batches * pairs >= 2
    for b in range(batches):
        low, high = b * pairs, (b + 1) * pairs
        if b == 0:
            for j in range(2):
                emit(b, j, j, 0)
            low += 1
        if b == batches - 1:
            high -= 1
        if high > low:
            with eng.Fori(low, high) as half:
                for j in range(2):
                    emit(b, half * 2 + j, j, half)
        if b == batches - 1:
            for j in range(2):
                emit(b, high * 2 + j, j, high)


def exists(n, count):
    return not isinstance(n, int) or 0 <= n < count


class Kit:

    def __init__(self, nc):
        self.nc, self.ctx, self.sems = nc, ExitStack(), []

    def sb(self, name, shape, dtype=F32):
        return self.ctx.enter_context(self.nc.sbuf_tensor(name, shape, dtype))

    def ps(self, name, shape, dtype=F32):
        return self.ctx.enter_context(self.nc.psum_tensor(name, shape, dtype))

    def sem(self, name):
        self.sems.append(self.nc.alloc_semaphore(name=name))
        return self.sems[-1]

    def count(self, name, early=0, unit=1):
        return Count(self.sem(name), early, unit)

    def __enter__(self):
        self.ctx.__enter__()
        return self

    def __exit__(self, *e):
        if e[0] is None and self.sems:
            self.nc.clear_and_free_semaphores(self.sems)
            self.nc.all_engine_barrier()
        return self.ctx.__exit__(*e)


def mm3(pe, out, a, b, start, stop):
    pe.matmul(out, a[0], b[0], start=start, stop=False)
    pe.matmul(out, a[0], b[1], start=False, stop=False)
    return pe.matmul(out, a[1], b[0], start=False, stop=stop)


def read_index(eng, index):
    return None if index is None else eng.value_load(index[0], min_val=0, max_val=index[1] - 1)


def split_weights(nc, tag, parts, index=None):
    with Kit(nc) as k:
        raw = k.sb(f"{tag}_raw", [P, 2, 2048])
        loaded = [k.count(f"{tag}_loaded{j}", unit=16) for j in range(2)]
        hi_done = k.count(f"{tag}_hi")
        lo_done = k.count(f"{tag}_lo")
        with nc.Block() as block:
            @block.sync
            def _(sp):
                e = read_index(sp, index)
                for n, (src, hi, lo, cols) in enumerate(parts):
                    if n >= 2:
                        sp.wait_ge(lo_done.sem, lo_done.at(n - 2))
                    view = src(e)
                    dst = raw[:, n % 2, 0:cols]
                    if len(view.shape) == 3:
                        dst = dst.rearrange("p (c n) -> p c n", n=view.shape[2])
                    sp.dma_start(dst, view).then_inc(loaded[n % 2].sem, 16)

            @block.scalar
            def _(act):
                for n, (src, hi, lo, cols) in enumerate(parts):
                    act.wait_ge(loaded[n % 2].sem, loaded[n % 2].at(n // 2))
                    act.activation(hi, raw[:, n % 2, 0:cols], ACT.Copy).then_inc(hi_done.sem, 1)

            @block.vector
            def _(dve):
                for n, (src, hi, lo, cols) in enumerate(parts):
                    dve.wait_ge(hi_done.sem, hi_done.at(n))
                    dve.tensor_tensor(lo, raw[:, n % 2, 0:cols], hi.bitcast(F32), ALU.subtract)\
                       .then_inc(lo_done.sem, 1)


def layer_stats(dve, st, mv, x):
    for t in range(TPC):
        dve.bn_stats(st[:, t, :], x[:, t, :])
    dve.drain()
    for t in range(TPC):
        dve.bn_aggr(mv[:, t, :], st[:, t, :])
    dve.drain()


def prepare(nc, d, scale1, shift, batches, dim):
    KT = dim // P
    with Kit(nc) as k:
        t_raw = k.sb("t_raw", [P, batches], I32)
        freqs = k.sb("freqs", [P, 2])
        w_ada = k.sb("w_ada", [P, KT, 2 * dim])
        b_ada = k.sb("b_ada", [P, 2 * dim])
        t = k.sb("t_f", [P, batches])
        q = k.sb("q", [P, batches])
        qh = k.sb("qh", [P, batches], F32R)
        ql = k.sb("ql", [P, batches])
        r = k.sb("r", [P, batches])
        x = k.sb("x_ang", [P, batches])
        e = k.sb("e", [P, batches, 2])
        turns = k.sb("turns", [P, batches, 2])
        ang = k.sb("ang", [P, batches, KT])
        sc = k.sb("sc_tab", [P, batches, KT])
        sg = k.sb("sg", [P, batches, KT])
        feat = k.sb("feat", [P, batches, KT])
        ones = k.sb("ones_p", [P, P])
        spread = k.sb("spread", [P, batches, KT, P])
        rows = k.ps("rows", [P, batches, 2, dim])
        loaded = k.sem("p_loaded")
        ang_ready, sin_ready, sig_ready = k.sem("ang_ready"), k.sem("sin_ready"), k.sem("sig_ready")
        spread_ready, rows_ready = k.sem("spread_ready"), k.sem("rows_ready")
        with nc.Block() as block:
            @block.sync
            def _(sp):
                sp.dma_start(t_raw[:], d["itok_B_34_63"].partition_broadcast(P)).then_inc(loaded, 16)
                sp.dma_start(freqs[:], d["freqs"]).then_inc(loaded, 16)
                sp.dma_start(w_ada[:], d["L0_cond_W_ada"].rearrange("(c p) n -> p c n", p=P)).then_inc(loaded, 16)
                sp.dma_start(b_ada[:], d["L0_cond_b_ada"].partition_broadcast(P)).then_inc(loaded, 16)

            @block.vector
            def _(dve):
                dve.wait_ge(loaded, 64)
                dve.memset(ones[:], 1.0)
                dve.tensor_copy(t[:], t_raw[:])
                dve.drain()
                dve.tensor_scalar(q[:], t[:], 0.01, None, ALU.mult)
                dve.drain()
                dve.tensor_copy(qh[:], q[:])
                dve.drain()
                dve.tensor_tensor(ql[:], q[:], qh[:].bitcast(F32), ALU.subtract)
                dve.drain()
                dve.scalar_tensor_tensor(out=r[:], in0=qh[:].bitcast(F32), scalar=-100.0, in1=t[:], op0=ALU.mult, op1=ALU.add)
                dve.drain()
                dve.scalar_tensor_tensor(out=x[:], in0=ql[:], scalar=-100.0, in1=r[:], op0=ALU.mult, op1=ALU.add)
                dve.drain()
                dve.scalar_tensor_tensor(out=r[:], in0=x[:], scalar=0.01, in1=q[:], op0=ALU.mult, op1=ALU.add)
                dve.drain()
                dve.tensor_scalar(x[:], r[:], 4000.0, None, ALU.mult)
                dve.drain()
                for b in range(batches):
                    dve.tensor_scalar(e[:, b, :], freqs[:], x[:, b:b + 1], None, ALU.mult)
                dve.drain()
                dve.tensor_scalar(turns[:], e[:], 1.0 / (2.0 * np.pi), MAGIC, ALU.mult, ALU.add)
                dve.drain()
                dve.tensor_scalar(turns[:], turns[:], MAGIC, None, ALU.subtract)
                for c in TWO_PI:
                    dve.drain()
                    dve.scalar_tensor_tensor(out=e[:], in0=turns[:], scalar=-c, in1=e[:], op0=ALU.mult, op1=ALU.add)
                dve.drain()
                dve.tensor_scalar(ang[:, :, 0:2], e[:], 3.1415925, -3.1415925, ALU.min, ALU.max)
                dve.tensor_scalar(turns[:], e[:], -1.0, None, ALU.mult)
                dve.drain()
                dve.tensor_tensor(turns[:], turns[:], e[:], ALU.max)
                dve.drain()
                dve.tensor_scalar(ang[:, :, 2:4], turns[:], -1.0, float(np.pi / 2), ALU.mult, ALU.add)
                dve.drain()
                dve.tensor_scalar(turns[:], turns[:], -1.0, None, ALU.mult).then_inc(ang_ready, 1)
                dve.wait_ge(sig_ready, 1)
                dve.tensor_tensor(feat[:], sc[:], sg[:], ALU.mult)
                dve.drain()
                for b in range(batches):
                    for c in range(KT):
                        last = dve.tensor_scalar(spread[:, b, c, :], ones[:], feat[:, b, c:c + 1], None, ALU.mult)
                last.then_inc(spread_ready, 1)
                dve.wait_ge(rows_ready, 1)
                for b in range(batches):
                    dve.tensor_tensor(scale1[:, b, :], rows[:, b, 0, :], b_ada[:, 0:dim], ALU.add)
                    dve.tensor_tensor(shift[:, b, :], rows[:, b, 1, :], b_ada[:, dim:], ALU.add)
                dve.drain()
                dve.tensor_scalar(scale1[:], scale1[:], 1.0, None, ALU.add)

            @block.scalar
            def _(act):
                act.wait_ge(ang_ready, 1)
                act.activation(sc[:], ang[:], ACT.Sin).then_inc(sin_ready, 1)
                act.wait_ge(sin_ready, 1)
                act.activation(sg[:], sc[:], ACT.Sigmoid).then_inc(sig_ready, 1)

            @block.tensor
            def _(pe):
                pe.wait_ge(spread_ready, 1)
                for b in range(batches):
                    for part in range(2):
                        for c in range(KT):
                            last = pe.matmul(rows[:, b, part, :], spread[:, b, c, :],
                                             w_ada[:, c, part * dim:(part + 1) * dim],
                                             start=(c == 0), stop=(c == KT - 1))
                last.then_inc(rows_ready, 1)


def project(nc, d, s, ident, scale1, shift, batches, seq, dim, heads):
    KT = dim // P
    HD = dim // heads
    NCB = seq // CH
    n_chunks = batches * NCB
    PD = 4
    q_scale = float(HD) ** -0.5
    src_v = d["x"].rearrange("b (n t p) c -> (b n) p t c", p=P, t=TPC)
    x0_v = s["x0"].rearrange("(n t p) c -> n p t c", p=P, t=TPC)
    mask_src = d["mask_Bx1xSxS_bk0"].rearrange("b o (n t p) m -> (b o n) p t m", p=P, t=TPC)
    mask_dst = s["mask"].rearrange("b (n t p) m -> (b n) p t m", p=P, t=TPC)
    v_v = s["v"].rearrange("(n t p) c -> n t p c", p=P, t=TPC)
    with Kit(nc) as k:
        w = {n: (k.sb(f"{n}_hi", [P, KT, dim], F32R), k.sb(f"{n}_lo", [P, KT, dim], F32R)) for n in ("wq", "wk", "wv")}
        split_weights(nc, "pw", [
            (lambda e, n=n: d["L0_cond_W" + n[1]].rearrange("(c p) n -> p c n", p=P), w[n][0][:].rearrange("p c n -> p (c n)"),
             w[n][1][:].rearrange("p c n -> p (c n)"), KT * dim) for n in ("wq", "wk", "wv")])
        b_qk = k.sb("b_qk", [P, 2, KT])
        b_v = k.sb("b_v", [P, dim])
        xin = k.sb("xin", [P, 2, TPC, dim])
        xm = k.sb("xm", [P, 2, TPC, dim])
        st = k.sb("st", [P, TPC, 6])
        mv = k.sb("mv", [P, TPC, 2])
        sd = k.sb("sd", [P, TPC])
        rstd = k.sb("rstd", [P, TPC])
        xT = [[k.sb(f"xT{j}{h}", [P, KT, CH], F32R) for h in ("hi", "lo")] for j in range(2)]
        full = k.sb("full", [P, 2, CH])
        parts = [[k.sb(f"part{j}{h}", [P, CH], F32R) for h in ("hi", "lo")] for j in range(PD)]
        vt = k.sb("vt", [P, 2, dim])
        turned = k.ps("turned", [P, 2, KT, P])
        pqk = k.ps("pqk", [P, 4, CH])
        pv = k.ps("pv", [P, 2, dim])
        consts = k.sem("consts")
        src_in = [k.count(f"src_in{j}", unit=16) for j in range(2)]
        var_ready, sd_ready = k.count("var_ready"), k.count("sd_ready")
        xm_ready = k.count("xm_ready", early=2)
        x0_out = [k.count(f"x0_out{j}", early=1, unit=16) for j in range(2)]
        tiles_turned = k.count("tiles_turned")
        hi_ready = k.count("hi_ready")
        lo_ready = k.count("lo_ready", early=2)
        qk_ready, v_ready = k.count("qk_ready"), k.count("v_ready", early=2 * TPC)
        full_ready = k.count("full_ready", early=4)
        parts_ready = k.count("parts_ready", early=2)
        parts_out = [k.count(f"parts_out{j}", early=1, unit=32) for j in range(PD)]
        vt_ready = k.count("vt_ready", early=2)
        v_out = [k.count(f"v_out{j}", early=1, unit=16) for j in range(2)]
        mask = k.sb("mask_rows", [P, TPC, seq], BF16)
        mask_in, mask_scaled = k.count("mask_in", unit=16), k.count("mask_scaled")
        mask_out = k.count("mask_out", unit=16 * TPC)
        passed = k.sem("passed_p")
        bias_ready = k.sem("bias_ready")
        NQK = 2 * KT

        def next_exists(n):
            return exists(n + 1 if isinstance(n, int) else n, n_chunks)

        with nc.Block() as block:
            @block.gpsimd
            def _(pool):
                def load_rows(n, j):
                    pool.wait_ge(xm_ready.sem, xm_ready.at(n - 2))
                    pool.sem_inc(passed, 1)
                    pool.dma_start(xin[:, j], src_v[n]).then_inc(src_in[j].sem, 16)

                def load(n, j, half):
                    pool.dma_start(mask[:], mask_src[n]).then_inc(mask_in.sem, 16)
                    if next_exists(n):
                        load_rows(n + 1, 1 - j)
                    pool.wait_ge(mask_scaled.sem, mask_scaled.at(n))
                    pool.sem_inc(passed, 1)
                    for t in range(TPC):
                        pool.dma_start(mask_dst[n, :, t], mask[:, t]).then_inc(mask_out.sem, 16)
                    pool.wait_ge(mask_out.sem, mask_out.at(n))
                    pool.sem_inc(passed, 1)
                load_rows(0, 0)
                sweep(pool, n_chunks, load, tail=2)

            @block.sync
            def _(sp):
                sp.dma_start(b_qk[:, 0, :], d["L0_cond_bq"].rearrange("(c p) -> p c", p=P)).then_inc(consts, 16)
                sp.dma_start(b_qk[:, 1, :], d["L0_cond_bk"].rearrange("(c p) -> p c", p=P)).then_inc(consts, 16)
                sp.dma_start(b_v[:], d["L0_cond_bv"].partition_broadcast(P)).then_inc(consts, 16)
                for c in x0_out + parts_out + v_out:
                    sp.sem_inc(c.sem, c.head_start)
                with sp.Fori(0, batches) as b:
                    with sp.Fori(0, NCB // 2) as half:
                        for j in range(2):
                            nb = half * 2 + j
                            n = b * NCB + nb
                            sp.wait_ge(xm_ready.sem, xm_ready.at(n))
                            sp.dma_start(x0_v[n], xm[:, j]).then_inc(x0_out[j].sem, 16)
                            for p in range(NQK):
                                sp.wait_ge(parts_ready.sem, parts_ready.at(n * NQK + p))
                                dst = s["q"] if p < KT else s["k"]
                                for part in range(2):
                                    sp.dma_start(dst[b, p % KT, part, :, bass.ds(nb * CH, CH)], parts[p % PD][part][:].bitcast(F32))\
                                      .then_inc(parts_out[p % PD].sem, 16)
                            for t in range(TPC):
                                sp.wait_ge(vt_ready.sem, vt_ready.at(n * TPC + t))
                                sp.dma_start(v_v[n, t], vt[:, t % 2]).then_inc(v_out[t % 2].sem, 16)
                for j in range(2):
                    sp.wait_ge(x0_out[j].sem, x0_out[j].at(n_chunks // 2 - 1))
                    sp.wait_ge(v_out[j].sem, v_out[j].at(n_chunks * TPC // 2 - 1))
                for j in range(PD):
                    sp.wait_ge(parts_out[j].sem, parts_out[j].at(n_chunks * NQK // PD - 1))

            @block.vector
            def _(dve):
                for c in (xm_ready, lo_ready, parts_ready, vt_ready):
                    dve.sem_inc(c.sem, c.head_start)
                dve.wait_ge(consts, 48)
                dve.tensor_scalar(b_qk[:, 0, :], b_qk[:, 0, :], q_scale, None, ALU.mult).then_inc(bias_ready, 1)

                def stats(n, j, use):
                    dve.wait_ge(src_in[j].sem, src_in[j].at(use))
                    layer_stats(dve, st, mv, xin[:, j])
                    dve.tensor_scalar(rstd[:], mv[:, :, 1], 1e-5, None, ALU.add).then_inc(var_ready.sem, 1)

                def normalise(n, j, use, b):
                    dve.wait_ge(sd_ready.sem, sd_ready.at(n))
                    dve.reciprocal(rstd[:], sd[:])
                    dve.wait_ge(x0_out[j].sem, x0_out[j].at(use - 1))
                    dve.drain()
                    for t in range(TPC):
                        dve.tensor_scalar(xm[:, j, t, :], xin[:, j, t, :], mv[:, t, 0:1], rstd[:, t:t + 1],
                                          ALU.subtract, ALU.mult)
                    dve.drain()
                    for t in range(TPC):
                        dve.tensor_tensor(xm[:, j, t, :], xm[:, j, t, :], scale1[:, b, :], ALU.mult)
                    dve.drain()
                    for t in range(TPC):
                        last = dve.tensor_tensor(xm[:, j, t, :], xm[:, j, t, :], shift[:, b, :], ALU.add)
                    last.then_inc(xm_ready.sem, 1)

                def turned_lo(n, j, t):
                    dve.wait_ge(hi_ready.sem, hi_ready.at(n * TPC + t))
                    dve.tensor_tensor(xT[j][1][:, :, t * P:(t + 1) * P], turned[:, t % 2],
                                      xT[j][0][:, :, t * P:(t + 1) * P].bitcast(F32), ALU.subtract).then_inc(lo_ready.sem, 1)

                def chunk(n, j, use, b, last):
                    for p in range(NQK):
                        dve.wait_ge(full_ready.sem, full_ready.at(n * NQK + p))
                        dve.wait_ge(parts_out[p % PD].sem, parts_out[p % PD].at(n * (NQK // PD) + p // PD - 1))
                        hi, lo = parts[p % PD]
                        dve.tensor_copy(hi[:], full[:, p % 2])
                        dve.drain()
                        dve.tensor_tensor(lo[:], full[:, p % 2], hi[:].bitcast(F32), ALU.subtract)\
                           .then_inc(parts_ready.sem, 1)
                        if p == 1 and next_exists(n):
                            stats(n + 1, 1 - j, use + j)
                        if p == 2 and next_exists(n):
                            normalise(n + 1, 1 - j, use + j, b + 1 if last else b)
                        if p == 3:
                            dve.wait_ge(mask_in.sem, mask_in.at(n))
                            dve.tensor_scalar(mask[:], mask[:], NEG, None, ALU.mult).then_inc(mask_scaled.sem, 1)
                    for t in range(TPC):
                        if next_exists(n):
                            turned_lo(n + 1, 1 - j, t)
                        dve.wait_ge(v_ready.sem, v_ready.at(n * TPC + t))
                        dve.wait_ge(v_out[t % 2].sem, v_out[t % 2].at(n * (TPC // 2) + t // 2 - 1))
                        dve.tensor_tensor(vt[:, t % 2], pv[:, t % 2], b_v[:], ALU.add).then_inc(vt_ready.sem, 1)

                stats(0, 0, 0)
                normalise(0, 0, 0, 0)
                for t in range(TPC):
                    turned_lo(0, 0, t)
                for b in range(batches):
                    if NCB > 2:
                        with dve.Fori(b * NCB // 2, (b + 1) * NCB // 2 - 1) as use:
                            for j in range(2):
                                chunk(use * 2 + j, j, use, b, False)
                    use = (b + 1) * NCB // 2 - 1
                    for j in range(2):
                        chunk(use * 2 + j, j, use, b, j == 1)

            @block.scalar
            def _(act):
                act.sem_inc(full_ready.sem, full_ready.head_start)
                act.wait_ge(bias_ready, 1)

                def root(n):
                    act.wait_ge(var_ready.sem, var_ready.at(n))
                    act.activation(sd[:], rstd[:], ACT.Sqrt).then_inc(sd_ready.sem, 1)

                def turned_hi(n, j, t):
                    act.wait_ge(tiles_turned.sem, tiles_turned.at(n * TPC + t))
                    act.activation(xT[j][0][:, :, t * P:(t + 1) * P], turned[:, t % 2], ACT.Copy).then_inc(hi_ready.sem, 1)

                def chunk(n, j, half):
                    for p in range(NQK):
                        act.wait_ge(qk_ready.sem, qk_ready.at(n * NQK + p))
                        act.wait_ge(parts_ready.sem, parts_ready.at(n * NQK + p - 2))
                        act.activation(full[:, p % 2], pqk[:, p % 4], ACT.Identity,
                                       bias=b_qk[:, p // KT, p % KT:p % KT + 1],
                                       scale=q_scale if p < KT else 1.0).then_inc(full_ready.sem, 1)
                        if p == 2 and next_exists(n):
                            root(n + 1)
                    for t in range(TPC):
                        if next_exists(n):
                            turned_hi(n + 1, 1 - j, t)
                root(0)
                for t in range(TPC):
                    turned_hi(0, 0, t)
                sweep(act, n_chunks, chunk, tail=2)

            @block.tensor
            def _(pe):
                pe.sem_inc(v_ready.sem, v_ready.head_start)

                def turn(n, j, t):
                    if t == 0:
                        pe.wait_ge(xm_ready.sem, xm_ready.at(n))
                    pe.wait_ge(lo_ready.sem, lo_ready.at(n * TPC + t - 2))
                    for c in range(KT):
                        last = pe.transpose(turned[:, t % 2, c, :], xm[:, j, t, c * P:(c + 1) * P], ident[:])
                    last.then_inc(tiles_turned.sem, 1)

                def chunk(n, j, half):
                    pe.wait_ge(lo_ready.sem, lo_ready.at(n * TPC + TPC - 1))
                    for p in range(NQK):
                        pe.wait_ge(full_ready.sem, full_ready.at(n * NQK + p - 4))
                        wh, wl = w["wq" if p < KT else "wk"]
                        o = (p % KT) * P
                        for c in range(KT):
                            last = mm3(pe, pqk[:, p % 4], (wh[:, c, o:o + P], wl[:, c, o:o + P]),
                                       (xT[j][0][:, c, :], xT[j][1][:, c, :]), c == 0, c == KT - 1)
                        last.then_inc(qk_ready.sem, 1)
                    for t in range(TPC):
                        if next_exists(n):
                            turn(n + 1, 1 - j, t)
                        pe.wait_ge(vt_ready.sem, vt_ready.at(n * TPC + t - 2))
                        for c in range(KT):
                            last = mm3(pe, pv[:, t % 2], (xT[j][0][:, c, t * P:(t + 1) * P], xT[j][1][:, c, t * P:(t + 1) * P]),
                                       (w["wv"][0][:, c, :], w["wv"][1][:, c, :]), c == 0, c == KT - 1)
                        last.then_inc(v_ready.sem, 1)
                for t in range(TPC):
                    turn(0, 0, t)
                sweep(pe, n_chunks, chunk, tail=2)


def attend(nc, d, s, ident, batches, seq, dim, heads):
    NT = seq // P
    HD = dim // heads
    HG = P // HD
    groups = batches * heads // HG
    NG = heads // HG
    n_it = groups * NT
    n_heads = n_it * HG
    HALF = seq // 2
    MM = min(HALF, 512)
    PE_MASKED = 1
    POOL_MASKED = HG - PE_MASKED
    QV = HG
    CT = 4
    TURNS = NT // CT
    bias_v = d["fside_Bx16xSxS_0"].rearrange("b (g i) (t p) m -> (b g) i t p m", i=HG, p=P)
    mask_v = s["mask"].rearrange("b (t p) m -> b t p m", p=P)
    q_v = s["q"].rearrange("b g a (i r) (t m) -> (b g) t a r i m", i=HG, m=P)
    k_v = s["k"].rearrange("b g a (i r) m -> (b g) a i r m", i=HG)
    v_v = s["v"].rearrange("(b t p) (g m) -> b g p t m", p=P, b=batches, m=P)
    with Kit(nc) as k:
        scores = k.sb("scores", [P, 2, HG, seq])
        keys = [k.sb(f"keys{h}", [P, seq], F32R) for h in range(HG)]
        queries = [k.sb(f"queries{j}", [P, HG, P], F32R) for j in range(2)]
        values = k.sb("values", [P, NT, P])
        mask = k.sb("mask", [P, 2, seq], BF16)
        ident16 = k.sb("ident16", [P, P], BF16)
        probsT = k.sb("probsT", [P, 2, HG, NT, P])
        top = k.sb("top", [P, HG, 2])
        neg_top = k.sb("neg_top", [P, HG])
        sums = k.sb("sums", [P, 2, HG])
        inv = k.sb("inv", [P, 2, HG])
        ctxT = k.sb("ctxT", [P, P])
        ctx_rows = k.sb("ctx_rows", [P, 2, P])
        ps_s = k.ps("ps_s", [P, 2, 1024])
        ps_t = k.ps("ps_t", [P, 2, 512])
        ps_pv = k.ps("ps_pv", [P, 512])
        ps_c = k.ps("ps_c", [P, 512])

        bias_in = [[k.count(f"bias_in{j}{h}", unit=16) for h in range(HG)] for j in range(2)]
        k_in = [k.count(f"k_in{h}", unit=64) for h in range(HG)]
        q_in = [k.count(f"q_in{j}", unit=64) for j in range(2)]
        v_in = [k.count(f"v_in{q}", unit=16) for q in range(QV)]
        mask_in = [k.count(f"mask_in{j}", unit=16) for j in range(2)]
        masked = k.count("masked")
        ident16_ready = k.sem("ident16_ready")
        kq_ready = k.count("kq_ready")
        v_ready = k.count("v_ready_b", early=QV)
        qk_done = k.count("qk_done")
        scored = k.count("scored", early=2)
        top_ready = k.count("top_ready", early=8)
        exp_done = k.count("exp_done")
        TB = TURNS // 2
        turned = [k.count(f"turned{x}", early=2 * HG * TB) for x in range(2)]
        moved = [k.count(f"moved{x}", early=1) for x in range(2)]
        pv_done = k.count("pv_done", early=2 * QV)
        ctxT_ready = k.count("ctxT_ready", early=1)
        ctx_turned = k.count("ctx_turned", early=1)
        inv_ready = k.count("inv_ready", early=2)
        ctx_ready = k.count("ctx_ready", early=1)
        ctx_out = [k.count(f"ctx_out{j}", early=1, unit=16) for j in range(2)]
        passed = k.sem("passed")

        def after_exists(it):
            return not isinstance(it, int) or 0 <= it + 1 < n_it

        def before_exists(it, back):
            return not isinstance(it, int) or 0 <= it - back < n_it

        with nc.Block() as block:
            @block.sync
            def _(sp):
                with sp.Fori(0, batches) as b:
                  with sp.Fori(0, NG) as gg:
                    g = b * NG + gg

                    def load_keys(h):
                        sp.wait_ge(top_ready.sem, top_ready.at(g * NT * HG - HG + h))
                        for u in range(4):
                            sp.dma_start(keys[h][u * HD:(u + 1) * HD].bitcast(F32), k_v[g, u % 2, h]).then_inc(k_in[h].sem, 16)

                    def tile(half, j, first):
                        t = half * 2 + j
                        it = g * NT + t
                        for h in range(HG):
                            if h == 1:
                                sp.wait_ge(top_ready.sem, top_ready.at(it * HG - HG - 1))
                                sp.dma_start(mask[:, j], mask_v[b, t]).then_inc(mask_in[j].sem, 16)
                                for u in range(4):
                                    sp.dma_start(queries[j][u * HD:(u + 1) * HD].bitcast(F32), q_v[g, t, u // 2])\
                                      .then_inc(q_in[j].sem, 16)
                            sp.wait_ge(turned[1].sem, turned[1].at((it * HG + h - 2 * HG) * TB + TB - 1))
                            sp.dma_start(scores[:, j, h, :], bias_v[g, h, t]).then_inc(bias_in[j][h].sem, 16)
                            if first and j == 0 and h == 2:
                                load_keys(0)
                        if first and j == 0:
                            for h in range(1, HG):
                                load_keys(h)

                    for j in range(2):
                        tile(0, j, True)
                    with sp.Fori(1, NT // 2) as half:
                        for j in range(2):
                            tile(half, j, False)

            @block.gpsimd
            def _(pool):
                with pool.Fori(0, batches) as b:
                  with pool.Fori(0, NG) as gg:
                    g = b * NG + gg

                    def tile(half, j, first):
                        it = g * NT + half * 2 + j
                        use = g * (NT // 2) + half
                        pool.wait_ge(mask_in[j].sem, mask_in[j].at(use))
                        pool.sem_inc(passed, 1)
                        pool.wait_ge(q_in[j].sem, q_in[j].at(use))
                        pool.sem_inc(passed, 1)

                        def relay(h):
                            if first and j == 0:
                                pool.wait_ge(k_in[h].sem, k_in[h].at(g))
                                pool.sem_inc(passed, 1)
                            pool.sem_inc(kq_ready.sem, 1)

                        for h in range(PE_MASKED):
                            relay(h)
                        for h in range(PE_MASKED, HG):
                            relay(h)
                            pool.wait_ge(bias_in[j][h].sem, bias_in[j][h].at(use))
                            pool.sem_inc(passed, 1)
                            pool.tensor_tensor(scores[:, j, h, :], scores[:, j, h, :], mask[:, j], ALU.add).then_inc(masked.sem, 1)
                        for q in range(QV):
                            if first and j == 1:
                                for c in range(QV - 1) if q == 0 else (QV - 1,) if q == 1 else ():
                                    pool.wait_ge(pv_done.sem, pv_done.at(QV * (it - 2) + c))
                                    pool.sem_inc(passed, 1)
                                    part = slice(c * NT // QV, (c + 1) * NT // QV)
                                    pool.dma_start(values[:, part], v_v[b, gg, :, part]).then_inc(v_in[c].sem, 16)
                                pool.wait_ge(v_in[q].sem, v_in[q].at(g))
                                pool.sem_inc(passed, 1)
                            pool.sem_inc(v_ready.sem, 1)

                    for j in range(2):
                        tile(0, j, True)
                    with pool.Fori(1, NT // 2) as half:
                        for j in range(2):
                            tile(half, j, False)
                pool.sem_inc(v_ready.sem, QV)

            @block.tensor
            def _(pe):
                for c in turned + [pv_done, ctx_turned]:
                    pe.sem_inc(c.sem, c.head_start)

                def qk(n, j, h, half):
                    if half == 0:
                        pe.wait_ge(kq_ready.sem, kq_ready.at(n))
                    pe.wait_ge(scored.sem, scored.at(2 * n + half - 2))
                    for c in range(HALF // MM):
                        a = half * HALF + c * MM
                        out = ps_s[:, half, c * MM:(c + 1) * MM]
                        last = pe.matmul(out, queries[j][:, h, :], keys[h][:, a:a + MM], start=True, stop=h >= PE_MASKED)
                        if h < PE_MASKED:
                            last = pe.matmul(out, ident16[:], mask[:, j, a:a + MM], start=False, stop=True)
                    last.then_inc(qk_done.sem, 1)

                def turn(n, j, h, half):
                    if half == 0:
                        pe.wait_ge(exp_done.sem, exp_done.at(n))
                    for c in range(half * TURNS // 2, (half + 1) * TURNS // 2):
                        pe.wait_ge(moved[c % 2].sem, moved[c % 2].at(n * TB + c // 2 - 1))
                        for i in range(CT):
                            kt = c * CT + i
                            last = pe.transpose(ps_t[:, c % 2, i * P:(i + 1) * P], scores[:, j, h, kt * P:(kt + 1) * P], ident[:])
                        last.then_inc(turned[c % 2].sem, 1)

                def pv(it, j, quarter):
                    pe.wait_ge(v_ready.sem, v_ready.at(QV * it + quarter))
                    if quarter == 0:
                        for x in range(2):
                            pe.wait_ge(moved[x].sem, moved[x].at((it * HG + HG) * TB - 1))
                        pe.wait_ge(ctxT_ready.sem, ctxT_ready.at(it - 1))
                    for kt in range(quarter * NT // QV, (quarter + 1) * NT // QV):
                        for h in range(HG):
                            last = pe.matmul(ps_pv[h * HD:(h + 1) * HD, 0:P], values[:, kt, h * HD:(h + 1) * HD],
                                             probsT[:, j, h, kt, :], start=(kt == 0), stop=(kt == NT - 1), skip_group_check=True)
                    last.then_inc(pv_done.sem, 1)

                def turn_ctx(it):
                    pe.wait_ge(ctxT_ready.sem, ctxT_ready.at(it))
                    pe.wait_ge(ctx_ready.sem, ctx_ready.at(it - 1))
                    pe.transpose(ps_c[:, 0:P], ctxT[:], ident[:]).then_inc(ctx_turned.sem, 1)

                def qk_ahead(it, j, h, x):
                    if h < HG and exists(it, n_it):
                        qk(it * HG + h, j, h, x)
                    if h >= HG and after_exists(it):
                        qk(it * HG + h, 1 - j, h - HG, x)

                def step(it, j, half):
                    for h in range(HG):
                        if exists(it, n_it):
                            turn(it * HG + h, j, h, 0)
                        qk_ahead(it, j, h + 2, 1)
                        if exists(it, n_it):
                            turn(it * HG + h, j, h, 1)
                        qk_ahead(it, j, h + 3, 0)
                        if before_exists(it, 1):
                            pv(it - 1, 1 - j, h)
                        if h == 1 and before_exists(it, 2):
                            turn_ctx(it - 2)

                pe.wait_ge(ident16_ready, 1)
                for h in range(2):
                    for x in range(2):
                        qk(h, 0, h, x)
                qk(2, 0, 2, 0)
                sweep(pe, n_it, step, head=2, tail=2, extra=2)

            @block.vector
            def _(dve):
                for c in (scored, top_ready, moved[0], ctxT_ready, ctx_ready, inv_ready):
                    dve.sem_inc(c.sem, c.head_start)
                dve.tensor_copy(ident16[:], ident[:]).then_inc(ident16_ready, 1)

                def score(n, j, h, it, half, x):
                    if x == 0 and h >= PE_MASKED:
                        dve.wait_ge(masked.sem, masked.at(it * POOL_MASKED + h - PE_MASKED))
                    elif x == 0:
                        dve.wait_ge(bias_in[j][h].sem, bias_in[j][h].at(half))
                    else:
                        dve.wait_ge(scored.sem, scored.at(2 * n))
                    dve.wait_ge(qk_done.sem, qk_done.at(2 * n + x))
                    dve.sem_inc(passed, 1)
                    part = scores[:, j, h, x * HALF:(x + 1) * HALF]
                    dve.tensor_tensor_reduce(out=part, in0=ps_s[:, x, 0:HALF], in1=part, scale=1.0,
                                             scalar=LOW if x == 0 else top[:, h, 0:1], op0=ALU.add, op1=ALU.max,
                                             accum_out=top[:, h, x:x + 1]).then_inc(scored.sem, 1)

                def negate(n, h):
                    dve.wait_ge(scored.sem, scored.at(2 * n + 1))
                    dve.tensor_scalar(neg_top[:, h:h + 1], top[:, h, 1:2], -1.0, None, ALU.mult).then_inc(top_ready.sem, 1)

                def move(n, j, h, x):
                    for c in range(x * TURNS // 2, (x + 1) * TURNS // 2):
                        if c % 2 == 0:
                            dve.wait_ge(turned[0].sem, turned[0].at(n * TB + c // 2))
                            dve.tensor_copy(probsT[:, j, h, c * CT:(c + 1) * CT, :],
                                            ps_t[:, 0].rearrange("p (i m) -> p i m", m=P)).then_inc(moved[0].sem, 1)

                def step(it, j, half):
                    here = exists(it, n_it)
                    for h in range(HG):
                        ahead = here if h < 2 else after_exists(it)
                        for x in range(2):
                            if ahead and h < 2:
                                score(it * HG + h + 2, j, h + 2, it, half, x)
                            if ahead and h >= 2:
                                score(it * HG + h + 2, 1 - j, h - 2, it + 1, half + j, x)
                            if here:
                                if h == 0 and x == 0:
                                    dve.wait_ge(pv_done.sem, pv_done.at(QV * (it - 2) + QV - 1))
                                move(it * HG + h, j, h, x)
                        if ahead:
                            negate(it * HG + h + 2, (h + 2) % HG)
                        if h == 0 and before_exists(it, 2):
                            dve.wait_ge(pv_done.sem, pv_done.at(QV * (it - 2) + QV - 1))
                            dve.wait_ge(ctx_turned.sem, ctx_turned.at(it - 3))
                            dve.tensor_copy(ctxT[:], ps_pv[:, 0:P]).then_inc(ctxT_ready.sem, 1)
                        if h == 2 and before_exists(it, 2):
                            dve.wait_ge(ctx_turned.sem, ctx_turned.at(it - 2))
                            dve.wait_ge(ctx_out[j].sem, ctx_out[j].at(half - 2))
                            dve.tensor_tensor(ctx_rows[:, j].rearrange("p (h m) -> p h m", m=HD),
                                              ps_c[:, 0:P].rearrange("p (h m) -> p h m", m=HD),
                                              inv[:, j, :].unsqueeze(2).broadcast_to([P, HG, HD]), ALU.mult).then_inc(ctx_ready.sem, 1)
                    if here:
                        dve.drain()
                        dve.wait_ge(exp_done.sem, exp_done.at(it * HG + HG - 1))
                        dve.reciprocal(inv[:, j, :], sums[:, j, :]).then_inc(inv_ready.sem, 1)

                for h in range(2):
                    for x in range(2):
                        score(h, 0, h, 0, 0, x)
                    negate(h, h)
                sweep(dve, n_it, step, head=2, tail=2, extra=2)

            @block.scalar
            def _(act):
                act.sem_inc(moved[1].sem, moved[1].head_start)
                for c in ctx_out:
                    act.sem_inc(c.sem, c.head_start)

                def exp(n, j, h):
                    act.wait_ge(top_ready.sem, top_ready.at(n))
                    act.activation(scores[:, j, h, :], scores[:, j, h, :], ACT.Exp, bias=neg_top[:, h:h + 1],
                                   accum_out=sums[:, j, h:h + 1]).then_inc(exp_done.sem, 1)

                def step(it, j, half):
                    here = exists(it, n_it)
                    for h in range(HG):
                        if h < HG - 1 and here:
                            exp(it * HG + h + 1, j, h + 1)
                        if h == HG - 1 and after_exists(it):
                            act.wait_ge(inv_ready.sem, inv_ready.at(it - 1))
                            exp(it * HG + HG, 1 - j, 0)
                        if here:
                            if h == 0:
                                act.wait_ge(pv_done.sem, pv_done.at(QV * (it - 2) + QV - 1))
                            for c in range(1, TURNS, 2):
                                act.wait_ge(turned[1].sem, turned[1].at((it * HG + h) * TB + c // 2))
                                act.activation(probsT[:, j, h, c * CT:(c + 1) * CT, :],
                                               ps_t[:, 1].rearrange("p (i m) -> p i m", m=P), ACT.Copy).then_inc(moved[1].sem, 1)

                    if before_exists(it, 2):
                        act.wait_ge(ctx_ready.sem, ctx_ready.at(it - 2))
                        act.dma_start(s["ctx"][it - 2], ctx_rows[:, j]).then_inc(ctx_out[j].sem, 16)

                exp(0, 0, 0)
                sweep(act, n_it, step, head=2, tail=2, extra=2)
                for j in range(2):
                    act.wait_ge(ctx_out[j].sem, ctx_out[j].at(n_it // 2 - 1))


def out_proj(nc, d, s, ident, batches, seq, dim, heads):
    KT = dim // P
    NT = seq // P
    NCB = seq // CH
    n_chunks = batches * NCB
    ctx_v = s["ctx"].rearrange("(b g t) p m -> b t p g m", b=batches, t=NT)
    x0_v = s["x0"].rearrange("(n t p) c -> n p t c", p=P, t=TPC)
    x1_v = s["x1"].rearrange("(n t p) c -> n p t c", p=P, t=TPC)
    with Kit(nc) as k:
        wo = (k.sb("wo_hi", [P, KT, dim], F32R), k.sb("wo_lo", [P, KT, dim], F32R))
        split_weights(nc, "ow", [(lambda e: d["L0_cond_Wo"].rearrange("(c p) n -> p c n", p=P),
                                  wo[0][:].rearrange("p c n -> p (c n)"), wo[1][:].rearrange("p c n -> p (c n)"), KT * dim)])
        bo = k.sb("bo", [P, dim])
        ctx = k.sb("ctx_in", [P, 2, TPC, dim])
        x0 = k.sb("x0_in", [P, 2, TPC, dim])
        x1 = k.sb("x1_sb", [P, 2, TPC, dim])
        cT = [[k.sb(f"cT{j}{h}", [P, KT, P], F32R) for h in ("hi", "lo")] for j in range(2)]
        turned = k.ps("turned_o", [P, 2, KT, P])
        out = k.ps("out_o", [P, 4, dim])
        consts = k.sem("consts_o")
        ctx_in = [k.count(f"ctx_in{j}", unit=16 * TPC) for j in range(2)]
        x0_in = [k.count(f"x0_in{j}", unit=16) for j in range(2)]
        tile_turned, hi_ready = k.count("tile_turned"), k.count("hi_ready_o", early=2)
        lo_ready = k.count("lo_ready_o", early=2)
        out_done = k.count("out_done", early=2)
        passed = k.sem("passed_o")
        x1_ready = k.count("x1_ready", early=2 * TPC)
        x1_out = [k.count(f"x1_out{j}", early=1, unit=16) for j in range(2)]
        with nc.Block() as block:
            @block.gpsimd
            def _(pool):
                pool.dma_start(bo[:], d["L0_cond_bo"].partition_broadcast(P)).then_inc(consts, 16)
                with pool.Fori(0, batches) as b:
                    with pool.Fori(0, NCB // 2) as half:
                        for j in range(2):
                            nb = half * 2 + j
                            n = b * NCB + nb
                            pool.wait_ge(x1_ready.sem, x1_ready.at((n - 1) * TPC - 1))
                            pool.sem_inc(passed, 1)
                            for t in range(TPC):
                                pool.dma_start(ctx[:, j, t].rearrange("p (g m) -> p g m", m=P), ctx_v[b, nb * TPC + t])\
                                    .then_inc(ctx_in[j].sem, 16)
                            pool.dma_start(x0[:, j], x0_v[n]).then_inc(x0_in[j].sem, 16)

            @block.sync
            def _(sp):
                for c in x1_out:
                    sp.sem_inc(c.sem, c.head_start)

                def store(n, j, half):
                    sp.wait_ge(x1_ready.sem, x1_ready.at((n + 1) * TPC - 1))
                    sp.dma_start(x1_v[n], x1[:, j]).then_inc(x1_out[j].sem, 16)
                sweep(sp, n_chunks, store)
                for j in range(2):
                    sp.wait_ge(x1_out[j].sem, x1_out[j].at(n_chunks // 2 - 1))

            @block.tensor
            def _(pe):
                pe.sem_inc(out_done.sem, out_done.head_start)

                def chunk(n, j, half):
                    pe.wait_ge(ctx_in[j].sem, ctx_in[j].at(half))
                    for t in range(TPC + 1):
                        if t < TPC:
                            pe.wait_ge(lo_ready.sem, lo_ready.at(n * TPC + t - 2))
                            for c in range(KT):
                                last = pe.transpose(turned[:, t % 2, c, :], ctx[:, j, t, c * P:(c + 1) * P], ident[:])
                            last.then_inc(tile_turned.sem, 1)
                        if t >= 1:
                            u = t - 1
                            pe.wait_ge(lo_ready.sem, lo_ready.at(n * TPC + u))
                            pe.wait_ge(x1_ready.sem, x1_ready.at(n * TPC + u - 4))
                            for c in range(KT):
                                last = mm3(pe, out[:, u, :], (cT[u % 2][0][:, c, :], cT[u % 2][1][:, c, :]),
                                           (wo[0][:, c, :], wo[1][:, c, :]), c == 0, c == KT - 1)
                            last.then_inc(out_done.sem, 1)
                sweep(pe, n_chunks, chunk)

            @block.scalar
            def _(act):
                act.sem_inc(hi_ready.sem, hi_ready.head_start)

                def chunk(n, j, half):
                    for t in range(TPC):
                        act.wait_ge(out_done.sem, out_done.at(n * TPC + t - 2))
                        act.wait_ge(tile_turned.sem, tile_turned.at(n * TPC + t))
                        act.activation(cT[t % 2][0][:], turned[:, t % 2], ACT.Copy).then_inc(hi_ready.sem, 1)
                sweep(act, n_chunks, chunk)

            @block.vector
            def _(dve):
                dve.sem_inc(lo_ready.sem, lo_ready.head_start)
                dve.sem_inc(x1_ready.sem, x1_ready.head_start)
                dve.wait_ge(consts, 16)

                def chunk(n, j, half):
                    dve.wait_ge(x0_in[j].sem, x0_in[j].at(half))
                    dve.wait_ge(x1_out[j].sem, x1_out[j].at(half - 1))
                    for t in range(TPC + 1):
                        if t < TPC:
                            dve.wait_ge(hi_ready.sem, hi_ready.at(n * TPC + t))
                            dve.tensor_tensor(cT[t % 2][1][:], turned[:, t % 2], cT[t % 2][0][:].bitcast(F32), ALU.subtract)\
                               .then_inc(lo_ready.sem, 1)
                            dve.tensor_tensor(x0[:, j, t, :], x0[:, j, t, :], bo[:], ALU.add)
                        if t >= 1:
                            u = t - 1
                            dve.drain()
                            dve.wait_ge(out_done.sem, out_done.at(n * TPC + u))
                            dve.tensor_tensor(x1[:, j, u, :], out[:, u, :], x0[:, j, u, :], ALU.add).then_inc(x1_ready.sem, 1)
                sweep(dve, n_chunks, chunk)


def ffn(nc, ident, tag, w, index, x_src, x_dst, first, n_chunks, dim, dff, total=None, ortho=None):
    KT = dim // P
    FT = dff // P
    QF = 4
    NQ = FT // QF
    PART = TPC * dim
    assert KT * QF * P == PART and QF * dim == PART
    half_ln = FT // 2
    x_v = x_src.rearrange("(n t p) c -> n p t c", p=P, t=TPC)
    y_v = x_dst.rearrange("(n t p) c -> n p t c", p=P, t=TPC)
    eps = 1e-5 if first else 1e-12
    with Kit(nc) as k:
        w1 = [k.sb(f"{tag}_w1{h}", [P, KT, dff], F32R) for h in ("hi", "lo")]
        w2 = [k.sb(f"{tag}_w2{h}", [P, FT, dim], F32R) for h in ("hi", "lo")]
        b1 = k.sb(f"{tag}_b1", [P, FT])
        b2 = k.sb(f"{tag}_b2", [P, dim])
        gain = k.sb(f"{tag}_gain", [P, dim])
        beta = k.sb(f"{tag}_beta", [P, dim])
        x = k.sb(f"{tag}_x", [P, 2, TPC, dim])
        y = k.sb(f"{tag}_y", [P, TPC, dim])
        hn = k.sb(f"{tag}_hn", [P, TPC, dim]) if first else None
        st = k.sb(f"{tag}_st", [P, TPC, 6])
        mv = k.sb(f"{tag}_mv", [P, TPC, 2])
        var = k.sb(f"{tag}_var", [P, TPC])
        sd = k.sb(f"{tag}_sd", [P, TPC])
        xT = [k.sb(f"{tag}_xT{h}", [P, KT, CH], F32R) for h in ("hi", "lo")]
        act_out = k.sb(f"{tag}_act", [P, 2, CH])
        a = [[k.sb(f"{tag}_a{j}{h}", [P, CH], F32R) for h in ("hi", "lo")] for j in range(2)]
        turned = k.ps(f"{tag}_turned", [P, 2, KT, P])
        up = k.ps(f"{tag}_up", [P, 2, CH])
        out = k.ps(f"{tag}_out", [P, TPC, dim])
        consts = k.sem(f"{tag}_consts")
        x_in = [k.count(f"{tag}_x_in{j}", unit=16) for j in range(2)]
        h_ready = k.count(f"{tag}_h_ready")
        var_ready, sd_ready = k.count(f"{tag}_var_ready"), k.count(f"{tag}_sd_ready")
        tile_turned, hi_ready = k.count(f"{tag}_tile_turned"), k.count(f"{tag}_hi_ready")
        lo_ready = k.count(f"{tag}_lo_ready", early=2)
        up_done = k.count(f"{tag}_up_done", early=2)
        act_ready = k.count(f"{tag}_act_ready", early=2)
        split = k.count(f"{tag}_split", early=2)
        down_done = k.count(f"{tag}_down_done", early=2)
        sums_read = k.count(f"{tag}_sums_read", early=1)
        taken = k.count(f"{tag}_taken", early=1)
        y_ready = k.count(f"{tag}_y_ready", early=1)
        normal = k.count(f"{tag}_normal")
        scaled = k.count(f"{tag}_scaled")
        passed = k.sem(f"{tag}_passed")
        y_out = k.count(f"{tag}_y_out", early=1, unit=16)
        y_added = k.count(f"{tag}_y_added", early=1)
        wide = None if first else k.sb(f"{tag}_wide", [P, TPC, dim])
        wide_set = k.sem(f"{tag}_wide_set")
        raw = [y, hn if first else wide]
        w_in = [k.count(f"{tag}_w_in{j}", unit=16) for j in range(2)]
        w_hi, w_lo = k.count(f"{tag}_w_hi"), k.count(f"{tag}_w_lo")

        def part_of(q, i, side):
            if i == 0:
                return w1[side][:, :, q * QF * P:(q + 1) * QF * P], raw[0][:]
            return w2[side][:, q * QF:(q + 1) * QF, :], raw[1][:]

        def raw_view(q, i, e):
            if i == 0:
                return w["w1"](e)[:, q * QF * P:(q + 1) * QF * P].rearrange("(c p) n -> p c n", p=P)
            return w["w2"](e)[q * QF * P:(q + 1) * QF * P, :].rearrange("(c p) n -> p c n", p=P)
        gs_sq, gs_root, gs_inv = k.count(f"{tag}_gs_sq"), k.count(f"{tag}_gs_root"), k.count(f"{tag}_gs_inv")
        steps = ortho["R"] // n_chunks if ortho else 1
        spacing = FT // steps
        if ortho:
            assert steps * n_chunks == ortho["R"] and spacing >= 2

        def later(n):
            return not isinstance(n, int) or n >= 1

        def next_exists(n):
            return exists(n + 1 if isinstance(n, int) else n, n_chunks)

        with nc.Block() as block:
            @block.sync
            def _(sp):
                sp.sem_inc(y_out.sem, y_out.head_start)
                e = read_index(sp, index)
                sp.dma_start(b1[:], w["b1"](e).rearrange("(c p) -> p c", p=P)).then_inc(consts, 16)
                for row, name in ((b2, "b2"), (gain, "gain"), (beta, "beta")):
                    sp.dma_start(row[:], w[name](e).partition_broadcast(P)).then_inc(consts, 16)
                for n in range(2):
                    sp.dma_start(x[:, n], x_v[n]).then_inc(x_in[n].sem, 16)
                for q in range(NQ):
                    for i in range(2):
                        if q >= 1:
                            sp.wait_ge(w_lo.sem, w_lo.at(2 * (q - 1) + i))
                        elif i == 1 and first:
                            sp.wait_ge(tile_turned.sem, tile_turned.at(TPC - 1))
                        sp.dma_start(raw[i][:], raw_view(q, i, e)).then_inc(w_in[i].sem, 16)

                def chunk(n, j, half):
                    if later(n) and next_exists(n):
                        sp.wait_ge(taken.sem, taken.at(n - 1))
                        sp.dma_start(x[:, 1 - j], x_v[n + 1]).then_inc(x_in[1 - j].sem, 16)
                    sp.wait_ge(y_ready.sem, y_ready.at(n))
                    sp.dma_start(y_v[n], y[:]).then_inc(y_out.sem, 16)
                sweep(sp, n_chunks, chunk, head=2, tail=2)
                sp.wait_ge(y_out.sem, y_out.at(n_chunks - 1))

            @block.gpsimd
            def _(pool):
                pool.sem_inc(y_added.sem, y_added.head_start)
                if not first:
                    pool.sem_inc(y_ready.sem, y_ready.head_start)
                    pool.wait_ge(consts, 64)
                if ortho:
                    gram_schmidt(nc, pool, k, ortho, gs_sq, gs_inv)
                if total is not None:
                    pool.wait_ge(w_lo.sem, w_lo.at(2 * NQ - 1))
                    pool.memset(wide[:], 0.0).then_inc(wide_set, 1)
                    pool.wait_ge(wide_set, 1)

                    def chunk(n, j, half):
                        if next_exists(n):
                            pool.wait_ge(normal.sem, normal.at(n))
                            pool.tensor_tensor(y[:], y[:], gain[:].unsqueeze(1).broadcast_to([P, TPC, dim]), ALU.mult)\
                                .then_inc(scaled.sem, 1)
                            pool.wait_ge(scaled.sem, scaled.at(n))
                            pool.sem_inc(passed, 1)
                            pool.tensor_tensor(y[:], y[:], beta[:].unsqueeze(1).broadcast_to([P, TPC, dim]), ALU.add)\
                                .then_inc(y_ready.sem, 1)
                        pool.wait_ge(y_ready.sem, y_ready.at(n))
                        pool.sem_inc(passed, 1)
                        pool.wait_ge(y_added.sem, y_added.at(n - 1))
                        pool.sem_inc(passed, 1)
                        pool.tensor_tensor(wide[:], wide[:], y[:], ALU.add).then_inc(y_added.sem, 1)
                    sweep(pool, n_chunks, chunk, tail=2)
                    pool.wait_ge(y_added.sem, y_added.at(n_chunks - 1))
                    pool.tensor_tensor(wide[:, 0:2], wide[:, 0:2], wide[:, 2:4], ALU.add).then_inc(wide_set, 1)
                    pool.wait_ge(wide_set, 2)
                    pool.tensor_tensor(total, wide[:, 0], wide[:, 1], ALU.add)

            @block.tensor
            def _(pe):
                pe.sem_inc(up_done.sem, up_done.head_start)
                pe.sem_inc(down_done.sem, down_done.head_start)

                def down(n, f):
                    pe.wait_ge(split.sem, split.at(n * FT + f))
                    if f == 0:
                        pe.wait_ge(sums_read.sem, sums_read.at(n - 1))
                    if not later(n) and f % QF == 0:
                        pe.wait_ge(w_lo.sem, w_lo.at(2 * (f // QF) + 1))
                    for t in range(TPC):
                        last = mm3(pe, out[:, t, :], (a[f % 2][0][:, t * P:(t + 1) * P], a[f % 2][1][:, t * P:(t + 1) * P]),
                                   (w2[0][:, f, :], w2[1][:, f, :]), f == 0, f == FT - 1)
                    last.then_inc(down_done.sem, 1)

                def turn(n, j, half, t):
                    if t == 0 and first:
                        pe.wait_ge(h_ready.sem, h_ready.at(n))
                    if t == 0 and not first:
                        pe.wait_ge(x_in[j].sem, x_in[j].at(half))
                    src = hn[:] if first else x[:, j]
                    pe.wait_ge(lo_ready.sem, lo_ready.at(n * TPC + t - 2))
                    for c in range(KT):
                        last = pe.transpose(turned[:, t % 2, c, :], src[:, t, c * P:(c + 1) * P], ident[:])
                    last.then_inc(tile_turned.sem, 1)

                def chunk(n, j, half):
                    pe.wait_ge(lo_ready.sem, lo_ready.at(n * TPC + TPC - 1))
                    for f in range(FT):
                        if not later(n) and f % QF == 0:
                            pe.wait_ge(w_lo.sem, w_lo.at(2 * (f // QF)))
                        pe.wait_ge(act_ready.sem, act_ready.at(n * FT + f - 2))
                        for c in range(KT):
                            last = mm3(pe, up[:, f % 2, :], (w1[0][:, c, f * P:(f + 1) * P], w1[1][:, c, f * P:(f + 1) * P]),
                                       (xT[0][:, c, :], xT[1][:, c, :]), c == 0, c == KT - 1)
                        last.then_inc(up_done.sem, 1)
                        if f >= 1 and f < FT - 1:
                            down(n, f - 1)
                    for t in range(TPC):
                        if next_exists(n):
                            turn(n + 1, 1 - j, half + j, t)
                        if t == 1:
                            down(n, FT - 2)
                    down(n, FT - 1)
                for t in range(TPC):
                    turn(0, 0, 0, t)
                sweep(pe, n_chunks, chunk, head=2, tail=2)

            @block.scalar
            def _(act):
                act.sem_inc(act_ready.sem, act_ready.head_start)
                act.wait_ge(consts, 64)

                def root(i):
                    act.wait_ge(var_ready.sem, var_ready.at(i))
                    act.activation(sd[:], var[:], ACT.Sqrt).then_inc(sd_ready.sem, 1)

                def weights_hi(q, i):
                    act.wait_ge(w_in[i].sem, w_in[i].at(q))
                    hi, src = part_of(q, i, 0)
                    act.activation(hi, src, ACT.Copy).then_inc(w_hi.sem, 1)

                def turned_hi(n):
                    for t in range(TPC):
                        act.wait_ge(tile_turned.sem, tile_turned.at(n * TPC + t))
                        act.activation(xT[0][:, :, t * P:(t + 1) * P], turned[:, t % 2], ACT.Copy).then_inc(hi_ready.sem, 1)

                def chunk(n, j, half):
                    for f in range(FT):
                        act.wait_ge(up_done.sem, up_done.at(n * FT + f))
                        act.wait_ge(split.sem, split.at(n * FT + f - 2))
                        act.activation(act_out[:, f % 2], up[:, f % 2], ACT.Gelu_apprx_sigmoid if first else ACT.Gelu,
                                       bias=b1[:, f:f + 1]).then_inc(act_ready.sem, 1)
                        if not later(n) and f // QF + 1 < NQ and f % QF < 2:
                            weights_hi(f // QF + 1, f % QF)
                        if ortho and f % spacing == 0:
                            act.wait_ge(gs_sq.sem, gs_sq.at(n * steps + f // spacing))
                            act.activation(ortho["root"][:], ortho["sq"][:], ACT.Sqrt).then_inc(gs_root.sem, 1)
                        if f == half_ln and first and next_exists(n):
                            root(n + 1)
                        if f == 2 and not first and later(n):
                            root(n - 1)
                    if next_exists(n):
                        turned_hi(n + 1)
                if first:
                    root(0)
                turned_hi(0)
                for i in range(2):
                    weights_hi(0, i)
                sweep(act, n_chunks, chunk, head=2, tail=2)
                if not first:
                    root(n_chunks - 1)

            @block.vector
            def _(dve):
                for c in (lo_ready, split, sums_read, taken) + ((y_ready,) if first else ()):
                    dve.sem_inc(c.sem, c.head_start)
                dve.wait_ge(consts, 64)

                def stats(v):
                    layer_stats(dve, st, mv, v)
                    dve.tensor_scalar(var[:], mv[:, :, 1], eps, None, ALU.add).then_inc(var_ready.sem, 1)

                def normalise(i, v, dst, whole=first):
                    dve.wait_ge(sd_ready.sem, sd_ready.at(i))
                    dve.reciprocal(var[:], sd[:])
                    dve.drain()
                    for t in range(TPC):
                        last = dve.tensor_scalar(dst[:, t, :], v[:, t, :], mv[:, t, 0:1], var[:, t:t + 1], ALU.subtract, ALU.mult)
                    if not whole:
                        last.then_inc(normal.sem, 1)
                        return
                    dve.drain()
                    dve.tensor_tensor(dst[:], dst[:], gain[:].unsqueeze(1).broadcast_to([P, TPC, dim]), ALU.mult)
                    dve.drain()
                    dve.tensor_tensor(dst[:], dst[:], beta[:].unsqueeze(1).broadcast_to([P, TPC, dim]), ALU.add)\
                       .then_inc((h_ready if first else y_ready).sem, 1)

                def weights_lo(q, i):
                    dve.wait_ge(w_hi.sem, w_hi.at(2 * q + i))
                    hi, src = part_of(q, i, 0)
                    dve.tensor_tensor(part_of(q, i, 1)[0], src, hi.bitcast(F32), ALU.subtract).then_inc(w_lo.sem, 1)

                def turned_lo(n):
                    for t in range(TPC):
                        dve.wait_ge(hi_ready.sem, hi_ready.at(n * TPC + t))
                        dve.tensor_tensor(xT[1][:, :, t * P:(t + 1) * P], turned[:, t % 2],
                                          xT[0][:, :, t * P:(t + 1) * P].bitcast(F32), ALU.subtract).then_inc(lo_ready.sem, 1)

                def chunk(n, j, half):
                    for f in range(FT):
                        dve.wait_ge(act_ready.sem, act_ready.at(n * FT + f))
                        dve.wait_ge(down_done.sem, down_done.at(n * FT + f - 2))
                        hi, lo = a[f % 2]
                        dve.tensor_copy(hi[:], act_out[:, f % 2])
                        dve.drain()
                        dve.tensor_tensor(lo[:], act_out[:, f % 2], hi[:].bitcast(F32), ALU.subtract).then_inc(split.sem, 1)
                        if not later(n) and f // QF + 1 < NQ and f % QF < 2:
                            weights_lo(f // QF + 1, f % QF)
                        if ortho and f % spacing == 1:
                            dve.wait_ge(gs_root.sem, gs_root.at(n * steps + f // spacing))
                            dve.tensor_scalar(ortho["inv"][:], ortho["root"][:], 1e-8, None, ALU.add)
                            dve.drain()
                            dve.reciprocal(ortho["inv"][:], ortho["inv"][:]).then_inc(gs_inv.sem, 1)
                        if f == half_ln and first and next_exists(n):
                            dve.wait_ge(x_in[1 - j].sem, x_in[1 - j].at(half + j))
                            stats(x[:, 1 - j])
                        if f == half_ln + 1 and first and next_exists(n):
                            normalise(n + 1, x[:, 1 - j], hn)
                        if f == 1 and not first and later(n):
                            stats(y)
                        if f == 3 and not first and later(n):
                            normalise(n - 1, y, y)
                    if next_exists(n):
                        turned_lo(n + 1)
                    dve.wait_ge(y_out.sem, y_out.at(n - 1))
                    if total is not None:
                        dve.wait_ge(y_added.sem, y_added.at(n - 1))
                    dve.wait_ge(down_done.sem, down_done.at((n + 1) * FT - 1))
                    dve.tensor_tensor(y[:], out[:], b2[:].unsqueeze(1).broadcast_to([P, TPC, dim]), ALU.add)\
                       .then_inc(sums_read.sem, 1)
                    dve.drain()
                    dve.tensor_tensor(y[:], y[:], x[:, j], ALU.add).then_inc(taken.sem, 1)
                    if first:
                        dve.drain().then_inc(y_ready.sem, 1)
                dve.wait_ge(x_in[0].sem, x_in[0].at(0))
                if first:
                    stats(x[:, 0])
                    normalise(0, x[:, 0], hn)
                turned_lo(0)
                for i in range(2):
                    weights_lo(0, i)
                sweep(dve, n_chunks, chunk, head=2, tail=2)
                if not first:
                    dve.wait_ge(taken.sem, taken.at(n_chunks - 1))
                    stats(y)
                    normalise(n_chunks - 1, y, y, whole=True)


def gram_schmidt(nc, pool, k, o, sq_ready, inv_ready):
    X, R, KT = o["X"], o["R"], o["KT"]
    later = k.sb("gs_later", [P, R, R])
    col = k.sb("gs_col", [P, 2, KT])
    prod = k.sb("gs_prod", [P, 2, R, KT])
    sums = k.sb("gs_sums", [P, 2, R])
    dots = k.sb("gs_dots", [P, 2, R])
    coef = k.sb("gs_coef", [P, 2, R])
    scale = k.sb("gs_scale", [P, 2, R])
    loaded = k.sem("gs_loaded")
    done = k.sem("gs_done")
    for m in range(2):
        for c in range(KT):
            pool.dma_start(o["raw"][:, m, c, :], o["src"][m][c * P:(c + 1) * P, :]).then_inc(loaded, 16)
    pool.dma_start(later[:], o["later_src"].rearrange("i j -> (i j)").partition_broadcast(P)).then_inc(loaded, 16)
    pool.wait_ge(loaded, 16 * (2 * KT + 1))
    pool.tensor_copy(X[:], o["raw"][:].rearrange("p m c j -> p m j c")).then_inc(done, 1)
    ops = 9

    def along(v):
        return v.unsqueeze(3).broadcast_to([P, 2, R, KT])

    with pool.Fori(0, R) as i:
        def after(c):
            pool.wait_ge(done, i * ops + c + 1)
            pool.sem_inc(o["passed"], 1)
        after(0)
        pool.tensor_copy(col[:], X[:, :, i, :]).then_inc(done, 1)
        after(1)
        pool.tensor_tensor(prod[:], X[:], col[:].unsqueeze(2).broadcast_to([P, 2, R, KT]), ALU.mult).then_inc(done, 1)
        after(2)
        pool.tensor_tensor(prod[:, :, :, 0:2], prod[:, :, :, 0:2], prod[:, :, :, 2:4], ALU.add).then_inc(done, 1)
        after(3)
        pool.tensor_tensor(sums[:], prod[:, :, :, 0], prod[:, :, :, 1], ALU.add).then_inc(done, 1)
        after(4)
        pool.partition_all_reduce(dots[:].rearrange("p m j -> p (m j)"), sums[:].rearrange("p m j -> p (m j)"), P, RADD).then_inc(done, 1)
        after(5)
        pool.tensor_copy(o["sq"][:], dots[:, :, i]).then_inc(sq_ready.sem, 1)
        pool.tensor_tensor(coef[:], dots[:], later[:, i, :].unsqueeze(1).broadcast_to([P, 2, R]), ALU.mult).then_inc(done, 1)
        pool.wait_ge(inv_ready.sem, inv_ready.at(i))
        pool.sem_inc(o["passed"], 1)
        after(6)
        pool.tensor_copy(scale[:, :, i], o["inv"][:])
        pool.tensor_tensor(coef[:], coef[:], o["inv"][:].unsqueeze(2).broadcast_to([P, 2, R]), ALU.mult).then_inc(done, 1)
        after(7)
        pool.tensor_tensor(coef[:], coef[:], o["inv"][:].unsqueeze(2).broadcast_to([P, 2, R]), ALU.mult).then_inc(done, 1)
        after(8)
        pool.tensor_tensor(prod[:], along(coef[:]), col[:].unsqueeze(2).broadcast_to([P, 2, R, KT]), ALU.mult)
        pool.drain()
        pool.tensor_tensor(X[:], X[:], prod[:], ALU.subtract).then_inc(done, 1)
    pool.wait_ge(done, R * ops + 1)
    pool.tensor_tensor(X[:], X[:], along(scale[:]), ALU.mult)


def finish(nc, d, s, ident, totals, ortho, experts, out, batches, seq, dim):
    KT = dim // P
    R = ortho["R"]
    X = ortho["X"]
    NCB = seq // CH
    x_v = s["x3"].rearrange("(n t p) c -> n p t c", p=P, t=TPC)
    y_v = out.rearrange("b (n t p) c -> (b n) p t c", p=P, t=TPC)
    NDOM = d["L3_cond_expert_W"].shape[0]
    with Kit(nc) as k:
        maps = k.sb("maps", [P, KT, R])
        resp_wT = k.sb("resp_wT", [R, dim])
        resp_row = k.sb("resp_row", [P, dim])
        strength = k.sb("strength", [P, batches])
        downT = k.sb("downT", [P, KT, P])
        upT = k.sb("upT", [P, dim])
        expertT = k.sb("expertT", [P, batches, P])
        down_b = k.sb("down_b", [P, 1])
        expert_b = k.sb("expert_b", [P, batches])
        up_b = k.sb("up_b", [P, dim])
        gain = k.sb("gain3", [P, dim])
        beta = k.sb("beta3", [P, dim])
        with Kit(nc) as q:
            ones = q.sb("ones_f", [P, P])
            bias2 = q.sb("bias2", [P, dim])
            gw1 = q.sb("gw1", [P, dim])
            gw1T = q.sb("gw1T", [P, KT, P])
            gb1 = q.sb("gb1", [P, 1])
            gw2 = q.sb("gw2", [P, 1])
            gw2_wide = q.sb("gw2_wide", [P, P])
            gb2 = q.sb("gb2", [P, 1])
            safety = q.sb("safety", [P, batches])
            domain = q.sb("domain", [P, batches], I32)
            dom = q.sb("dom", [P, batches])
            valid = q.sb("valid", [P, 2, batches])
            resp_w = q.sb("resp_w_in", [P, KT, R])
            down_w = q.sb("down_w", [P, dim])
            up_w = q.sb("up_w", [P, KT, P])
            exp_w = q.sb("exp_w", [P, batches, P])
            exp_b = q.sb("exp_b", [P, batches, 2])
            pooled = q.sb("pooled", [P, KT, batches])
            h1 = q.sb("h1", [P, batches])
            gate = q.sb("gate", [P, 2, batches])
            uT = q.sb("uT", [R, 2, dim])
            b32T = q.sb("b32T", [P, KT, R])
            mid = q.sb("mid", [R, R])
            ps = q.ps("ps_setup", [P, 8, 512])
            loaded = q.sem("f_loaded")
            pe_done, dve_done, act_done = q.sem("f_pe"), q.sem("f_dve"), q.sem("f_act")
            plain = [
                (bias2[:], d["L2_cond_safety_bias"].partition_broadcast(P)),
                (resp_row[:], d["L2_cond_resp_b"].partition_broadcast(P)),
                (gw1[:], d["L2_cond_gate_w1"]),
                (gb1[:], d["L2_cond_gate_b1"].rearrange("(p o) -> p o", o=1)),
                (gw2[:], d["L2_cond_gate_w2"].rearrange("o p -> p o")),
                (gb2[:], d["L2_cond_gate_b2"].partition_broadcast(P)),
                (safety[:], d["condB_safetyscore"].partition_broadcast(P)),
                (domain[:], d["itok_B_0_15"].partition_broadcast(P)),
                (resp_w[:], d["L2_cond_resp_w"].rearrange("(c p) r -> p c r", p=P)),
                (down_w[:], d["L3_cond_down_W"]),
                (up_w[:], d["L3_cond_up_W"].rearrange("(c p) a -> p c a", p=P)),
                (down_b[:], d["L3_cond_down_b"].rearrange("(p o) -> p o", o=1)),
                (up_b[:], d["L3_cond_up_b"].partition_broadcast(P)),
                (gain[:], d["L3_cond_ln_gamma"].partition_broadcast(P)),
                (beta[:], d["L3_cond_ln_beta"].partition_broadcast(P)),
            ]
            n_loads = len(plain) + 3 * batches
            with nc.Block() as block:
                @block.sync
                def _(sp):
                    for dst, src in plain:
                        sp.dma_start(dst, src).then_inc(loaded, 16)
                    for b in range(batches):
                        e = read_index(sp, (experts[b], NDOM))
                        sp.dma_start(exp_w[:, b, :], d["L3_cond_expert_W"][e]).then_inc(loaded, 16)
                        sp.dma_start(exp_b[:, b, 0:1], d["L3_cond_expert_b"][e].rearrange("(p o) -> p o", o=1)).then_inc(loaded, 16)
                        sp.dma_start(exp_b[:, b, 1:2], d["L3_cond_domain_emb"][e].rearrange("(p o) -> p o", o=1)).then_inc(loaded, 16)

                @block.tensor
                def _(pe):
                    pe.wait_ge(loaded, 16 * n_loads)
                    for c in range(KT):
                        pe.transpose(ps[:, 0, c * P:(c + 1) * P], gw1[:, c * P:(c + 1) * P], ident[:])
                        pe.transpose(ps[:, 1, c * P:(c + 1) * P], down_w[:, c * P:(c + 1) * P], ident[:])
                        pe.transpose(ps[:, 2, c * P:(c + 1) * P], up_w[:, c, :], ident[:])
                        pe.transpose(ps[0:R, 3, c * P:(c + 1) * P], resp_w[:, c, :], ident[:])
                        for m in range(2):
                            pe.transpose(ps[0:R, 4 + m, c * P:(c + 1) * P], X[:, m, :, c], ident[:])
                    for b in range(batches):
                        pe.transpose(ps[:, 6, b * P:(b + 1) * P], exp_w[:, b, :], ident[:])
                    pe.wait_ge(dve_done, 1)
                    for b in range(batches):
                        for c in range(KT):
                            last = pe.matmul(ps[:, 7, c * batches + b:c * batches + b + 1], totals[b][:, c * P:(c + 1) * P],
                                             ones[:, 0:1], start=True, stop=True)
                    last.then_inc(pe_done, 1)
                    pe.wait_ge(dve_done, 2)
                    for c in range(KT):
                        pe.matmul(ps[:, 0, c * R:(c + 1) * R], uT[:, 1, c * P:(c + 1) * P], uT[:, 0, 0:R], start=True, stop=True)
                    for c in range(KT):
                        last = pe.matmul(ps[:, 1, 0:batches], gw1T[:, c, :], pooled[:, c, :], start=(c == 0), stop=(c == KT - 1))
                    last.then_inc(pe_done, 1)
                    pe.wait_ge(dve_done, 3)
                    for c in range(KT):
                        pe.matmul(ps[0:R, 2, 0:R], X[:, 1, :, c], b32T[:, c, :], start=(c == 0), stop=(c == KT - 1))
                    pe.matmul(ps[:, 3, 0:batches], gw2_wide[:], h1[:], start=True, stop=True).then_inc(pe_done, 1)
                    pe.wait_ge(dve_done, 4)
                    for c in range(KT):
                        last = pe.matmul(ps[:, 4, c * R:(c + 1) * R], uT[:, 0, c * P:(c + 1) * P], mid[:], start=True, stop=True)
                    last.then_inc(pe_done, 1)

                @block.scalar
                def _(act):
                    act.wait_ge(pe_done, 3)
                    act.activation(gate[:, 0, :], ps[:, 3, 0:batches], ACT.Sigmoid, bias=gb2[:])
                    act.activation(gate[:, 1, :], safety[:], ACT.Sigmoid).then_inc(act_done, 1)

                @block.vector
                def _(dve):
                    dve.memset(ones[:], 1.0).then_inc(dve_done, 1)
                    dve.wait_ge(loaded, 16 * n_loads)
                    dve.tensor_tensor(resp_row[:], resp_row[:], bias2[:], ALU.add)
                    dve.tensor_copy(dom[:], domain[:])
                    dve.drain()
                    dve.tensor_scalar(valid[:, 0], dom[:], 0.0, None, ALU.is_ge)
                    dve.tensor_scalar(valid[:, 1], dom[:], float(NDOM), None, ALU.is_lt)
                    dve.tensor_scalar(gw2_wide[:], ones[:], gw2[:], None, ALU.mult)
                    dve.drain()
                    dve.tensor_tensor(valid[:, 0], valid[:, 0], valid[:, 1], ALU.mult)
                    dve.drain()
                    dve.tensor_scalar(valid[:, 1], valid[:, 0], -1.0, 1.0, ALU.mult, ALU.add)
                    dve.drain()
                    for b in range(batches):
                        dve.scalar_tensor_tensor(out=expert_b[:, b:b + 1], in0=exp_b[:, b, 0:1], scalar=valid[:, 0, b:b + 1],
                                                 in1=exp_b[:, b, 1:2], op0=ALU.mult, op1=ALU.add)
                        dve.tensor_scalar(expertT[:, b, :], ident[:], valid[:, 1, b:b + 1], None, ALU.mult)
                    dve.wait_ge(pe_done, 1)
                    dve.drain()
                    for b in range(batches):
                        dve.scalar_tensor_tensor(out=expertT[:, b, :], in0=ps[:, 6, b * P:(b + 1) * P], scalar=valid[:, 0, b:b + 1],
                                                 in1=expertT[:, b, :], op0=ALU.mult, op1=ALU.add)
                    dve.tensor_copy(gw1T[:].rearrange("p c a -> p (c a)"), ps[:, 0, :])
                    dve.tensor_copy(downT[:].rearrange("p c a -> p (c a)"), ps[:, 1, :])
                    dve.tensor_copy(upT[:], ps[:, 2, :])
                    dve.tensor_copy(resp_wT[:], ps[0:R, 3, :])
                    for m in range(2):
                        dve.tensor_copy(uT[:, m, :], ps[0:R, 4 + m, :])
                    dve.tensor_scalar(pooled[:].rearrange("p c b -> p (c b)"), ps[:, 7, 0:KT * batches], 1.0 / seq, None, ALU.mult)
                    dve.drain().then_inc(dve_done, 1)
                    dve.wait_ge(pe_done, 2)
                    dve.tensor_copy(b32T[:].rearrange("p c r -> p (c r)"), ps[:, 0, 0:KT * R])
                    dve.tensor_scalar(h1[:], ps[:, 1, 0:batches], gb1[:], 0.0, ALU.add, ALU.max)
                    dve.drain().then_inc(dve_done, 1)
                    dve.wait_ge(pe_done, 3)
                    dve.tensor_copy(mid[:], ps[0:R, 2, 0:R]).then_inc(dve_done, 1)
                    dve.wait_ge(pe_done, 4)
                    dve.tensor_copy(maps[:].rearrange("p c r -> p (c r)"), ps[:, 4, 0:KT * R])
                    dve.wait_ge(act_done, 1)
                    dve.tensor_tensor(strength[:], gate[:, 0, :], gate[:, 1, :], ALU.mult)

        x = k.sb("x_f", [P, 2, TPC, dim])
        x4 = k.sb("x4", [P, TPC, dim])
        resp = k.sb("resp", [P, 2, dim])
        y = k.sb("y_f", [P, 2, TPC, dim])
        xT = k.sb("xT_f", [P, KT, CH])
        x4T = k.sb("x4T", [P, KT, CH])
        feats = k.sb("feats", [R, CH])
        hid = k.sb("hid", [P, CH])
        exo = k.sb("exo", [P, CH])
        st = k.sb("st_f", [P, TPC, 6])
        mv = k.sb("mv_f", [P, TPC, 2])
        var = k.sb("var_f", [P, TPC])
        sd = k.sb("sd_f", [P, TPC])
        turned = k.ps("turned_f", [P, 2, KT, P])
        ps_feat = k.ps("ps_feat", [P, CH])
        ps_hid = k.ps("ps_hid", [P, CH])
        ps_exp = k.ps("ps_exp", [P, CH])
        wide = k.ps("wide_f", [P, 2, dim])
        x_in = [k.count(f"f_x_in{j}", unit=16) for j in range(2)]
        tile_turned = k.count("f_tile_turned")
        turned_out = k.count("f_turned_out", early=2)
        feat_done, feat_ready = k.count("f_feat_done"), k.count("f_feat_ready")
        wide_done = k.count("f_wide_done")
        wide_out = k.count("f_wide_out", early=2)
        x4_ready = k.count("f_x4_ready", early=1)
        hid_done, hid_ready = k.count("f_hid_done"), k.count("f_hid_ready")
        exp_done, exp_ready = k.count("f_exp_done"), k.count("f_exp_ready")
        var_ready, sd_ready = k.count("f_var_ready"), k.count("f_sd_ready")
        scaled = k.count("f_scaled")
        y_ready = k.count("f_y_ready")
        y_out = [k.count(f"f_y_out{j}", early=1, unit=16) for j in range(2)]
        half_done = k.count("f_half_done")
        passed = k.sem("passed_f")
        n_chunks = batches * NCB

        def next_exists(n):
            return exists(n + 1 if isinstance(n, int) else n, n_chunks)

        def last_exists(n):
            return not isinstance(n, int) or n >= 1

        with nc.Block() as block:
            @block.sync
            def _(sp):
                for c in y_out:
                    sp.sem_inc(c.sem, c.head_start)
                sp.dma_start(x[:, 0], x_v[0]).then_inc(x_in[0].sem, 16)

                def store(n, j):
                    sp.wait_ge(y_ready.sem, y_ready.at(n))
                    sp.dma_start(y_v[n], y[:, j]).then_inc(y_out[j].sem, 16)

                def chunk(n, j, half):
                    if next_exists(n):
                        sp.wait_ge(x4_ready.sem, x4_ready.at(n * TPC - 1))
                        sp.dma_start(x[:, 1 - j], x_v[n + 1]).then_inc(x_in[1 - j].sem, 16)
                    if last_exists(n):
                        store(n - 1, 1 - j)
                sweep(sp, n_chunks, chunk, head=2, tail=2)
                store(n_chunks - 1, 1)
                for j in range(2):
                    sp.wait_ge(y_out[j].sem, y_out[j].at(n_chunks // 2 - 1))

            @block.gpsimd
            def _(pool):
                def chunk(n, j, half):
                    pool.wait_ge(scaled.sem, scaled.at(n))
                    pool.sem_inc(passed, 1)
                    pool.tensor_tensor(y[:, j], y[:, j], gain[:].unsqueeze(1).broadcast_to([P, TPC, dim]), ALU.mult)\
                        .then_inc(half_done.sem, 1)
                    pool.wait_ge(half_done.sem, half_done.at(n))
                    pool.sem_inc(passed, 1)
                    pool.tensor_tensor(y[:, j], y[:, j], beta[:].unsqueeze(1).broadcast_to([P, TPC, dim]), ALU.add)\
                        .then_inc(y_ready.sem, 1)
                sweep(pool, n_chunks, chunk)

            @block.tensor
            def _(pe):
                def turn(src, first_event, t):
                    pe.wait_ge(turned_out.sem, turned_out.at(first_event + t - 2))
                    for c in range(KT):
                        last = pe.transpose(turned[:, t % 2, c, :], src[:, t, c * P:(c + 1) * P], ident[:])
                    last.then_inc(tile_turned.sem, 1)

                def turn_x(n, j, half):
                    pe.wait_ge(x_in[j].sem, x_in[j].at(half))
                    for t in range(TPC):
                        turn(x[:, j], n * 8, t)

                def features(n):
                    pe.wait_ge(turned_out.sem, turned_out.at(n * 8 + 3))
                    for c in range(KT):
                        last = pe.matmul(ps_feat[0:R, :], maps[:, c, :], xT[:, c, :], start=(c == 0), stop=(c == KT - 1))
                    last.then_inc(feat_done.sem, 1)

                def chunk(b, n, j, half):
                    pe.wait_ge(feat_ready.sem, feat_ready.at(n))
                    for t in range(TPC):
                        pe.wait_ge(wide_out.sem, wide_out.at(n * 8 + t - 2))
                        pe.matmul(wide[:, t % 2, :], feats[:, t * P:(t + 1) * P], resp_wT[:], start=True, stop=True)\
                          .then_inc(wide_done.sem, 1)
                    for t in range(TPC):
                        pe.wait_ge(x4_ready.sem, x4_ready.at(n * TPC + t))
                        turn(x4, n * 8 + 4, t)
                    pe.wait_ge(turned_out.sem, turned_out.at(n * 8 + 7))
                    for c in range(KT):
                        last = pe.matmul(ps_hid[:], downT[:, c, :], x4T[:, c, :], start=(c == 0), stop=(c == KT - 1))
                    last.then_inc(hid_done.sem, 1)
                    if next_exists(n):
                        turn_x(n + 1, 1 - j, half + j)
                    pe.wait_ge(hid_ready.sem, hid_ready.at(n))
                    pe.matmul(ps_exp[:], expertT[:, b, :], hid[:], start=True, stop=True).then_inc(exp_done.sem, 1)
                    if next_exists(n):
                        features(n + 1)
                    pe.wait_ge(exp_ready.sem, exp_ready.at(n))
                    for t in range(TPC):
                        pe.wait_ge(wide_out.sem, wide_out.at(n * 8 + 4 + t - 2))
                        pe.matmul(wide[:, t % 2, :], exo[:, t * P:(t + 1) * P], upT[:], start=True, stop=True)\
                          .then_inc(wide_done.sem, 1)
                turn_x(0, 0, 0)
                features(0)
                sweep_batches(pe, batches, NCB // 2, chunk)

            @block.scalar
            def _(act):
                act.sem_inc(turned_out.sem, turned_out.head_start)

                def turned_to(dst, first_event):
                    for t in range(TPC):
                        act.wait_ge(tile_turned.sem, tile_turned.at(first_event + t))
                        act.activation(dst[:, :, t * P:(t + 1) * P], turned[:, t % 2], ACT.Copy).then_inc(turned_out.sem, 1)

                def features_out(n):
                    act.wait_ge(feat_done.sem, feat_done.at(n))
                    act.activation(feats[:], ps_feat[0:R, :], ACT.Copy).then_inc(feat_ready.sem, 1)

                def root(n):
                    act.wait_ge(var_ready.sem, var_ready.at(n))
                    act.activation(sd[:], var[:], ACT.Sqrt).then_inc(sd_ready.sem, 1)

                def chunk(b, n, j, half):
                    turned_to(x4T, n * 8 + 4)
                    act.wait_ge(hid_done.sem, hid_done.at(n))
                    act.activation(hid[:], ps_hid[:], ACT.Gelu, bias=down_b[:]).then_inc(hid_ready.sem, 1)
                    if next_exists(n):
                        turned_to(xT, (n + 1) * 8)
                    act.wait_ge(exp_done.sem, exp_done.at(n))
                    act.activation(exo[:], ps_exp[:], ACT.Identity, bias=expert_b[:, b:b + 1]).then_inc(exp_ready.sem, 1)
                    if next_exists(n):
                        features_out(n + 1)
                    if last_exists(n):
                        root(n - 1)
                turned_to(xT, 0)
                features_out(0)
                sweep_batches(act, batches, NCB // 2, chunk)
                root(n_chunks - 1)

            @block.vector
            def _(dve):
                for c in (wide_out, x4_ready):
                    dve.sem_inc(c.sem, c.head_start)

                def norm(n, j):
                    layer_stats(dve, st, mv, y[:, j])
                    dve.tensor_scalar(var[:], mv[:, :, 1], 1e-5, None, ALU.add).then_inc(var_ready.sem, 1)
                    dve.wait_ge(sd_ready.sem, sd_ready.at(n))
                    dve.reciprocal(var[:], sd[:])
                    dve.drain()
                    for t in range(TPC):
                        last = dve.tensor_scalar(y[:, j, t, :], y[:, j, t, :], mv[:, t, 0:1], var[:, t:t + 1],
                                                 ALU.subtract, ALU.mult)
                    last.then_inc(scaled.sem, 1)

                def chunk(b, n, j, half):
                    dve.wait_ge(x_in[j].sem, x_in[j].at(half))
                    for t in range(TPC):
                        dve.wait_ge(wide_done.sem, wide_done.at(n * 8 + t))
                        dve.tensor_tensor(resp[:, t % 2], wide[:, t % 2], resp_row[:], ALU.add).then_inc(wide_out.sem, 1)
                        dve.drain()
                        dve.scalar_tensor_tensor(out=x4[:, t, :], in0=resp[:, t % 2], scalar=strength[:, b:b + 1],
                                                 in1=x[:, j, t, :], op0=ALU.mult, op1=ALU.add).then_inc(x4_ready.sem, 1)
                    if last_exists(n):
                        norm(n - 1, 1 - j)
                    dve.wait_ge(y_out[j].sem, y_out[j].at(half - 1))
                    for t in range(TPC):
                        dve.drain()
                        dve.wait_ge(wide_done.sem, wide_done.at(n * 8 + 4 + t))
                        dve.tensor_tensor(resp[:, t % 2], wide[:, t % 2], up_b[:], ALU.add).then_inc(wide_out.sem, 1)
                        dve.drain()
                        dve.tensor_tensor(y[:, j, t, :], resp[:, t % 2], x4[:, t, :], ALU.add)
                    dve.drain()
                sweep_batches(dve, batches, NCB // 2, chunk)
                norm(n_chunks - 1, 1)


def program(nc, d, out):
    batches, seq, dim = d["x"].shape
    heads = d["fside_Bx16xSxS_0"].shape[1]
    dff = d["L0_cond_W1"].shape[1]
    R = d["L2_cond_U"].shape[1]
    rows = batches * seq
    n_chunks = rows // CH
    E = d["L1_cond_Wi"].shape[0]

    def scratch(name, shape, dtype=F32):
        return nc.dram_tensor(f"scratch_{name}", shape, dtype, kind="Internal").ap()

    s = {
        "x0": scratch("x0", (rows, dim)),
        "q": scratch("q", (batches, dim // P, 2, P, seq)),
        "k": scratch("k", (batches, dim // P, 2, P, seq)),
        "v": scratch("v", (rows, dim)),
        "ctx": scratch("ctx", (rows // P * (dim // P), P, P)),
        "mask": scratch("mask", (batches, seq, seq), BF16),
        "x1": scratch("x1", (rows, dim)),
        "x2": scratch("x2", (rows, dim)),
        "x3": scratch("x3", (rows, dim)),
    }
    with Kit(nc) as k:
        ident = k.sb("ident", [P, P])
        index = k.sb("index", [1, 2, batches], I32)
        start = k.sem("start")
        with nc.Block() as block:
            @block.sync
            def _(sp):
                sp.dma_start(ident[:], d["ident"]).then_inc(start, 16)
                sp.dma_start(index[:, 0, :], d["itok_B_0_7"].rearrange("(o b) -> o b", o=1)).then_inc(start, 16)
                sp.dma_start(index[:, 1, :], d["itok_B_0_15"].rearrange("(o b) -> o b", o=1)).then_inc(start, 16)
                sp.wait_ge(start, 48)
        with Kit(nc) as m:
            scale1 = m.sb("scale1", [P, batches, dim])
            shift = m.sb("shift", [P, batches, dim])
            prepare(nc, d, scale1, shift, batches, dim)
            project(nc, d, s, ident, scale1, shift, batches, seq, dim, heads)
        attend(nc, d, s, ident, batches, seq, dim, heads)
        out_proj(nc, d, s, ident, batches, seq, dim, heads)
        KT = dim // P
        ortho = {"X": k.sb("gs_X", [P, 2, R, KT]), "raw": k.sb("gs_raw", [P, 2, KT, R]), "R": R, "KT": KT,
                 "src": (d["L2_cond_U"], d["L2_cond_V"]), "later_src": d["later"], "root": k.sb("gs_root_t", [P, 2]),
                 "sq": k.sb("gs_sq_t", [P, 2]), "inv": k.sb("gs_inv_t", [P, 2]), "passed": k.sem("gs_passed")}
        totals = [k.sb(f"total{b}", [P, dim]) for b in range(batches)]
        w = {"w1": lambda e: d["L0_cond_W1"], "w2": lambda e: d["L0_cond_W2"], "b1": lambda e: d["L0_cond_b1"],
             "b2": lambda e: d["L0_cond_b2"], "gain": lambda e: d["L0_cond_g2"], "beta": lambda e: d["L0_cond_beta2"]}
        ffn(nc, ident, "fa", w, None, s["x1"], s["x2"], True, n_chunks, dim, dff, ortho=ortho)
        w = {"w1": lambda e: d["L1_cond_Wi"][e], "w2": lambda e: d["L1_cond_Wo"][e], "b1": lambda e: d["L1_cond_bi"][e],
             "b2": lambda e: d["L1_cond_bo"][e], "gain": lambda e: d["L1_cond_gamma"][e], "beta": lambda e: d["L1_cond_beta"][e]}
        for b in range(batches):
            part = slice(b * seq, (b + 1) * seq)
            ffn(nc, ident, f"fb{b}", w, (index[0:1, 0, b:b + 1], E), s["x2"][part], s["x3"][part], False, seq // CH, dim, dff,
                total=totals[b][:])
        finish(nc, d, s, ident, totals, ortho, [index[0:1, 1, b:b + 1] for b in range(batches)], out, batches, seq, dim)


def kernel(**inputs):
    import concourse.bacc as _bacc
    from concourse.bass_utils import run_bass_kernel_spmd as _run

    nc = _bacc.Bacc("TRN2", target_bir_lowering=False, num_devices=1)
    arrays = {name: np.ascontiguousarray(a) for name, a in inputs.items()}
    dim = arrays["x"].shape[-1]
    R = arrays["L2_cond_U"].shape[1]
    half = dim // 2
    freqs = np.exp(np.arange(half, dtype=np.float32) * np.float32(-np.log(10000.0) / (half - 1))).astype(np.float32)
    arrays["freqs"] = np.ascontiguousarray(freqs.reshape(half // P, P).T)
    arrays["ident"] = np.eye(P, dtype=np.float32)
    arrays["later"] = np.triu(np.ones((R, R), np.float32), 1)
    d = {name: nc.dram_tensor(f"in_{name}", a.shape, mybir.dt.from_np(a.dtype), kind="ExternalInput").ap()
         for name, a in arrays.items()}
    shape = arrays["x"].shape
    out = nc.dram_tensor("out_0", shape, F32, kind="ExternalOutput").ap()
    with nc.allow_non_contiguous_dma(reason="bias columns of a few KB"):
        program(nc, d, out)
    r = _run(nc, [{f"in_{name}": a for name, a in arrays.items()}], core_ids=[0])
    return r.results[0]["out_0"]
```
